# Optimizing a Trainium2 kernel written in Bass

```python
import numpy as np
import jax
import jax.numpy as jnp

def _softmax(x, axis=-1):
    return jax.nn.softmax(x, axis=axis)

def _gelu(x):
    return jax.nn.gelu(x, approximate=True)

def _silu(x):
    return jax.nn.silu(x)

def _sigmoid(x):
    return jax.nn.sigmoid(x)

def _layernorm(x, axis=-1, eps=1e-05):
    m = jnp.mean(x, axis=axis, keepdims=True)
    v = jnp.var(x, axis=axis, keepdims=True)
    return (x - m) / jnp.sqrt(v + eps)

def _scatter_add(tgt, idx, src, axis=0):
    return tgt.at[idx].add(src)

def _segment_sum(src, seg, n):
    return jax.ops.segment_sum(src, seg, n)
kernel_name = 'mk_seq_postln_d2_jaxref_r8_7955b1'

def setup_inputs(seed: int=0):
    np.random.seed(seed)
    _w = jnp.asarray

    def _L0_attn_setup():
        import jax, jax.numpy as jnp
        import numpy as np
        D_MODEL = 128
        N_HEADS = 16
        HEAD_DIM = D_MODEL // N_HEADS
        EPS_ATTN = 1e-06
        EPS_LN = 1e-05

        def layer_norm(x, gamma, beta):
            mu = jnp.mean(x, axis=-1, keepdims=True)
            var = jnp.var(x, axis=-1, keepdims=True)
            return (x - mu) * jax.lax.rsqrt(var + EPS_LN) * gamma + beta

        def linear_attention(x, Wq, bq, Wk, bk, Wv, bv, Wo, bo):
            N, L, _ = x.shape
            H, Dh = (N_HEADS, HEAD_DIM)
            Q = (x @ Wq + bq).reshape(N, L, H, Dh)
            K = (x @ Wk + bk).reshape(N, L, H, Dh)
            V = (x @ Wv + bv).reshape(N, L, H, Dh)
            Q = jax.nn.elu(Q) + 1.0
            K = jax.nn.elu(K) + 1.0
            KV = jnp.einsum('nshd,nshm->nhmd', K, V)
            Ksum = K.sum(axis=1)
            Z = 1.0 / (jnp.einsum('nlhd,nhd->nlh', Q, Ksum) + EPS_ATTN)
            out = jnp.einsum('nlhd,nhmd,nlh->nlhm', Q, KV, Z)
            out = out.reshape(N, L, H * Dh)
            return out @ Wo + bo
        key = jax.random.key(seed)
        ks = jax.random.split(key, 16)
        s = 1.0 / np.sqrt(D_MODEL)
        inp = {'x': jax.random.normal(ks[0], (4, 512, D_MODEL), dtype=jnp.float32), 'Wq': jax.random.normal(ks[1], (D_MODEL, D_MODEL), dtype=jnp.float32) * s, 'bq': jnp.zeros((D_MODEL,), jnp.float32), 'Wk': jax.random.normal(ks[2], (D_MODEL, D_MODEL), dtype=jnp.float32) * s, 'bk': jnp.zeros((D_MODEL,), jnp.float32), 'Wv': jax.random.normal(ks[3], (D_MODEL, D_MODEL), dtype=jnp.float32) * s, 'bv': jnp.zeros((D_MODEL,), jnp.float32), 'Wo': jax.random.normal(ks[4], (D_MODEL, D_MODEL), dtype=jnp.float32) * s, 'bo': jnp.zeros((D_MODEL,), jnp.float32), 'W1': jax.random.normal(ks[5], (D_MODEL, 4 * D_MODEL), dtype=jnp.float32) * s, 'b1': jnp.zeros((4 * D_MODEL,), jnp.float32), 'W2': jax.random.normal(ks[6], (4 * D_MODEL, D_MODEL), dtype=jnp.float32) * (0.5 * s), 'b2': jnp.zeros((D_MODEL,), jnp.float32), 'g1': jnp.ones((D_MODEL,), jnp.float32), 'beta1': jnp.zeros((D_MODEL,), jnp.float32), 'g2': jnp.ones((D_MODEL,), jnp.float32), 'beta2': jnp.zeros((D_MODEL,), jnp.float32)}
        return inp
    _L0_attn_in = _L0_attn_setup()

    def _L0_ffn_setup():
        import jax, jax.numpy as jnp
        import numpy as np
        D_MODEL = 128
        key = jax.random.key(seed)
        k_x, k_w, k_a1, k_a2 = jax.random.split(key, 4)
        x = jax.random.normal(k_x, (4, 256, D_MODEL), dtype=jnp.float32)
        weight = jax.random.normal(k_w, (D_MODEL, D_MODEL), dtype=jnp.float32) * 0.02
        aux_weight1 = jax.random.normal(k_a1, (D_MODEL, D_MODEL), dtype=jnp.float32) * 0.02
        aux_weight2 = jax.random.normal(k_a2, (D_MODEL, D_MODEL), dtype=jnp.float32) * 0.02
        bias = jnp.zeros((D_MODEL,), dtype=jnp.float32)
        return {'x': x, 'weight': weight, 'aux_weight1': aux_weight1, 'aux_weight2': aux_weight2, 'bias': bias}
    _L0_ffn_in = _L0_ffn_setup()

    def _L1_attn_setup():
        import jax, jax.numpy as jnp
        import numpy as np
        D_MODEL = 128
        N_HEADS = 16
        D_LATENT = 32
        HEAD_DIM = D_MODEL // N_HEADS

        def apply_rope(x):
            B, T, H, D = x.shape
            inv_freq = 1.0 / 10000.0 ** (jnp.arange(0, D, 2, dtype=jnp.float32) / D)
            t = jnp.arange(T, dtype=jnp.float32)
            freqs = t[:, None] * inv_freq[None, :]
            sin_f = jnp.sin(freqs)[None, :, None, :]
            cos_f = jnp.cos(freqs)[None, :, None, :]
            x1, x2 = jnp.split(x, 2, axis=-1)
            return jnp.concatenate([x1 * cos_f - x2 * sin_f, x1 * sin_f + x2 * cos_f], axis=-1)
        key = jax.random.key(seed)
        ks = jax.random.split(key, 10)
        B, T = (4, 512)
        s = lambda fan_in: 1.0 / np.sqrt(fan_in)
        return {'x': jax.random.normal(ks[0], (B, T, D_MODEL), dtype=jnp.float32), 'Wq': jax.random.normal(ks[1], (D_MODEL, D_MODEL), dtype=jnp.float32) * s(D_MODEL), 'bq': jnp.zeros((D_MODEL,), jnp.float32), 'Wdown': jax.random.normal(ks[2], (D_MODEL, D_LATENT), dtype=jnp.float32) * s(D_MODEL), 'bdown': jnp.zeros((D_LATENT,), jnp.float32), 'Wup': jax.random.normal(ks[3], (D_LATENT, 2 * D_MODEL), dtype=jnp.float32) * s(D_LATENT), 'bup': jnp.zeros((2 * D_MODEL,), jnp.float32), 'Wout': jax.random.normal(ks[4], (D_MODEL, D_MODEL), dtype=jnp.float32) * s(D_MODEL), 'bout': jnp.zeros((D_MODEL,), jnp.float32)}
    _L1_attn_in = _L1_attn_setup()

    def _L1_ffn_setup():
        import jax, jax.numpy as jnp
        import numpy as np
        H = 128
        I = 128
        E = 8
        key = jax.random.key(seed)
        ks = jax.random.split(key, 8)
        s = 0.02
        x = jax.random.normal(ks[0], (4, 256, H), dtype=jnp.float32)
        Wg = jax.random.normal(ks[1], (H, E), dtype=jnp.float32) * s
        bg = jnp.zeros((E,), dtype=jnp.float32)
        W1 = jax.random.normal(ks[2], (E, H, I), dtype=jnp.float32) * s
        b1 = jnp.zeros((E, I), dtype=jnp.float32)
        W2 = jax.random.normal(ks[3], (E, I, H), dtype=jnp.float32) * s
        b2 = jnp.zeros((E, H), dtype=jnp.float32)
        return {'x': x, 'Wg': Wg, 'bg': bg, 'W1': W1, 'b1': b1, 'W2': W2, 'b2': b2}
    _L1_ffn_in = _L1_ffn_setup()
    _d = {'L0_attn_x': _L0_attn_in['x'], 'L0_attn_Wq': _L0_attn_in['Wq'], 'L0_attn_bq': _L0_attn_in['bq'], 'L0_attn_Wk': _L0_attn_in['Wk'], 'L0_attn_bk': _L0_attn_in['bk'], 'L0_attn_Wv': _L0_attn_in['Wv'], 'L0_attn_bv': _L0_attn_in['bv'], 'L0_attn_Wo': _L0_attn_in['Wo'], 'L0_attn_bo': _L0_attn_in['bo'], 'L0_attn_W1': _L0_attn_in['W1'], 'L0_attn_b1': _L0_attn_in['b1'], 'L0_attn_W2': _L0_attn_in['W2'], 'L0_attn_b2': _L0_attn_in['b2'], 'L0_attn_g1': _L0_attn_in['g1'], 'L0_attn_beta1': _L0_attn_in['beta1'], 'L0_attn_g2': _L0_attn_in['g2'], 'L0_attn_beta2': _L0_attn_in['beta2'], 'L0_ffn_weight': _L0_ffn_in['weight'], 'L0_ffn_aux_weight1': _L0_ffn_in['aux_weight1'], 'L0_ffn_aux_weight2': _L0_ffn_in['aux_weight2'], 'L0_ffn_bias': _L0_ffn_in['bias'], 'L1_attn_Wq': _L1_attn_in['Wq'], 'L1_attn_bq': _L1_attn_in['bq'], 'L1_attn_Wdown': _L1_attn_in['Wdown'], 'L1_attn_bdown': _L1_attn_in['bdown'], 'L1_attn_Wup': _L1_attn_in['Wup'], 'L1_attn_bup': _L1_attn_in['bup'], 'L1_attn_Wout': _L1_attn_in['Wout'], 'L1_attn_bout': _L1_attn_in['bout'], 'L1_ffn_Wg': _L1_ffn_in['Wg'], 'L1_ffn_bg': _L1_ffn_in['bg'], 'L1_ffn_W1': _L1_ffn_in['W1'], 'L1_ffn_b1': _L1_ffn_in['b1'], 'L1_ffn_W2': _L1_ffn_in['W2'], 'L1_ffn_b2': _L1_ffn_in['b2']}
    _x0 = _d['L0_attn_x']
    _d['L0_attn_x'] = jax.random.normal(jax.random.fold_in(jax.random.key(seed), 1), (8, 1024, 128), dtype=_x0.dtype)
    del _x0
    return _d

def reference(L0_attn_x, L0_attn_Wq, L0_attn_bq, L0_attn_Wk, L0_attn_bk, L0_attn_Wv, L0_attn_bv, L0_attn_Wo, L0_attn_bo, L0_attn_W1, L0_attn_b1, L0_attn_W2, L0_attn_b2, L0_attn_g1, L0_attn_beta1, L0_attn_g2, L0_attn_beta2, L0_ffn_weight, L0_ffn_aux_weight1, L0_ffn_aux_weight2, L0_ffn_bias, L1_attn_Wq, L1_attn_bq, L1_attn_Wdown, L1_attn_bdown, L1_attn_Wup, L1_attn_bup, L1_attn_Wout, L1_attn_bout, L1_ffn_Wg, L1_ffn_bg, L1_ffn_W1, L1_ffn_b1, L1_ffn_W2, L1_ffn_b2):

    def _L0_attn_ref(x, Wq, bq, Wk, bk, Wv, bv, Wo, bo, W1, b1, W2, b2, g1, beta1, g2, beta2):
        import jax, jax.numpy as jnp
        import numpy as np
        D_MODEL = 128
        N_HEADS = 16
        HEAD_DIM = D_MODEL // N_HEADS
        EPS_ATTN = 1e-06
        EPS_LN = 1e-05

        def layer_norm(x, gamma, beta):
            mu = jnp.mean(x, axis=-1, keepdims=True)
            var = jnp.var(x, axis=-1, keepdims=True)
            return (x - mu) * jax.lax.rsqrt(var + EPS_LN) * gamma + beta

        def linear_attention(x, Wq, bq, Wk, bk, Wv, bv, Wo, bo):
            N, L, _ = x.shape
            H, Dh = (N_HEADS, HEAD_DIM)
            Q = (x @ Wq + bq).reshape(N, L, H, Dh)
            K = (x @ Wk + bk).reshape(N, L, H, Dh)
            V = (x @ Wv + bv).reshape(N, L, H, Dh)
            Q = jax.nn.elu(Q) + 1.0
            K = jax.nn.elu(K) + 1.0
            KV = jnp.einsum('nshd,nshm->nhmd', K, V)
            Ksum = K.sum(axis=1)
            Z = 1.0 / (jnp.einsum('nlhd,nhd->nlh', Q, Ksum) + EPS_ATTN)
            out = jnp.einsum('nlhd,nhmd,nlh->nlhm', Q, KV, Z)
            out = out.reshape(N, L, H * Dh)
            return out @ Wo + bo
        x = x + linear_attention(x, Wq, bq, Wk, bk, Wv, bv, Wo, bo)
        x = layer_norm(x, g1, beta1)
        y = jax.nn.relu(x @ W1 + b1) @ W2 + b2
        return layer_norm(x + y, g2, beta2)

    def _L0_ffn_ref(x, weight, aux_weight1, aux_weight2, bias):
        import jax, jax.numpy as jnp
        import numpy as np
        D_MODEL = 128
        h = jnp.einsum('btc,cd->btd', x, weight)
        h = jnp.einsum('btc,cd->btd', h, aux_weight1)
        h = jnp.einsum('btc,cd->btd', h, aux_weight2)
        return jnp.tanh(h + bias)

    def _L1_attn_ref(x, Wq, bq, Wdown, bdown, Wup, bup, Wout, bout):
        import jax, jax.numpy as jnp
        import numpy as np
        D_MODEL = 128
        N_HEADS = 16
        D_LATENT = 32
        HEAD_DIM = D_MODEL // N_HEADS

        def apply_rope(x):
            B, T, H, D = x.shape
            inv_freq = 1.0 / 10000.0 ** (jnp.arange(0, D, 2, dtype=jnp.float32) / D)
            t = jnp.arange(T, dtype=jnp.float32)
            freqs = t[:, None] * inv_freq[None, :]
            sin_f = jnp.sin(freqs)[None, :, None, :]
            cos_f = jnp.cos(freqs)[None, :, None, :]
            x1, x2 = jnp.split(x, 2, axis=-1)
            return jnp.concatenate([x1 * cos_f - x2 * sin_f, x1 * sin_f + x2 * cos_f], axis=-1)
        B, T, D = x.shape
        H, Dh = (N_HEADS, HEAD_DIM)
        q = x @ Wq + bq
        kv_latent = x @ Wdown + bdown
        kv = kv_latent @ Wup + bup
        q = q.reshape(B, T, H, Dh)
        kv = kv.reshape(B, T, H, 2 * Dh)
        k, v = jnp.split(kv, 2, axis=-1)
        q = apply_rope(q)
        k = apply_rope(k)
        att = jnp.einsum('bthd,btgd->bthg', q, k) / jnp.sqrt(jnp.float32(Dh))
        att = jax.nn.softmax(att, axis=-1)
        out = jnp.einsum('bthg,btgd->bthd', att, v)
        out = out.reshape(B, T, D)
        return out @ Wout + bout

    def _L1_ffn_ref(x, Wg, bg, W1, b1, W2, b2):
        import jax, jax.numpy as jnp
        import numpy as np
        H = 128
        I = 128
        E = 8
        B, S, Hd = x.shape
        xf = x.reshape(-1, Hd)
        logits = xf @ Wg + bg
        gates = jax.nn.softmax(logits, axis=-1)
        idx = jnp.argmax(gates, axis=-1)
        h = jax.nn.gelu(jnp.einsum('th,ehi->tei', xf, W1) + b1, approximate=False)
        y = jnp.einsum('tei,eih->teh', h, W2) + b2
        out = jnp.take_along_axis(y, idx[:, None, None], axis=1)[:, 0, :]
        return out.reshape(B, S, Hd)
    x = L0_attn_x
    x = _layernorm(x + _L0_attn_ref(x, L0_attn_Wq, L0_attn_bq, L0_attn_Wk, L0_attn_bk, L0_attn_Wv, L0_attn_bv, L0_attn_Wo, L0_attn_bo, L0_attn_W1, L0_attn_b1, L0_attn_W2, L0_attn_b2, L0_attn_g1, L0_attn_beta1, L0_attn_g2, L0_attn_beta2), axis=-1)
    x = _layernorm(x + _L0_ffn_ref(x, L0_ffn_weight, L0_ffn_aux_weight1, L0_ffn_aux_weight2, L0_ffn_bias), axis=-1)
    x = _layernorm(x + _L1_attn_ref(x, L1_attn_Wq, L1_attn_bq, L1_attn_Wdown, L1_attn_bdown, L1_attn_Wup, L1_attn_bup, L1_attn_Wout, L1_attn_bout), axis=-1)
    x = _layernorm(x + _L1_ffn_ref(x, L1_ffn_Wg, L1_ffn_bg, L1_ffn_W1, L1_ffn_b1, L1_ffn_W2, L1_ffn_b2), axis=-1)
    return x

_drawn_inputs = setup_inputs


def setup_inputs(seed=0):
    import zlib

    import numpy as np

    out = dict(_drawn_inputs(seed))
    spreads = {'L0_attn_bq': (0.0, 0.8),
     'L0_attn_bk': (0.0, 0.8),
     'L0_attn_bv': (0.0, 0.1),
     'L0_attn_bo': (0.0, 0.1),
     'L0_attn_b1': (0.0, 0.1),
     'L0_attn_b2': (0.0, 0.1),
     'L0_attn_g1': (1.0, 0.2),
     'L0_attn_beta1': (0.0, 0.1),
     'L0_attn_g2': (1.0, 0.2),
     'L0_attn_beta2': (0.0, 0.1),
     'L0_ffn_bias': (0.0, 0.1),
     'L1_attn_bq': (0.0, 0.1),
     'L1_attn_bdown': (0.0, 0.1),
     'L1_attn_bup': (0.0, 0.1),
     'L1_attn_bout': (0.0, 0.1),
     'L1_ffn_bg': (0.0, 0.1),
     'L1_ffn_b1': (0.0, 0.652),
     'L1_ffn_b2': (0.0, 0.1)}
    factors = {'L0_attn_Wq': 4.634,
     'L0_attn_Wk': 2.807,
     'L0_ffn_weight': 3.472,
     'L0_ffn_aux_weight1': 3.217,
     'L0_ffn_aux_weight2': 3.244}
    for name, (base, spread) in spreads.items():
        noise = np.random.default_rng([zlib.crc32(name.encode()), seed]).standard_normal(out[name].shape)
        drawn = base * np.exp(spread * noise) if base else spread * noise
        out[name] = jnp.asarray(drawn.astype(out[name].dtype))
    for name, factor in factors.items():
        out[name] = (out[name] * factor).astype(out[name].dtype)
    return out
```

```python
from contextlib import ExitStack

import concourse.bass as bass
from concourse import mybir

F32 = mybir.dt.float32
BF16 = mybir.dt.bfloat16
ALU = mybir.AluOpType
ACT = mybir.ActivationFunctionType
AX = mybir.AxisListType

P = 128
HEADS = 16
HD = P // HEADS
TILES = 4
CHUNK = TILES * P
EPS_LN = 1e-5
EPS_ATTN = 1e-6
FF = 4
EXPERTS = 8
LATENT = 32

ROW = {"bq": 0, "bk": 1, "bv": 2, "bo": 3, "b2": 4, "bout": 5, "bqkv": 6}
N_ROWS = 9

LAG_IN, LAG_MLP, LAG_TANH, LAG_HEADS, LAG_OUT = range(5)


class Step:

    def __init__(self, s, chunks, inside=None, pair=None):
        self.s, self.chunks, self.inside, self.pair = s, chunks, inside, pair
        self.par = (s if inside is None else inside) % 2

    def runs(self, lag):
        return self.inside is not None or 0 <= self.s - lag < self.chunks

    def chunk(self, lag):
        return self.s - lag

    def buf(self, lag):
        return (self.par - lag) % 2

    def done(self, lag, before=0):
        n = self.s - (lag + before - 1)
        return n if self.inside is not None else max(0, min(self.chunks, n))

    def batch(self, lag):
        return (self.s - lag) // 2 if self.inside is None else self.pair + (self.inside - lag) // 2

    def wait(self, eng, sem, lag, per=1, short=0, before=0):
        n = self.done(lag, before)
        if self.inside is not None:
            eng.wait_ge(sem, n * per - short if short else n * per)
        elif n * per - short > 0:
            eng.wait_ge(sem, n * per - short)


def run_steps(eng, chunks, body):
    for s in range(LAG_OUT):
        body(Step(s, chunks))
    with eng.Fori(LAG_OUT // 2, chunks // 2) as pair:
        for u in range(2):
            body(Step(2 * pair + u, chunks, inside=u, pair=pair))
    for s in range(chunks, chunks + LAG_OUT):
        body(Step(s, chunks))


def build(nc, t, out, scratch):
    n_tokens = t["L0_attn_x"].shape[0] * t["L0_attn_x"].shape[1]
    chunks = n_tokens // CHUNK
    per_batch = t["L0_attn_x"].shape[1] // CHUNK
    assert per_batch == 2 and chunks % 2 == 0 and chunks > 2 * LAG_OUT // 2

    x_d = t["L0_attn_x"].rearrange("n (c p j) d -> (n c) p (j d)", c=per_batch, j=TILES)
    out_d = out.rearrange("n (c p j) d -> (n c) p (j d)", c=per_batch, j=TILES)
    scratch_d = scratch.rearrange("(c p) w -> c p w", p=P)

    with ExitStack() as ctx:
        def sb(name, shape, dt=F32):
            return ctx.enter_context(nc.sbuf_tensor(name, shape, dt))

        def sem(name):
            return ctx.enter_context(nc.semaphore(name))

        bank = [ctx.enter_context(nc.psum_tensor(f"bank{i}", [P, CHUNK], F32)) for i in range(8)]
        kv_acc, o_acc = bank[6], bank[7]

        ident = sb("ident", [P, P])
        ident_bf = sb("ident_bf", [P, P], BF16)
        ones_bf = sb("ones_bf", [P, CHUNK], BF16)
        head_of = sb("head_of", [P, HEADS])
        head_mask = sb("head_mask", [P, P])
        minus_half = sb("minus_half", [P, TILES])
        prefer = sb("prefer", [P, EXPERTS])
        pick_f = sb("pick_f", [EXPERTS, EXPERTS, P])
        pick = sb("pick", [EXPERTS, EXPERTS, P], BF16)

        wq, wk, wv, wo = (sb(n, [P, P]) for n in ("wq", "wk", "wv", "wo"))
        w1 = sb("w1", [P, FF * P])
        w2 = sb("w2", [P, FF, P])
        wt = [sb(f"wt{i}", [P, P]) for i in range(3)]
        wtT = sb("wtT", [P, P])
        wt01T = sb("wt01T", [P, P])
        w_tanh = sb("w_tanh", [P, P])
        w_qkv = sb("w_qkv", [P, 3 * P])
        wdown = sb("wdown", [P, LATENT])
        wdownT = sb("wdownT", [LATENT, P])
        wup = sb("wup", [LATENT, 2 * P])
        bdown = sb("bdown", [LATENT, 1])
        wout = sb("wout", [P, P])
        wg = sb("wg", [P, EXPERTS])
        e1 = sb("e1", [P, EXPERTS, P])
        e2 = sb("e2", [P, EXPERTS, P])
        eb1 = sb("eb1", [EXPERTS, P])
        eb2 = sb("eb2", [EXPERTS, P])
        cols = sb("cols", [P, FF + 5])
        col_rows = sb("col_rows", [FF + 5, P])
        rows = sb("rows", [1, N_ROWS * P + EXPERTS])
        rows_left = sb("rows_left", [1, N_ROWS * P + EXPERTS])
        parts = sb("parts", [1, 3, N_ROWS * P + EXPERTS], BF16)
        bias3 = sb("bias3", [P, N_ROWS * P + EXPERTS], BF16)

        def row3(name, n=1):
            return bias3[:, ROW[name] * P:(ROW[name] + n) * P]

        def row3_by_tile(name):
            return row3(name).unsqueeze(1).broadcast_to([P, TILES, P])

        x_tok = [sb(f"x_tok{i}", [P, CHUNK]) for i in range(2)]
        xT = [sb(f"xT{i}", [P, CHUNK]) for i in range(2)]
        qT = [sb(f"qT{i}", [P, CHUNK]) for i in range(2)]
        neg_q, neg_k = sb("neg_q", [P, CHUNK]), sb("neg_k", [P, CHUNK])
        exp_q, exp_k = sb("exp_q", [P, CHUNK]), sb("exp_k", [P, CHUNK])
        k_tok = sb("k_tok", [P, CHUNK])
        v_one = sb("v_one", [P, TILES, P + 1])
        kv = sb("kv", [P, P + HEADS])
        k_sum = sb("k_sum", [P, 1])
        den = sb("den", [P, TILES * HEADS])
        z = sb("z", [P, TILES * HEADS])
        attn_tok = sb("attn_tok", [P, CHUNK])
        attnT = sb("attnT", [P, CHUNK])
        n1 = sb("n1", [P, CHUNK])
        x1T = sb("x1T", [P, CHUNK])
        hT = sb("hT", [P, FF, CHUNK])
        n2 = sb("n2", [P, CHUNK])
        uT = sb("uT", [P, CHUNK])
        x2 = sb("x2", [P, CHUNK])
        x2T = sb("x2T", [P, CHUNK])
        tT = sb("tT", [P, CHUNK])
        x3 = sb("x3", [P, CHUNK])
        x3T = [sb(f"x3T{i}", [P, CHUNK]) for i in range(2)]
        q_tok = sb("q_tok", [P, TILES, P])
        v_tok = sb("v_tok", [P, TILES, P])
        qk = [sb(f"qk{i}", [P, HEADS * P]) for i in range(2)]
        score = sb("score", [P, TILES, HEADS * HEADS])
        top = sb("top", [P, TILES, HEADS])
        prob_e = sb("prob_e", [P, TILES, HEADS * HEADS])
        total = sb("total", [P, TILES, HEADS])
        inv_total = sb("inv_total", [P, TILES, HEADS])
        prob = sb("prob", [P, TILES, HEADS * HEADS])
        pv = [sb(f"pv{i}", [P, HEADS * P]) for i in range(TILES)]
        oT = sb("oT", [P, CHUNK])
        x4 = [sb(f"x4{i}", [P, CHUNK]) for i in range(2)]

        norms = range(1, 7)
        stats = {k: sb(f"stats{k}", [P, TILES, 6]) for k in norms}
        mean_var = {k: sb(f"mean_var{k}", [P, TILES, 2]) for k in norms}
        minus_mean = {k: sb(f"minus_mean{k}", [P, TILES]) for k in norms}
        var_eps = {k: sb(f"var_eps{k}", [P, TILES]) for k in norms}
        rstd = {k: sb(f"rstd{k}", [P, TILES]) for k in norms}
        shift = {k: sb(f"shift{k}", [P, TILES]) for k in norms}
        stats_done = {k: sem(f"stats_done{k}") for k in norms}
        mean_done = {k: sem(f"mean_done{k}") for k in norms}
        moments_ready = {k: sem(f"moments_ready{k}") for k in norms}
        rstd_ready = {k: sem(f"rstd_ready{k}") for k in norms}
        shift_ready = {k: sem(f"shift_ready{k}") for k in norms}
        normed = {k: sem(f"normed{k}") for k in norms}

        y_tok = [sb(f"y_tok{i}", [P, CHUNK]) for i in range(2)]
        yT = sb("yT", [P, CHUNK])
        gate = sb("gate", [P, TILES, EXPERTS])
        gate_top = sb("gate_top", [P, TILES])
        gate_is = sb("gate_is", [P, TILES, EXPERTS])
        gate_pref = sb("gate_pref", [P, TILES, EXPERTS])
        gate_first = sb("gate_first", [P, TILES])
        chosen = sb("chosen", [P, TILES, EXPERTS], BF16)
        chosenT = sb("chosenT", [EXPERTS, CHUNK], BF16)
        chosenTf = sb("chosenTf", [EXPERTS, CHUNK])
        masked = [sb(f"masked{i}", [P, CHUNK]) for i in range(2)]
        gT = sb("gT", [P, CHUNK])
        moeT = sb("moeT", [P, CHUNK])
        result = [sb(f"result{i}", [P, CHUNK]) for i in range(2)]

        weights_in = sem("weights_in")
        x_in = [sem(f"x_in{i}") for i in range(2)]
        consts = sem("consts")
        pool_prep = sem("pool_prep")
        dve_prep = sem("dve_prep")
        prep_mm = sem("prep_mm")
        prep_out = sem("prep_out")
        kv_bias_ready = sem("kv_bias_ready")
        rows_split = sem("rows_split")
        bias3_in = sem("bias3_in")
        xT_psum, xT_ready = sem("xT_psum"), sem("xT_ready")
        q_psum, q_neg, q_exp, q_ready = sem("q_psum"), sem("q_neg"), sem("q_exp"), sem("q_ready")
        k_psum, k_neg, k_exp, k_ready = sem("k_psum"), sem("k_neg"), sem("k_exp"), sem("k_ready")
        v_psum, v_ready = sem("v_psum"), sem("v_ready")
        kv_psum, kv_sum, kv_ready = sem("kv_psum"), sem("kv_sum"), sem("kv_ready")
        den_psum, den_ready, z_ready = sem("den_psum"), sem("den_ready"), sem("z_ready")
        num_psum, attn_ready = sem("num_psum"), sem("attn_ready")
        attnT_psum, attnT_ready = sem("attnT_psum"), sem("attnT_ready")
        s_psum = {k: sem(f"s_psum{k}") for k in norms}
        n1T_psum, x1T_ready = sem("n1T_psum"), sem("x1T_ready")
        h_psum, h_act, h_dve = sem("h_psum"), sem("h_act"), sem("h_dve")
        n2T_psum, uT_ready = sem("n2T_psum"), sem("uT_ready")
        x2T_psum, x2T_ready = sem("x2T_psum"), sem("x2T_ready")
        t_psum, tT_ready = sem("t_psum"), sem("tT_ready")
        x3T_psum, x3T_ready = sem("x3T_psum"), sem("x3T_ready")
        qkv_psum, qv_ready = sem("qkv_psum"), sem("qv_ready")
        qk_ready, score_ready = sem("qk_ready"), sem("score_ready")
        top_ready, below_top, exp_ready = sem("top_ready"), sem("below_top"), sem("exp_ready")
        total_ready, inv_ready, prob_ready = sem("total_ready"), sem("inv_ready"), sem("prob_ready")
        pv_ready, o_psum, oT_ready = sem("pv_ready"), sem("o_psum"), sem("oT_ready")
        x4_out = [sem(f"x4_out{i}") for i in range(2)]
        y_in = [sem(f"y_in{i}") for i in range(2)]
        yT_psum, yT_ready = sem("yT_psum"), sem("yT_ready")
        gate_psum, gate_ready, gate_step = sem("gate_psum"), sem("gate_ready"), sem("gate_step")
        chosen_ready, chosenT_psum, chosenT_ready = sem("chosen_ready"), sem("chosenT_psum"), sem("chosenT_ready")
        mask_psum, masked_ready, used = sem("mask_psum"), sem("masked_ready"), sem("used")
        pre_psum, gT_ready = sem("pre_psum"), sem("gT_ready")
        moe_psum, moeT_ready = sem("moe_psum"), sem("moeT_ready")
        result_out = [sem(f"result_out{i}") for i in range(2)]

        loads = [
            (wq, t["L0_attn_Wq"]), (wk, t["L0_attn_Wk"]), (wv, t["L0_attn_Wv"]), (wo, t["L0_attn_Wo"]),
            (w1, t["L0_attn_W1"]), (w2, t["L0_attn_W2"].rearrange("(f p) n -> p f n", p=P)),
            (wt[0], t["L0_ffn_weight"]), (wt[1], t["L0_ffn_aux_weight1"]), (wt[2], t["L0_ffn_aux_weight2"]),
            (w_qkv[:, 0:P], t["L1_attn_Wq"]), (wdown, t["L1_attn_Wdown"]), (wup, t["L1_attn_Wup"]),
            (bdown, t["L1_attn_bdown"].rearrange("(p a) -> p a", a=1)),
            (wout, t["L1_attn_Wout"]), (wg, t["L1_ffn_Wg"]),
            (e1, t["L1_ffn_W1"].rearrange("e p i -> p e i")),
            (e2, t["L1_ffn_W2"].rearrange("e p i -> p e i")),
            (eb1, t["L1_ffn_b1"]), (eb2, t["L1_ffn_b2"]),
            (col_rows[0:FF, :], t["L0_attn_b1"].rearrange("(f p) -> f p", p=P)),
        ]
        for i, name in enumerate(("L0_ffn_bias", "L0_attn_g1", "L0_attn_beta1", "L0_attn_g2", "L0_attn_beta2")):
            loads.append((col_rows[FF + i:FF + i + 1, :], t[name].rearrange("(a p) -> a p", a=1)))
        for key, name in (("bq", "L0_attn_bq"), ("bk", "L0_attn_bk"), ("bv", "L0_attn_bv"), ("bo", "L0_attn_bo"),
                          ("b2", "L0_attn_b2"), ("bout", "L1_attn_bout"), ("bqkv", "L1_attn_bq")):
            loads.append((rows[:, ROW[key] * P:(ROW[key] + 1) * P], t[name].rearrange("(a n) -> a n", a=1)))
        loads.append((rows[:, (ROW["bqkv"] + 1) * P:(ROW["bqkv"] + 3) * P], t["L1_attn_bup"].rearrange("(a n) -> a n", a=1)))
        loads.append((rows[:, N_ROWS * P:], t["L1_ffn_bg"].rearrange("(a n) -> a n", a=1)))
        all_loads = 16 * len(loads)
        b1_col, tanh_col, g1_col, beta1_col, g2_col, beta2_col = (
            0, *(FF + i for i in range(5)))

        def col(i):
            return cols[:, i:i + 1]

        def tile(a, j):
            return a[:, j * P:(j + 1) * P]

        block = ctx.enter_context(nc.Block())

        @block.sync
        def _(sp):
            def load_x(st):
                if not st.runs(LAG_IN):
                    return
                st.wait(sp, xT_psum, LAG_IN, before=2)
                sp.dma_start(x_tok[st.buf(LAG_IN)][:], x_d[st.chunk(LAG_IN)]).then_inc(x_in[st.buf(LAG_IN)], 16)

            def store_x4(st):
                if not st.runs(LAG_OUT):
                    return
                st.wait(sp, normed[5], LAG_OUT)
                sp.dma_start(scratch_d[st.chunk(LAG_OUT)], x4[st.buf(LAG_OUT)][:]).then_inc(x4_out[st.buf(LAG_OUT)], 16)

            def body(st):
                load_x(st)
                if st.inside is not None or st.s >= LAG_OUT:
                    store_x4(st)

            sp.dma_start(x_tok[0][:], x_d[0]).then_inc(x_in[0], 16)
            for dst, src in loads:
                sp.dma_start(dst[:], src).then_inc(weights_in, 16)
            sp.wait_ge(rows_split, 5)
            sp.dma_start(bias3[0:3, :], parts[0:1, :, :]).then_inc(bias3_in, 16)
            for s in range(1, LAG_OUT):
                body(Step(s, chunks))
            with sp.Fori(LAG_OUT // 2, chunks // 2) as pair:
                for u in range(2):
                    body(Step(2 * pair + u, chunks, inside=u, pair=pair))
            for s in range(chunks, chunks + LAG_OUT):
                body(Step(s, chunks))

            for i in range(2):
                sp.wait_ge(x4_out[i], 16 * (chunks // 2))

            def load_y(c, u, first):
                if not first:
                    sp.wait_ge(normed[6], c - 1)
                sp.dma_start(y_tok[u][:], scratch_d[c]).then_inc(y_in[u], 16)

            def store(c, u):
                sp.wait_ge(normed[6], c + 1)
                sp.dma_start(out_d[c], result[u][:]).then_inc(result_out[u], 16)

            load_y(0, 0, True)
            load_y(1, 1, True)
            with sp.Fori(0, chunks // 2 - 1) as pair:
                for u in range(2):
                    store(2 * pair + u, u)
                    load_y(2 * pair + u + 2, u, False)
            for u in range(2):
                store(chunks - 2 + u, u)
            for u in range(2):
                sp.wait_ge(result_out[u], 16 * (chunks // 2))

        @block.tensor
        def _(pe):
            def mm(out_, lhsT, rhs, start=False, stop=False):
                return pe.matmul(out_, lhsT, rhs, start=start, stop=stop, skip_group_check=True)

            def turn(out_, in_, start=True, stop=True):
                return pe.matmul(out_, in_, ident[:], is_transpose=True, start=start, stop=stop,
                                 skip_group_check=True)

            def turn4(out_, in_, start=True, stop=True):
                for j in range(TILES):
                    last = turn(tile(out_, j), tile(in_, j), start=start and j == 0, stop=stop)
                return last

            pe.wait_ge(consts, 1)
            pe.wait_ge(weights_in, all_loads)
            turn(bank[0][:, 0:P], wt[0][:]).then_inc(prep_mm, 1)
            pe.matmul(bank[1][0:LATENT, 0:P], wdown[:], ident[:], is_transpose=True,
                      start=True, stop=True).then_inc(prep_mm, 1)
            pe.matmul(bank[3][:, 0:FF + 5], col_rows[:], ident[0:FF + 5, 0:FF + 5], is_transpose=True,
                      start=True, stop=True).then_inc(prep_mm, 1)
            pe.wait_ge(prep_out, 1)
            mm(bank[0][:, 0:P], wt[1][:], wtT[:], True, True).then_inc(prep_mm, 1)
            pe.wait_ge(prep_out, 2)
            mm(bank[1][:, 0:2 * P], wdownT[:], wup[:], True, True).then_inc(prep_mm, 1)
            mm(bank[2][0:1, 0:2 * P], bdown[:], wup[:], True, True).then_inc(prep_mm, 1)
            pe.wait_ge(prep_out, 4)
            mm(bank[0][:, 0:P], wt01T[:], wt[2][:], True, True).then_inc(prep_mm, 1)
            pe.wait_ge(kv_bias_ready, 1)
            pe.wait_ge(prep_out, 6)
            pe.wait_ge(bias3_in, 16)
            pe.wait_ge(dve_prep, 7 + EXPERTS)

            def xT_mm(st):
                if not st.runs(LAG_IN):
                    return
                b = st.buf(LAG_IN)
                pe.wait_ge(x_in[b], 16 * (st.batch(LAG_IN) + 1))
                st.wait(pe, normed[3], LAG_MLP, before=1)
                turn4(bank[0], x_tok[b]).then_inc(xT_psum, 1)

            def qkv_in(st):
                if not st.runs(LAG_IN):
                    return
                x = xT[st.buf(LAG_IN)]
                st.wait(pe, xT_ready, LAG_IN)
                if st.done(LAG_MLP, 1) if st.inside is None else True:
                    st.wait(pe, normed[2], LAG_MLP, before=1)
                else:
                    st.wait(pe, q_ready, LAG_IN, before=1)
                mm(bank[3][:], row3("bq"), ones_bf[:], start=True)
                mm(bank[3][:], wq[:], x[:], stop=True).then_inc(q_psum, 1)
                st.wait(pe, uT_ready, LAG_MLP, before=1)
                mm(bank[4][:], ones_bf[:, 0:P], row3_by_tile("bk"), start=True)
                for j in range(TILES):
                    last = mm(tile(bank[4], j), tile(x, j), wk[:], stop=True)
                last.then_inc(k_psum, 1)
                st.wait(pe, x3T_ready, LAG_TANH, before=1)
                mm(bank[5][:], ones_bf[:, 0:P], row3_by_tile("bv"), start=True)
                for j in range(TILES):
                    last = mm(tile(bank[5], j), tile(x, j), wv[:], stop=True)
                last.then_inc(v_psum, 1)

            def kv_sums(st):
                if not st.runs(LAG_IN):
                    return
                st.wait(pe, k_ready, LAG_IN)
                st.wait(pe, v_ready, LAG_IN)
                first = st.buf(LAG_IN) == 0
                if first and (st.inside is not None or st.s >= 2):
                    pe.wait_ge(kv_ready, st.batch(LAG_IN))
                for j in range(TILES):
                    last = mm(kv_acc[:, 0:P + 1], tile(k_tok, j), v_one[:, j, :], start=first and j == 0,
                              stop=not first and j == TILES - 1)
                last.then_inc(kv_psum, 1)

            def linear_attn(st):
                if not st.runs(LAG_MLP):
                    return
                q = qT[st.buf(LAG_MLP)]
                pe.wait_ge(kv_ready, st.batch(LAG_MLP) + 1)
                if st.runs(LAG_IN):
                    st.wait(pe, q_ready, LAG_IN)
                else:
                    st.wait(pe, q_ready, LAG_MLP)
                    st.wait(pe, normed[2], LAG_MLP, before=1)
                for j in range(TILES):
                    last = mm(bank[3][:, j * HEADS:(j + 1) * HEADS], tile(q, j), kv[:, P:], start=j == 0, stop=True)
                last.then_inc(den_psum, 1)
                if st.runs(LAG_IN):
                    st.wait(pe, xT_ready, LAG_IN)
                else:
                    st.wait(pe, normed[3], LAG_MLP, before=1)
                for j in range(TILES):
                    last = mm(tile(bank[0], j), tile(q, j), kv[:, 0:P], start=j == 0, stop=True)
                last.then_inc(num_psum, 1)

            def attnT_mm(st):
                if not st.runs(LAG_MLP):
                    return
                st.wait(pe, attn_ready, LAG_MLP)
                turn4(bank[0], attn_tok).then_inc(attnT_psum, 1)

            def s1_mm(st):
                if not st.runs(LAG_MLP):
                    return
                st.wait(pe, attnT_ready, LAG_MLP)
                st.wait(pe, den_ready, LAG_MLP)
                mm(bank[3][:], ones_bf[:, 0:P], row3_by_tile("bo"), start=True)
                turn4(bank[3], xT[st.buf(LAG_MLP)], start=False)
                for j in range(TILES):
                    last = mm(tile(bank[3], j), tile(attnT, j), wo[:], stop=True)
                last.then_inc(s_psum[1], 1)

            def x1T_mm(st):
                if not st.runs(LAG_MLP):
                    return
                st.wait(pe, normed[1], LAG_MLP)
                st.wait(pe, attnT_ready, LAG_MLP)
                turn4(bank[0], n1).then_inc(n1T_psum, 1)

            def mlp(st):
                if not st.runs(LAG_MLP):
                    return
                st.wait(pe, x1T_ready, LAG_MLP)
                st.wait(pe, tT_ready, LAG_TANH)
                mm(bank[2][:], w1[:, 0:P], x1T[:], True, True).then_inc(h_psum, 1)
                st.wait(pe, qk_ready, LAG_HEADS, per=TILES, short=2)
                mm(bank[4][:], w1[:, P:2 * P], x1T[:], True, True).then_inc(h_psum, 1)
                mm(bank[0][:], w1[:, 2 * P:3 * P], x1T[:], True, True).then_inc(h_psum, 1)
                st.wait(pe, h_act, LAG_MLP, per=2, short=1)
                mm(bank[2][:], w1[:, 3 * P:4 * P], x1T[:], True, True).then_inc(h_psum, 1)
                mm(bank[3][:], ones_bf[:, 0:P], row3_by_tile("b2"), start=True)
                turn4(bank[3], x1T, start=False)
                for f in range(FF):
                    if f % 2 == 0:
                        st.wait(pe, h_act, LAG_MLP, per=2, short=1 - f // 2)
                    else:
                        st.wait(pe, h_dve, LAG_MLP, per=2, short=1 - f // 2)
                    for j in range(TILES):
                        last = mm(tile(bank[3], j), tile(hT[:, f, :], j), w2[:, f, :], stop=f == FF - 1)
                last.then_inc(s_psum[2], 1)

            def n2T_mm(st):
                if not st.runs(LAG_MLP):
                    return
                st.wait(pe, normed[2], LAG_MLP)
                turn4(bank[4], n2).then_inc(n2T_psum, 1)

            def s3_mm(st):
                if not st.runs(LAG_MLP):
                    return
                st.wait(pe, uT_ready, LAG_MLP)
                turn4(bank[0], xT[st.buf(LAG_MLP)], stop=False)
                turn4(bank[0], uT, start=False).then_inc(s_psum[3], 1)

            def x2T_mm(st):
                if not st.runs(LAG_TANH):
                    return
                st.wait(pe, normed[3], LAG_TANH)
                if st.runs(LAG_IN):
                    st.wait(pe, v_ready, LAG_IN)
                else:
                    st.wait(pe, x3T_ready, LAG_TANH, before=1)
                turn4(bank[5], x2).then_inc(x2T_psum, 1)

            def tanh_mm(st):
                if not st.runs(LAG_TANH):
                    return
                st.wait(pe, x2T_ready, LAG_TANH)
                st.wait(pe, normed[5], LAG_OUT, before=1)
                mm(bank[2][:], w_tanh[:], x2T[:], True, True).then_inc(t_psum, 1)

            def s4_mm(st):
                if not st.runs(LAG_TANH):
                    return
                st.wait(pe, tT_ready, LAG_TANH)
                turn4(bank[5], x2T, stop=False)
                turn4(bank[5], tT, start=False).then_inc(s_psum[4], 1)

            def x3T_mm(st):
                if not st.runs(LAG_TANH):
                    return
                st.wait(pe, normed[4], LAG_TANH)
                turn4(bank[5], x3).then_inc(x3T_psum, 1)

            def heads_qkv(st, j):
                if not st.runs(LAG_HEADS):
                    return
                x = x3T[st.buf(LAG_HEADS)]
                st.wait(pe, x3T_ready, LAG_HEADS)
                if j == 0:
                    st.wait(pe, qk_ready, LAG_HEADS, per=TILES, before=1)
                elif j == 1 and st.runs(LAG_IN):
                    st.wait(pe, k_ready, LAG_IN)
                elif j == 1:
                    st.wait(pe, uT_ready, LAG_MLP, before=1)
                elif j == 2:
                    st.wait(pe, qk_ready, LAG_HEADS, per=TILES, short=3)
                else:
                    st.wait(pe, qk_ready, LAG_HEADS, per=TILES, short=1)
                b = bank[4 if j == 1 else 1][:, 0:3 * P]
                mm(b, ones_bf[:, 0:P], row3("bqkv", 3), start=True)
                mm(b, tile(x, j), w_qkv[:], stop=True).then_inc(qkv_psum, 1)

            def o_sums(st, tiles):
                if not st.runs(LAG_OUT):
                    return
                for j in tiles:
                    st.wait(pe, pv_ready, LAG_OUT, per=TILES, short=TILES - 1 - j)
                    if j == 0:
                        st.wait(pe, oT_ready, LAG_OUT, before=1)
                    for g in range(HEADS):
                        last = turn(tile(o_acc, j), tile(pv[j], g), start=g == 0, stop=g == HEADS - 1)
                    last.then_inc(o_psum, 1)

            def s5_mm(st):
                if not st.runs(LAG_OUT):
                    return
                st.wait(pe, oT_ready, LAG_OUT)
                st.wait(pe, h_dve, LAG_MLP, per=2)
                if st.runs(LAG_TANH):
                    st.wait(pe, tT_ready, LAG_TANH)
                else:
                    st.wait(pe, normed[5], LAG_OUT, before=1)
                mm(bank[2][:], ones_bf[:, 0:P], row3_by_tile("bout"), start=True)
                turn4(bank[2], x3T[st.buf(LAG_OUT)], start=False)
                for j in range(TILES):
                    last = mm(tile(bank[2], j), tile(oT, j), wout[:], stop=True)
                last.then_inc(s_psum[5], 1)

            def body(st):
                xT_mm(st)
                heads_qkv(st, 0)
                o_sums(st, (0, 1))
                qkv_in(st)
                kv_sums(st)
                linear_attn(st)
                heads_qkv(st, 1)
                o_sums(st, (2,))
                x2T_mm(st)
                attnT_mm(st)
                tanh_mm(st)
                s1_mm(st)
                o_sums(st, (3,))
                heads_qkv(st, 2)
                s4_mm(st)
                x1T_mm(st)
                mlp(st)
                s5_mm(st)
                x3T_mm(st)
                heads_qkv(st, 3)
                n2T_mm(st)
                s3_mm(st)

            run_steps(pe, chunks, body)

            def moe(c, u, pair):
                pe.wait_ge(y_in[u], 16 * (pair + 1))
                turn4(bank[0], y_tok[u]).then_inc(yT_psum, 1)
                pe.wait_ge(yT_ready, c + 1)
                mm(bank[1][:, 0:TILES * EXPERTS], ones_bf[:, 0:P],
                   bias3[:, N_ROWS * P:].unsqueeze(1).broadcast_to([P, TILES, EXPERTS]), start=True)
                for j in range(TILES):
                    last = mm(bank[1][:, j * EXPERTS:(j + 1) * EXPERTS], tile(yT, j), wg[:], stop=True)
                last.then_inc(gate_psum, 1)
                pe.wait_ge(chosen_ready, c + 1)
                chT = bank[0][0:EXPERTS, 0:CHUNK // 2].bitcast(BF16)
                for j in range(TILES):
                    last = pe.matmul(chT[:, j * P:(j + 1) * P], chosen[:, j, :], ident_bf[:], is_transpose=True,
                                     start=True, stop=True, skip_group_check=True)
                last.then_inc(chosenT_psum, 1)
                pe.wait_ge(chosenT_ready, 2 * (c + 1))
                for layer, (w, b, acc, ready) in enumerate(((e1, eb1, bank[4], pre_psum), (e2, eb2, bank[5], moe_psum))):
                    if layer:
                        pe.wait_ge(gT_ready, c + 1)
                    mm(acc[:], b[:], chosenTf[:], start=True)
                    for e in range(EXPERTS + 1):
                        if e < EXPERTS:
                            n = 2 * EXPERTS * c + layer * EXPERTS + e
                            if layer or e >= 2:
                                pe.wait_ge(masked_ready, n - 1)
                            mm(bank[2 + e % 2][:], pick[:, e, :], chosenT[:], True, True).then_inc(mask_psum, 1)
                        if e > 0:
                            n = 2 * EXPERTS * c + layer * EXPERTS + e
                            pe.wait_ge(masked_ready, n)
                            last = mm(acc[:], w[:, e - 1, :], masked[(e - 1) % 2][:], stop=e == EXPERTS)
                            last.then_inc(used, 1)
                            if e == EXPERTS:
                                pass
                pe.wait_ge(moeT_ready, c + 1)
                turn4(bank[6], yT, stop=False)
                turn4(bank[6], moeT, start=False).then_inc(s_psum[6], 1)

            with pe.Fori(0, chunks // 2) as pair:
                for u in range(2):
                    moe(2 * pair + u, u, pair)

        @block.scalar
        def _(act):
            def normalise(st, k, lag, src, dst):
                st.wait(act, shift_ready[k], lag)
                for j in range(TILES):
                    last = act.activation(tile(dst, j), tile(src, j), ACT.Identity,
                                          bias=shift[k][:, j:j + 1], scale=rstd[k][:, j:j + 1])
                last.then_inc(normed[k], 1)

            act.wait_ge(prep_mm, 1)
            act.activation(wtT[:], bank[0][:, 0:P], ACT.Copy).then_inc(prep_out, 1)
            act.wait_ge(prep_mm, 2)
            act.activation(wdownT[:], bank[1][0:LATENT, 0:P], ACT.Copy).then_inc(prep_out, 1)
            act.wait_ge(prep_mm, 3)
            act.activation(cols[:], bank[3][:, 0:FF + 5], ACT.Copy).then_inc(prep_out, 1)
            act.wait_ge(prep_mm, 4)
            act.activation(wt01T[:], bank[0][:, 0:P], ACT.Copy).then_inc(prep_out, 1)
            act.wait_ge(prep_mm, 5)
            act.activation(w_qkv[:, P:3 * P], bank[1][:, 0:2 * P], ACT.Copy).then_inc(prep_out, 1)
            act.wait_ge(prep_mm, 7)
            act.activation(w_tanh[:], bank[0][:, 0:P], ACT.Copy).then_inc(prep_out, 1)

            def xT_copy(st):
                if not st.runs(LAG_IN):
                    return
                st.wait(act, xT_psum, LAG_IN)
                st.wait(act, s_psum[3], LAG_MLP, before=1)
                act.activation(xT[st.buf(LAG_IN)][:], bank[0][:], ACT.Copy).then_inc(xT_ready, 1)

            def elu(st, psum, psum_bank, neg, neg_done, exp, exp_done, ready):
                st.wait(act, psum, LAG_IN)
                st.wait(act, exp_done, LAG_IN, before=1)
                act.activation(neg[:], psum_bank[:], ACT.Relu, scale=-1.0).then_inc(neg_done, 1)
                st.wait(act, neg_done, LAG_IN)
                st.wait(act, ready, LAG_IN, before=1)
                act.activation(exp[:], neg[:], ACT.Exp, scale=-1.0).then_inc(exp_done, 1)

            def q_k_v(st):
                if not st.runs(LAG_IN):
                    return
                elu(st, q_psum, bank[3], neg_q, q_neg, exp_q, q_exp, q_ready)
                elu(st, k_psum, bank[4], neg_k, k_neg, exp_k, k_exp, k_ready)
                st.wait(act, v_psum, LAG_IN)
                st.wait(act, kv_psum, LAG_IN, before=1)
                act.activation(v_one[:, :, 0:P], bank[5][:].rearrange("p (j d) -> p j d", j=TILES),
                               ACT.Copy).then_inc(v_ready, 1)

            def attnT_copy(st):
                if not st.runs(LAG_MLP):
                    return
                st.wait(act, attnT_psum, LAG_MLP)
                act.activation(attnT[:], bank[0][:], ACT.Copy).then_inc(attnT_ready, 1)

            def n1_act(st):
                if st.runs(LAG_MLP):
                    normalise(st, 1, LAG_MLP, bank[3], n1)

            def x1T_act(st):
                if not st.runs(LAG_MLP):
                    return
                st.wait(act, n1T_psum, LAG_MLP)
                act.activation(x1T[:], bank[0][:], ACT.Identity, bias=col(beta1_col),
                               scale=col(g1_col)).then_inc(x1T_ready, 1)

            def relu_act(st):
                if not st.runs(LAG_MLP):
                    return
                for f in (0, 2):
                    st.wait(act, h_psum, LAG_MLP, per=FF, short=FF - 1 - f)
                    act.activation(hT[:, f, :], bank[2 if f == 0 else 0][:], ACT.Relu,
                                   bias=col(b1_col + f)).then_inc(h_act, 1)

            def n2_act(st):
                if st.runs(LAG_MLP):
                    normalise(st, 2, LAG_MLP, bank[3], n2)

            def uT_act(st):
                if not st.runs(LAG_MLP):
                    return
                st.wait(act, n2T_psum, LAG_MLP)
                act.activation(uT[:], bank[4][:], ACT.Identity, bias=col(beta2_col),
                               scale=col(g2_col)).then_inc(uT_ready, 1)

            def x2_act(st):
                if st.runs(LAG_MLP):
                    st.wait(act, x2T_psum, LAG_MLP, before=1)
                    normalise(st, 3, LAG_MLP, bank[0], x2)

            def x2T_copy(st):
                if not st.runs(LAG_TANH):
                    return
                st.wait(act, x2T_psum, LAG_TANH)
                act.activation(x2T[:], bank[5][:], ACT.Copy).then_inc(x2T_ready, 1)

            def tanh_act(st):
                if not st.runs(LAG_TANH):
                    return
                st.wait(act, t_psum, LAG_TANH)
                act.activation(tT[:], bank[2][:], ACT.Tanh, bias=col(tanh_col)).then_inc(tT_ready, 1)

            def x3_act(st):
                if st.runs(LAG_TANH):
                    normalise(st, 4, LAG_TANH, bank[5], x3)

            def x3T_copy(st):
                if not st.runs(LAG_TANH):
                    return
                st.wait(act, x3T_psum, LAG_TANH)
                st.wait(act, s_psum[5], LAG_OUT)
                act.activation(x3T[st.buf(LAG_TANH)][:], bank[5][:], ACT.Copy).then_inc(x3T_ready, 1)

            def qv_copy(st, j):
                if not st.runs(LAG_HEADS):
                    return
                b = bank[4 if j == 1 else 1]
                st.wait(act, qkv_psum, LAG_HEADS, per=TILES, short=TILES - 1 - j)
                st.wait(act, qk_ready, LAG_HEADS, per=TILES, short=TILES - 1 - j, before=1)
                st.wait(act, pv_ready, LAG_OUT, per=TILES, short=TILES - 1 - j)
                act.activation(q_tok[:, j, :], b[:, 0:P], ACT.Copy)
                act.activation(v_tok[:, j, :].rearrange("p (g d) -> p g d", g=HEADS),
                               b[:, P:3 * P].rearrange("p (g w) -> p g w", g=HEADS)[:, :, HD:],
                               ACT.Copy).then_inc(qv_ready, 1)

            def prob_exp(st, pair):
                if not st.runs(LAG_HEADS):
                    return
                st.wait(act, below_top, LAG_HEADS, per=2, short=1 - pair)
                st.wait(act, prob_ready, LAG_HEADS, per=2, short=1 - pair, before=1)
                act.activation(prob_e[:, 2 * pair:2 * pair + 2, :], score[:, 2 * pair:2 * pair + 2, :], ACT.Exp,
                               scale=float(HD) ** -0.5).then_inc(exp_ready, 1)

            def oT_copy(st):
                if not st.runs(LAG_OUT):
                    return
                st.wait(act, o_psum, LAG_OUT, per=TILES)
                act.activation(oT[:], o_acc[:], ACT.Copy).then_inc(oT_ready, 1)

            def x4_act(st):
                if not st.runs(LAG_OUT):
                    return
                b = st.buf(LAG_OUT)
                if st.inside is not None or st.s - LAG_OUT >= 2:
                    act.wait_ge(x4_out[b], 16 * st.batch(LAG_OUT))
                normalise(st, 5, LAG_OUT, bank[2], x4[b])

            def body(st):
                xT_copy(st)
                qv_copy(st, 0)
                q_k_v(st)
                qv_copy(st, 1)
                x2T_copy(st)
                attnT_copy(st)
                tanh_act(st)
                n1_act(st)
                oT_copy(st)
                qv_copy(st, 2)
                prob_exp(st, 0)
                x3_act(st)
                x1T_act(st)
                relu_act(st)
                n2_act(st)
                x4_act(st)
                x3T_copy(st)
                qv_copy(st, 3)
                uT_act(st)
                x2_act(st)
                prob_exp(st, 1)

            run_steps(act, chunks, body)

            def moe(c, u, pair):
                act.wait_ge(yT_psum, c + 1)
                act.activation(yT[:], bank[0][:], ACT.Copy).then_inc(yT_ready, 1)
                act.wait_ge(chosenT_psum, c + 1)
                chT = bank[0][0:EXPERTS, 0:CHUNK // 2].bitcast(BF16)
                act.activation(chosenT[:], chT, ACT.Copy).then_inc(chosenT_ready, 1)
                act.activation(chosenTf[:], chT, ACT.Copy).then_inc(chosenT_ready, 1)
                act.wait_ge(used, 2 * EXPERTS * c + EXPERTS)
                act.activation(gT[:], bank[4][:], ACT.Gelu).then_inc(gT_ready, 1)
                act.wait_ge(used, 2 * EXPERTS * (c + 1))
                act.activation(moeT[:], bank[5][:], ACT.Copy).then_inc(moeT_ready, 1)
                act.wait_ge(result_out[u], 16 * pair)
                act.wait_ge(shift_ready[6], c + 1)
                for j in range(TILES):
                    last = act.activation(tile(result[u], j), tile(bank[6], j), ACT.Identity,
                                          bias=shift[6][:, j:j + 1], scale=rstd[6][:, j:j + 1])
                last.then_inc(normed[6], 1)

            with act.Fori(0, chunks // 2) as pair:
                for u in range(2):
                    moe(2 * pair + u, u, pair)

        @block.vector
        def _(dve):
            dve.memset(ones_bf[:], 1.0).then_inc(dve_prep, 1)
            dve.memset(v_one[:, :, P:], 1.0).then_inc(dve_prep, 1)
            dve.memset(minus_half[:], -0.5).then_inc(dve_prep, 1)
            dve.memset(bias3[:], 0.0).then_inc(dve_prep, 1)
            dve.wait_ge(consts, 1)
            dve.tensor_copy(ident_bf[:], ident[:]).then_inc(dve_prep, 1)
            dve.wait_ge(pool_prep, 4)
            dve.tensor_copy(head_mask[:].rearrange("p (h m) -> p h m", h=HEADS),
                            head_of[:].unsqueeze(2).broadcast_to([P, HEADS, HD])).then_inc(dve_prep, 1)
            dve.wait_ge(pool_prep, 6)
            dve.tensor_copy(pick[:], pick_f[:]).then_inc(dve_prep, 1)
            for e in range(EXPERTS):
                dve.memset(prefer[:, e:e + 1], float(EXPERTS - e)).then_inc(dve_prep, 1)
            dve.wait_ge(dve_prep, 7 + EXPERTS)
            up = rows[:, (ROW["bqkv"] + 1) * P:(ROW["bqkv"] + 3) * P]
            dve.wait_ge(prep_mm, 6)
            dve.tensor_tensor(up, bank[2][0:1, 0:2 * P], up, ALU.add).then_inc(kv_bias_ready, 1)
            dve.wait_ge(kv_bias_ready, 1)
            dve.tensor_copy(parts[:, 0, :], rows[:]).then_inc(rows_split, 1)
            dve.wait_ge(rows_split, 1)
            dve.tensor_tensor(rows_left[:], rows[:], parts[:, 0, :], ALU.subtract).then_inc(rows_split, 1)
            dve.wait_ge(rows_split, 2)
            dve.tensor_copy(parts[:, 1, :], rows_left[:]).then_inc(rows_split, 1)
            dve.wait_ge(rows_split, 3)
            dve.tensor_tensor(rows_left[:], rows_left[:], parts[:, 1, :], ALU.subtract).then_inc(rows_split, 1)
            dve.wait_ge(rows_split, 4)
            dve.tensor_copy(parts[:, 2, :], rows_left[:]).then_inc(rows_split, 1)

            def moments(n, k, src):
                for j in range(TILES):
                    last = dve.bn_stats(stats[k][:, j, :], tile(src, j))
                last.then_inc(stats_done[k], 1)
                dve.wait_ge(dve_prep, 1)
                dve.wait_ge(stats_done[k], n)
                for j in range(TILES):
                    last = dve.bn_aggr(mean_var[k][:, j, :], stats[k][:, j, :])
                last.then_inc(mean_done[k], 1)
                dve.wait_ge(mean_done[k], n)
                dve.tensor_scalar(minus_mean[k][:], mean_var[k][:, :, 0], -1.0, None, ALU.mult)
                dve.tensor_scalar(var_eps[k][:], mean_var[k][:, :, 1], EPS_LN, None, ALU.add).then_inc(moments_ready[k], 1)

            def elu_q(st):
                if not st.runs(LAG_IN):
                    return
                st.wait(dve, q_exp, LAG_IN)
                st.wait(dve, num_psum, LAG_IN, before=2)
                dve.scalar_tensor_tensor(qT[st.buf(LAG_IN)][:], bank[3][:], 0.0, exp_q[:], ALU.max,
                                         ALU.add).then_inc(q_ready, 1)

            def elu_k(st):
                if not st.runs(LAG_IN):
                    return
                st.wait(dve, k_exp, LAG_IN)
                st.wait(dve, kv_psum, LAG_IN, before=1)
                dve.scalar_tensor_tensor(k_tok[:], bank[4][:], 0.0, exp_k[:], ALU.max,
                                         ALU.add).then_inc(k_ready, 1)

            def kv_blocks(st):
                if not st.runs(LAG_IN) or st.buf(LAG_IN) == 0:
                    return
                st.wait(dve, kv_psum, LAG_IN)
                st.wait(dve, num_psum, LAG_MLP, before=1)
                dve.tensor_copy(k_sum[:], kv_acc[:, P:P + 1]).then_inc(kv_sum, 1)
                dve.tensor_tensor(kv[:, 0:P], kv_acc[:, 0:P], head_mask[:], ALU.mult)
                dve.wait_ge(kv_sum, st.batch(LAG_IN) + 1)
                dve.tensor_scalar(kv[:, P:], head_of[:], k_sum[:, 0:1], None, ALU.mult).then_inc(kv_ready, 1)

            def attn(st):
                if not st.runs(LAG_MLP):
                    return
                st.wait(dve, den_psum, LAG_MLP)
                dve.tensor_scalar(den[:], bank[3][:, 0:TILES * HEADS], EPS_ATTN, None, ALU.add).then_inc(den_ready, 1)
                st.wait(dve, den_ready, LAG_MLP)
                dve.reciprocal(z[:], den[:]).then_inc(z_ready, 1)
                st.wait(dve, z_ready, LAG_MLP)
                st.wait(dve, num_psum, LAG_MLP)
                dve.tensor_tensor(attn_tok[:].rearrange("p (a m) -> p a m", m=HD),
                                  bank[0][:].rearrange("p (a m) -> p a m", m=HD),
                                  z[:].unsqueeze(2).broadcast_to([P, TILES * HEADS, HD]),
                                  ALU.mult).then_inc(attn_ready, 1)

            def moments_of(st, k, lag, src):
                if st.runs(lag):
                    st.wait(dve, s_psum[k], lag)
                    moments(st.done(lag), k, src)

            def relu_dve(st):
                if not st.runs(LAG_MLP):
                    return
                for f in (1, 3):
                    st.wait(dve, h_psum, LAG_MLP, per=FF, short=FF - 1 - f)
                    dve.tensor_scalar(hT[:, f, :], bank[4 if f == 1 else 2][:], col(b1_col + f), 0.0,
                                      ALU.add, ALU.max).then_inc(h_dve, 1)

            def heads_scores(st, j):
                if not st.runs(LAG_HEADS):
                    return
                b = bank[4 if j == 1 else 1]
                k_view = b[:, P:3 * P].rearrange("p (g w) -> p g w", g=HEADS)[:, :, 0:HD]
                q_view = q_tok[:, j, :].rearrange("p (h d) -> p h d", h=HEADS)
                st.wait(dve, qv_ready, LAG_HEADS, per=TILES, short=TILES - 1 - j)
                dve.tensor_tensor(qk[j % 2][:].rearrange("p (h g d) -> p h g d", h=HEADS, g=HEADS),
                                  k_view.unsqueeze(1).broadcast_to([P, HEADS, HEADS, HD]),
                                  q_view.unsqueeze(2).broadcast_to([P, HEADS, HEADS, HD]),
                                  ALU.mult).then_inc(qk_ready, 1)
                st.wait(dve, qk_ready, LAG_HEADS, per=TILES, short=TILES - 1 - j)
                if j % 2 == 0:
                    st.wait(dve, exp_ready, LAG_HEADS, per=2, short=1 - j // 2, before=1)
                dve.tensor_reduce(score[:, j, :], qk[j % 2][:].rearrange("p (a d) -> p a d", d=HD), AX.X,
                                  ALU.add).then_inc(score_ready, 1)

            def softmax_top(st, pair):
                if not st.runs(LAG_HEADS):
                    return
                two = slice(2 * pair, 2 * pair + 2)
                view = score[:, two, :].rearrange("p j (h g) -> p (j h) g", g=HEADS)
                st.wait(dve, score_ready, LAG_HEADS, per=TILES, short=2 - 2 * pair)
                dve.tensor_reduce(top[:, two, :].rearrange("p j h -> p (j h)"), view, AX.X, ALU.max).then_inc(top_ready, 1)
                st.wait(dve, top_ready, LAG_HEADS, per=2, short=1 - pair)
                dve.tensor_tensor(view, view, top[:, two, :].rearrange("p j h -> p (j h)").unsqueeze(2)
                                  .broadcast_to([P, 2 * HEADS, HEADS]), ALU.subtract).then_inc(below_top, 1)

            def softmax_total(st, pair):
                if not st.runs(LAG_HEADS):
                    return
                two = slice(2 * pair, 2 * pair + 2)
                st.wait(dve, exp_ready, LAG_HEADS, per=2, short=1 - pair)
                dve.tensor_reduce(total[:, two, :].rearrange("p j h -> p (j h)"),
                                  prob_e[:, two, :].rearrange("p j (h g) -> p (j h) g", g=HEADS), AX.X,
                                  ALU.add).then_inc(total_ready, 1)
                st.wait(dve, total_ready, LAG_HEADS, per=2, short=1 - pair)
                st.wait(dve, prob_ready, LAG_HEADS, per=2, short=1 - pair, before=1)
                dve.reciprocal(inv_total[:, two, :], total[:, two, :]).then_inc(inv_ready, 1)

            def body(st):
                heads_scores(st, 0)
                elu_q(st)
                elu_k(st)
                kv_blocks(st)
                attn(st)
                heads_scores(st, 1)
                moments_of(st, 1, LAG_MLP, bank[3])
                softmax_top(st, 0)
                heads_scores(st, 2)
                moments_of(st, 4, LAG_TANH, bank[5])
                softmax_total(st, 0)
                relu_dve(st)
                moments_of(st, 2, LAG_MLP, bank[3])
                moments_of(st, 5, LAG_OUT, bank[2])
                heads_scores(st, 3)
                moments_of(st, 3, LAG_MLP, bank[0])
                softmax_top(st, 1)
                softmax_total(st, 1)

            run_steps(dve, chunks, body)

            def moe(c, u, pair):
                def step(n):
                    dve.wait_ge(gate_step, 5 * c + n)
                dve.wait_ge(gate_psum, c + 1)
                dve.tensor_copy(gate[:], bank[1][:, 0:TILES * EXPERTS]
                                .rearrange("p (j e) -> p j e", e=EXPERTS)).then_inc(gate_step, 1)
                step(1)
                dve.tensor_reduce(gate_top[:], gate[:], AX.X, ALU.max).then_inc(gate_step, 1)
                step(2)
                dve.tensor_tensor(gate_is[:], gate[:], gate_top[:].unsqueeze(2).broadcast_to([P, TILES, EXPERTS]),
                                  ALU.is_equal).then_inc(gate_step, 1)
                step(3)
                dve.tensor_tensor(gate_pref[:], gate_is[:], prefer[:].unsqueeze(1).broadcast_to([P, TILES, EXPERTS]),
                                  ALU.mult).then_inc(gate_step, 1)
                step(4)
                dve.tensor_reduce(gate_first[:], gate_pref[:], AX.X, ALU.max).then_inc(gate_step, 1)
                step(5)
                dve.tensor_tensor(chosen[:], gate_pref[:], gate_first[:].unsqueeze(2).broadcast_to([P, TILES, EXPERTS]),
                                  ALU.is_equal).then_inc(chosen_ready, 1)
                for layer in range(2):
                    src = gT if layer else yT
                    if layer:
                        dve.wait_ge(gT_ready, c + 1)
                    for e in range(EXPERTS):
                        n = 2 * EXPERTS * c + layer * EXPERTS + e
                        dve.wait_ge(mask_psum, n + 1)
                        if layer or e >= 2:
                            dve.wait_ge(used, n - 1)
                        dve.tensor_tensor(masked[e % 2][:], bank[2 + e % 2][:], src[:], ALU.mult).then_inc(masked_ready, 1)
                dve.wait_ge(s_psum[6], c + 1)
                moments(c + 1, 6, bank[6])

            with dve.Fori(0, chunks // 2) as pair:
                for u in range(2):
                    moe(2 * pair + u, u, pair)

        @block.gpsimd
        def _(pool):
            pool.memset(ident[:], 0.0).then_inc(pool_prep, 1)
            pool.memset(head_of[:], 1.0).then_inc(pool_prep, 1)
            pool.wait_ge(pool_prep, 2)
            pool.affine_select(out=ident[:], in_=ident[:], compare_op=ALU.not_equal, fill=1.0, base=0,
                               pattern=[[-1, P]], channel_multiplier=1).then_inc(consts, 1)
            pool.affine_select(out=head_of[:], in_=head_of[:], compare_op=ALU.is_ge, fill=0.0, base=0,
                               pattern=[[-HD, HEADS]], channel_multiplier=1).then_inc(pool_prep, 1)
            pool.wait_ge(pool_prep, 3)
            pool.affine_select(out=head_of[:], in_=head_of[:], compare_op=ALU.is_ge, fill=0.0, base=HD - 1,
                               pattern=[[HD, HEADS]], channel_multiplier=-1).then_inc(pool_prep, 1)
            pool.memset(pick_f[:], 0.0).then_inc(pool_prep, 1)
            pool.wait_ge(pool_prep, 5)
            pool.affine_select(out=pick_f[:], in_=pick_f[:], compare_op=ALU.not_equal, fill=1.0, base=0,
                               pattern=[[-1, EXPERTS], [0, P]], channel_multiplier=1).then_inc(pool_prep, 1)

            def rsqrt(n, k):
                pool.wait_ge(moments_ready[k], n)
                pool.tensor_tensor(rstd[k][:], var_eps[k][:], minus_half[:], ALU.pow).then_inc(rstd_ready[k], 1)
                pool.wait_ge(rstd_ready[k], n)
                pool.tensor_tensor(shift[k][:], minus_mean[k][:], rstd[k][:], ALU.mult).then_inc(shift_ready[k], 1)

            def rsqrt_of(st, k, lag):
                if st.runs(lag):
                    rsqrt(st.done(lag), k)

            def probs(st, pair, lag, before=0):
                if not st.runs(lag):
                    return
                two = slice(2 * pair, 2 * pair + 2)
                st.wait(pool, inv_ready, lag, per=2, short=1 - pair)
                pool.tensor_tensor(prob[:, two, :].rearrange("p j (h g) -> p (j h) g", g=HEADS),
                                   prob_e[:, two, :].rearrange("p j (h g) -> p (j h) g", g=HEADS),
                                   inv_total[:, two, :].rearrange("p j h -> p (j h)").unsqueeze(2)
                                   .broadcast_to([P, 2 * HEADS, HEADS]), ALU.mult).then_inc(prob_ready, 1)

            def weigh(st, j, lag):
                if not st.runs(lag):
                    return
                st.wait(pool, prob_ready, lag, per=2, short=1 - j // 2)
                st.wait(pool, o_psum, lag, per=TILES, short=TILES - 1 - j if lag < LAG_OUT else 0, before=1)
                p_view = prob[:, j, :].rearrange("p (h g) -> p g h", g=HEADS)
                v_view = v_tok[:, j, :].rearrange("p (g d) -> p g d", g=HEADS)
                quarter = HEADS // 4
                for part in range(4):
                    g = slice(part * quarter, (part + 1) * quarter)
                    last = pool.tensor_tensor(
                        pv[j][:, part * quarter * P:(part + 1) * quarter * P]
                        .rearrange("p (g h d) -> p g h d", g=quarter, h=HEADS),
                        p_view[:, g, :].unsqueeze(3).broadcast_to([P, quarter, HEADS, HD]),
                        v_view[:, g, :].unsqueeze(2).broadcast_to([P, quarter, HEADS, HD]), ALU.mult)
                last.then_inc(pv_ready, 1)

            def body(st):
                probs(st, 1, LAG_OUT)
                weigh(st, 2, LAG_OUT)
                weigh(st, 3, LAG_OUT)
                rsqrt_of(st, 1, LAG_MLP)
                rsqrt_of(st, 4, LAG_TANH)
                probs(st, 0, LAG_HEADS)
                rsqrt_of(st, 2, LAG_MLP)
                rsqrt_of(st, 5, LAG_OUT)
                rsqrt_of(st, 3, LAG_MLP)
                weigh(st, 0, LAG_HEADS)
                weigh(st, 1, LAG_HEADS)

            run_steps(pool, chunks, body)
            with pool.Fori(0, chunks // 2) as pair:
                for u in range(2):
                    rsqrt(2 * pair + u + 1, 6)


def kernel(**inputs):
    import numpy as np
    import concourse.bacc as bacc
    from concourse.bass_utils import run_bass_kernel_spmd

    nc = bacc.Bacc("TRN2", target_bir_lowering=False, num_devices=1)
    arrays, aps = {}, {}
    for name, value in inputs.items():
        a = np.ascontiguousarray(value)
        arrays[f"in_{name}"] = a
        aps[name] = nc.dram_tensor(f"in_{name}", a.shape, mybir.dt.from_np(a.dtype), kind="ExternalInput").ap()
    shape = arrays["in_L0_attn_x"].shape
    out = nc.dram_tensor("out_0", shape, F32, kind="ExternalOutput").ap()
    scratch = nc.dram_tensor("x4_scratch", (shape[0] * shape[1] // TILES, CHUNK), F32, kind="Internal").ap()
    build(nc, aps, out, scratch)
    r = run_bass_kernel_spmd(nc, [arrays], core_ids=[0])
    return r.results[0]["out_0"]
```

```python
from contextlib import ExitStack

import concourse.bass as bass
from concourse import mybir

F32 = mybir.dt.float32
BF16 = mybir.dt.bfloat16
ALU = mybir.AluOpType
ACT = mybir.ActivationFunctionType
AX = mybir.AxisListType

P = 128
HEADS = 16
HD = P // HEADS
TILES = 4
CHUNK = TILES * P
EPS_LN = 1e-5
EPS_ATTN = 1e-6
FF = 4
EXPERTS = 8
LATENT = 32

ROW = {"bq": 0, "bk": 1, "bv": 2, "bo": 3, "b2": 4, "bout": 5, "bqkv": 6}
N_ROWS = 9

LAG_IN, LAG_MLP, LAG_TANH, LAG_HEADS, LAG_OUT = 0, 2, 3, 4, 5
LAG_Y, LAG_GATE, LAG_EXPERTS, LAG_RESULT = range(4)
PEELED2 = 4
AHEAD = 8
PEELED = LAG_OUT + 1


class Step:

    def __init__(self, s, chunks, inside=None, pair=None):
        self.s, self.chunks, self.inside, self.pair = s, chunks, inside, pair
        self.par = (s if inside is None else inside) % 2

    def runs(self, lag):
        return self.inside is not None or 0 <= self.s - lag < self.chunks

    def chunk(self, lag):
        return self.s - lag

    def buf(self, lag):
        return (self.par - lag) % 2

    def done(self, lag, before=0):
        n = self.s - (lag + before - 1)
        return n if self.inside is not None else max(0, min(self.chunks, n))

    def ran(self, lag, before=0):
        return self.inside is not None or 0 <= self.s - lag - before < self.chunks

    def after(self, eng, *uses):
        for sem, lag, *more in uses:
            before, per, short = (*more, *(0, 1, 0)[len(more):])
            if self.ran(lag, before):
                return self.wait(eng, sem, lag, per, short, before)

    def batch(self, lag):
        return (self.s - lag) // 2 if self.inside is None else self.pair + (self.inside - lag) // 2

    def wait(self, eng, sem, lag, per=1, short=0, before=0):
        n = self.done(lag, before)
        if self.inside is not None:
            eng.wait_ge(sem, n * per - short if short else n * per)
        elif n * per - short > 0:
            eng.wait_ge(sem, n * per - short)


def run_steps(eng, chunks, body, first=0, peeled=PEELED, last_lag=LAG_OUT):
    for s in range(first, peeled):
        body(Step(s, chunks))
    with eng.Fori(peeled // 2, chunks // 2) as pair:
        for u in range(2):
            body(Step(2 * pair + u, chunks, inside=u, pair=pair))
    for s in range(chunks, chunks + last_lag):
        body(Step(s, chunks))


def build(nc, t, out, scratch, choice):
    n_tokens = t["L0_attn_x"].shape[0] * t["L0_attn_x"].shape[1]
    chunks = n_tokens // CHUNK
    per_batch = t["L0_attn_x"].shape[1] // CHUNK
    assert per_batch == 2 and chunks % 2 == 0 and chunks > PEELED

    x_d = t["L0_attn_x"].rearrange("n (c p j) d -> (n c) p (j d)", c=per_batch, j=TILES)
    out_d = out.rearrange("n (c p j) d -> (n c) p (j d)", c=per_batch, j=TILES)
    choice_d = choice.rearrange("(c e) n -> c e n", e=EXPERTS)
    scratch_d = scratch.rearrange("(c p) w -> c p w", p=P)

    with ExitStack() as ctx:
        def sb(name, shape, dt=F32):
            return ctx.enter_context(nc.sbuf_tensor(name, shape, dt))

        def sem(name):
            return ctx.enter_context(nc.semaphore(name))

        bank = [ctx.enter_context(nc.psum_tensor(f"bank{i}", [P, CHUNK], F32)) for i in range(8)]
        kv_acc, o_acc = bank[6], bank[7]

        ident = sb("ident", [P, P])
        ident_bf = sb("ident_bf", [P, P], BF16)
        ones_bf = sb("ones_bf", [P, CHUNK], BF16)
        head_of = sb("head_of", [P, HEADS])
        head_mask = sb("head_mask", [P, P])
        minus_half = sb("minus_half", [P, TILES])
        prefer = sb("prefer", [P, EXPERTS])

        wq, wk, wv, wo = (sb(n, [P, P]) for n in ("wq", "wk", "wv", "wo"))
        w1 = sb("w1", [P, FF * P])
        w2 = sb("w2", [P, FF, P])
        wt = [sb(f"wt{i}", [P, P]) for i in range(3)]
        wtT = sb("wtT", [P, P])
        wt01T = sb("wt01T", [P, P])
        w_tanh = sb("w_tanh", [P, P])
        w_qkv = sb("w_qkv", [P, 3 * P])
        wdown = sb("wdown", [P, LATENT])
        wdownT = sb("wdownT", [LATENT, P])
        wup = sb("wup", [LATENT, 2 * P])
        bdown = sb("bdown", [LATENT, 1])
        wout = sb("wout", [P, P])
        wg = sb("wg", [P, EXPERTS])
        e1 = sb("e1", [P, EXPERTS, P])
        e2 = sb("e2", [P, EXPERTS, P])
        eb = sb("eb", [EXPERTS, 2 * P])
        eb_left = sb("eb_left", [EXPERTS, 2 * P])
        eb_parts = sb("eb_parts", [EXPERTS, 3, 2 * P], BF16)
        eb3 = sb("eb3", [3 * EXPERTS, 2 * P], BF16)
        cols = sb("cols", [P, FF + 5])
        col_rows = sb("col_rows", [FF + 5, P])
        rows = sb("rows", [1, N_ROWS * P + EXPERTS])
        rows_left = sb("rows_left", [1, N_ROWS * P + EXPERTS])
        parts = sb("parts", [1, 3, N_ROWS * P + EXPERTS], BF16)
        bias3 = sb("bias3", [P, N_ROWS * P + EXPERTS], BF16)

        def row3(name, n=1):
            return bias3[:, ROW[name] * P:(ROW[name] + n) * P]

        def row3_by_tile(name):
            return row3(name).unsqueeze(1).broadcast_to([P, TILES, P])

        x_tok = [sb(f"x_tok{i}", [P, CHUNK]) for i in range(2)]
        xT = [sb(f"xT{i}", [P, CHUNK]) for i in range(2)]
        qT = [sb(f"qT{i}", [P, CHUNK]) for i in range(2)]
        neg_q, neg_k = sb("neg_q", [P, CHUNK]), sb("neg_k", [P, CHUNK])
        exp_q, exp_k = sb("exp_q", [P, CHUNK]), sb("exp_k", [P, CHUNK])
        k_tok = sb("k_tok", [P, CHUNK])
        v_one = sb("v_one", [P, TILES, P + 1])
        kv = sb("kv", [P, P + HEADS])
        k_sum = sb("k_sum", [P, 1])
        den = sb("den", [P, TILES * HEADS])
        z = sb("z", [P, TILES * HEADS])
        attn_tok = sb("attn_tok", [P, CHUNK])
        attnT = sb("attnT", [P, CHUNK])
        n1 = sb("n1", [P, CHUNK])
        x1T = sb("x1T", [P, CHUNK])
        hT = sb("hT", [P, FF, CHUNK])
        n2 = sb("n2", [P, CHUNK])
        uT = sb("uT", [P, CHUNK])
        x2 = sb("x2", [P, CHUNK])
        x2T = sb("x2T", [P, CHUNK])
        tT = sb("tT", [P, CHUNK])
        x3 = sb("x3", [P, CHUNK])
        x3T = [sb(f"x3T{i}", [P, CHUNK]) for i in range(2)]
        q_tok = sb("q_tok", [P, TILES, P])
        v_tok = sb("v_tok", [P, TILES, P])
        qk = [sb(f"qk{i}", [P, HEADS * P]) for i in range(2)]
        score = sb("score", [P, TILES, HEADS * HEADS])
        top = sb("top", [P, TILES, HEADS])
        prob_e = sb("prob_e", [P, TILES, HEADS * HEADS])
        total = sb("total", [P, TILES, HEADS])
        inv_total = sb("inv_total", [P, TILES, HEADS])
        prob = sb("prob", [P, TILES, HEADS * HEADS])
        pv = [sb(f"pv{i}", [P, HEADS * P]) for i in range(TILES)]
        oT = sb("oT", [P, CHUNK])
        x_kept = [sb(f"x_kept{i}", [P, CHUNK]) for i in range(2)]
        x4 = [sb(f"x4{i}", [P, CHUNK]) for i in range(2)]

        norms = range(1, 7)
        stats = {k: sb(f"stats{k}", [P, TILES, 6]) for k in norms}
        mean_var = {k: sb(f"mean_var{k}", [P, TILES, 2]) for k in norms}
        minus_mean = {k: sb(f"minus_mean{k}", [P, TILES]) for k in norms}
        var_eps = {k: sb(f"var_eps{k}", [P, TILES]) for k in norms}
        rstd = {k: sb(f"rstd{k}", [P, TILES]) for k in norms}
        shift = {k: sb(f"shift{k}", [P, TILES]) for k in norms}
        stats_done = {k: sem(f"stats_done{k}") for k in norms}
        mean_done = {k: sem(f"mean_done{k}") for k in norms}
        moments_ready = {k: sem(f"moments_ready{k}") for k in norms}
        rstd_ready = {k: sem(f"rstd_ready{k}") for k in norms}
        shift_ready = {k: sem(f"shift_ready{k}") for k in norms}
        normed = {k: sem(f"normed{k}") for k in norms}

        y_tok = [sb(f"y_tok{i}", [P, CHUNK]) for i in range(2)]
        yT = [sb(f"yT{i}", [P, CHUNK]) for i in range(2)]
        gate = sb("gate", [P, TILES, EXPERTS])
        gate_top = sb("gate_top", [P, TILES])
        gate_is = sb("gate_is", [P, TILES, EXPERTS])
        gate_pref = sb("gate_pref", [P, TILES, EXPERTS])
        gate_first = sb("gate_first", [P, TILES])
        chosen = sb("chosen", [P, TILES, 3 * EXPERTS], BF16)
        chosenT = [sb(f"chosenT{i}", [3 * EXPERTS, CHUNK], BF16) for i in range(2)]
        chosenT_bank = bank[2][0:3 * EXPERTS, 0:CHUNK // 2].bitcast(BF16)
        mask = [pv[i][:].bitcast(BF16) for i in range(2)]
        masked = [qk[i // 4][:, (i % 4) * CHUNK:(i % 4 + 1) * CHUNK] for i in range(AHEAD)]
        gT, moeT, *result = (hT[:, i, :] for i in range(FF))
        y_kept = [pv[2][:, i * CHUNK:(i + 1) * CHUNK] for i in range(2)]

        weights_in = sem("weights_in")
        x_in = [sem(f"x_in{i}") for i in range(2)]
        consts = sem("consts")
        pool_prep = sem("pool_prep")
        dve_prep = sem("dve_prep")
        prep_mm = sem("prep_mm")
        prep_out = sem("prep_out")
        kv_bias_ready = sem("kv_bias_ready")
        rows_split = sem("rows_split")
        bias3_in = sem("bias3_in")
        eb_split = sem("eb_split")
        xT_psum, xT_ready = sem("xT_psum"), sem("xT_ready")
        q_psum, q_neg, q_exp, q_ready = sem("q_psum"), sem("q_neg"), sem("q_exp"), sem("q_ready")
        k_psum, k_neg, k_exp, k_ready = sem("k_psum"), sem("k_neg"), sem("k_exp"), sem("k_ready")
        v_psum, v_ready = sem("v_psum"), sem("v_ready")
        kv_psum, kv_sum, kv_ready = sem("kv_psum"), sem("kv_sum"), sem("kv_ready")
        den_psum, den_ready, z_ready = sem("den_psum"), sem("den_ready"), sem("z_ready")
        num_psum, attn_ready = sem("num_psum"), sem("attn_ready")
        attnT_psum, attnT_ready = sem("attnT_psum"), sem("attnT_ready")
        s_psum = {k: sem(f"s_psum{k}") for k in norms}
        n1T_psum, x1T_ready = sem("n1T_psum"), sem("x1T_ready")
        h_psum, h_act = sem("h_psum"), sem("h_act")
        n2T_psum, uT_ready = sem("n2T_psum"), sem("uT_ready")
        x2T_psum, x2T_ready = sem("x2T_psum"), sem("x2T_ready")
        t_psum, tT_ready = sem("t_psum"), sem("tT_ready")
        x3T_psum, x3T_ready = sem("x3T_psum"), sem("x3T_ready")
        qkv_psum, qv_ready = sem("qkv_psum"), sem("qv_ready")
        qk_ready, score_ready = sem("qk_ready"), sem("score_ready")
        top_ready, below_top, exp_ready = sem("top_ready"), sem("below_top"), sem("exp_ready")
        total_ready, inv_ready, prob_ready = sem("total_ready"), sem("inv_ready"), sem("prob_ready")
        pv_ready, o_psum, oT_ready = sem("pv_ready"), sem("o_psum"), sem("oT_ready")
        x_copied = [sem(f"x_copied{i}") for i in range(2)]
        x4_out = [sem(f"x4_out{i}") for i in range(2)]
        y_copied = [sem(f"y_copied{i}") for i in range(2)]
        y_in = [sem(f"y_in{i}") for i in range(2)]
        yT_psum, yT_ready = sem("yT_psum"), sem("yT_ready")
        gate_psum, gate_step = sem("gate_psum"), sem("gate_step")
        gate_read = sem("gate_read")
        chosen_ready, chosenT_psum, chosenT_ready = sem("chosen_ready"), sem("chosenT_psum"), sem("chosenT_ready")
        choice_out = [sem(f"choice_out{i}") for i in range(2)]
        mask_in = [sem(f"mask_in{i}") for i in range(2)]
        masked_ready, used = sem("masked_ready"), sem("used")
        gT_ready, moeT_ready = sem("gT_ready"), sem("moeT_ready")
        result_out = [sem(f"result_out{i}") for i in range(2)]

        loads = [
            (wq, t["L0_attn_Wq"]), (wk, t["L0_attn_Wk"]), (wv, t["L0_attn_Wv"]), (wo, t["L0_attn_Wo"]),
            (w1, t["L0_attn_W1"]), (w2, t["L0_attn_W2"].rearrange("(f p) n -> p f n", p=P)),
            (wt[0], t["L0_ffn_weight"]), (wt[1], t["L0_ffn_aux_weight1"]), (wt[2], t["L0_ffn_aux_weight2"]),
            (w_qkv[:, 0:P], t["L1_attn_Wq"]), (wdown, t["L1_attn_Wdown"]), (wup, t["L1_attn_Wup"]),
            (bdown, t["L1_attn_bdown"].rearrange("(p a) -> p a", a=1)),
            (wout, t["L1_attn_Wout"]), (wg, t["L1_ffn_Wg"]),
            (e1, t["L1_ffn_W1"].rearrange("e p i -> p e i")),
            (e2, t["L1_ffn_W2"].rearrange("e p i -> p e i")),
            (eb[:, 0:P], t["L1_ffn_b1"]), (eb[:, P:], t["L1_ffn_b2"]),
            (col_rows[0:FF, :], t["L0_attn_b1"].rearrange("(f p) -> f p", p=P)),
        ]
        for i, name in enumerate(("L0_ffn_bias", "L0_attn_g1", "L0_attn_beta1", "L0_attn_g2", "L0_attn_beta2")):
            loads.append((col_rows[FF + i:FF + i + 1, :], t[name].rearrange("(a p) -> a p", a=1)))
        for key, name in (("bq", "L0_attn_bq"), ("bk", "L0_attn_bk"), ("bv", "L0_attn_bv"), ("bo", "L0_attn_bo"),
                          ("b2", "L0_attn_b2"), ("bout", "L1_attn_bout"), ("bqkv", "L1_attn_bq")):
            loads.append((rows[:, ROW[key] * P:(ROW[key] + 1) * P], t[name].rearrange("(a n) -> a n", a=1)))
        loads.append((rows[:, (ROW["bqkv"] + 1) * P:(ROW["bqkv"] + 3) * P], t["L1_attn_bup"].rearrange("(a n) -> a n", a=1)))
        loads.append((rows[:, N_ROWS * P:], t["L1_ffn_bg"].rearrange("(a n) -> a n", a=1)))
        all_loads = 16 * len(loads)
        b1_col, tanh_col, g1_col, beta1_col, g2_col, beta2_col = (
            0, *(FF + i for i in range(5)))

        def col(i):
            return cols[:, i:i + 1]

        def tile(a, j):
            return a[:, j * P:(j + 1) * P]

        block = ctx.enter_context(nc.Block())

        @block.sync
        def _(sp):
            def load_x(st):
                if not st.runs(LAG_IN):
                    return
                st.wait(sp, xT_psum, LAG_IN, before=2)
                sp.dma_start(x_tok[st.buf(LAG_IN)][:], x_d[st.chunk(LAG_IN)]).then_inc(x_in[st.buf(LAG_IN)], 16)

            def store_x4(st):
                if not st.runs(LAG_OUT):
                    return
                st.wait(sp, normed[5], LAG_OUT)
                sp.dma_start(scratch_d[st.chunk(LAG_OUT)], x4[st.buf(LAG_OUT)][:]).then_inc(x4_out[st.buf(LAG_OUT)], 16)

            def keep_x(st):
                if not st.runs(LAG_MLP):
                    return
                b = st.buf(LAG_MLP)
                sp.wait_ge(rows_split, 5)
                st.wait(sp, xT_ready, LAG_MLP)
                st.wait(sp, s_psum[3], LAG_TANH, before=1)
                sp.dma_start(x_kept[b][:], xT[b][:]).then_inc(x_copied[b], 16)

            def body(st):
                load_x(st)
                keep_x(st)
                store_x4(st)

            sp.dma_start(x_tok[0][:], x_d[0]).then_inc(x_in[0], 16)
            for dst, src in loads:
                sp.dma_start(dst[:], src).then_inc(weights_in, 16)
            sp.wait_ge(rows_split, 5)
            sp.dma_start(bias3[0:3, :], parts[0:1, :, :]).then_inc(bias3_in, 16)
            sp.wait_ge(eb_split, 5)
            for r in range(3):
                sp.dma_start(eb3[r * EXPERTS:(r + 1) * EXPERTS, :], eb_parts[:, r, :]).then_inc(bias3_in, 16)
            run_steps(sp, chunks, body, first=1)

            for i in range(2):
                sp.wait_ge(x4_out[i], 16 * (chunks // 2))

            def load_y(st):
                if not st.runs(LAG_Y):
                    return
                if st.ran(LAG_Y, 2):
                    st.wait(sp, yT_psum, LAG_Y, before=2)
                sp.dma_start(y_tok[st.buf(LAG_Y)][:], scratch_d[st.chunk(LAG_Y)]
                             ).then_inc(y_in[st.buf(LAG_Y)], 16)

            def keep_y(st):
                if not st.runs(LAG_EXPERTS):
                    return
                b = st.buf(LAG_EXPERTS)
                sp.wait_ge(rows_split, 5)
                st.wait(sp, yT_ready, LAG_EXPERTS)
                if st.ran(LAG_RESULT, 1):
                    st.wait(sp, s_psum[6], LAG_RESULT, before=1)
                sp.dma_start(y_kept[b], yT[b][:]).then_inc(y_copied[b], 16)

            def spread_choice(st):
                if not st.runs(LAG_GATE):
                    return
                b = st.buf(LAG_GATE)
                st.wait(sp, chosenT_ready, LAG_GATE)
                sp.dma_start(choice_d[st.chunk(LAG_GATE)], chosenT[b][0:EXPERTS, :]).then_inc(choice_out[b], 16)
                sp.wait_ge(choice_out[b], 16 * (st.batch(LAG_GATE) + 1))
                sp.dma_start(mask[b], choice_d[st.chunk(LAG_GATE)].rearrange("(a e) n -> a (e n)", a=1)
                             .broadcast_to([P, EXPERTS * CHUNK])).then_inc(mask_in[b], 16)

            def store(st):
                if not st.runs(LAG_RESULT):
                    return
                st.wait(sp, normed[6], LAG_RESULT)
                sp.dma_start(out_d[st.chunk(LAG_RESULT)], result[st.buf(LAG_RESULT)]
                             ).then_inc(result_out[st.buf(LAG_RESULT)], 16)

            def body2(st):
                load_y(st)
                keep_y(st)
                spread_choice(st)
                store(st)

            run_steps(sp, chunks, body2, 0, PEELED2, LAG_RESULT)
            for u in range(2):
                sp.wait_ge(result_out[u], 16 * (chunks // 2))

        @block.tensor
        def _(pe):
            def mm(out_, lhsT, rhs, start=False, stop=False):
                return pe.matmul(out_, lhsT, rhs, start=start, stop=stop, skip_group_check=True)

            def turn(out_, in_, start=True, stop=True):
                return pe.matmul(out_, in_, ident[:], is_transpose=True, start=start, stop=stop,
                                 skip_group_check=True)

            def turn4(out_, in_, start=True, stop=True):
                for j in range(TILES):
                    last = turn(tile(out_, j), tile(in_, j), start=start and j == 0, stop=stop)
                return last

            pe.wait_ge(consts, 1)
            pe.wait_ge(weights_in, all_loads)
            turn(bank[0][:, 0:P], wt[0][:]).then_inc(prep_mm, 1)
            pe.matmul(bank[1][0:LATENT, 0:P], wdown[:], ident[:], is_transpose=True,
                      start=True, stop=True).then_inc(prep_mm, 1)
            pe.matmul(bank[3][:, 0:FF + 5], col_rows[:], ident[0:FF + 5, 0:FF + 5], is_transpose=True,
                      start=True, stop=True).then_inc(prep_mm, 1)
            pe.wait_ge(prep_out, 1)
            mm(bank[0][:, 0:P], wt[1][:], wtT[:], True, True).then_inc(prep_mm, 1)
            pe.wait_ge(prep_out, 2)
            mm(bank[1][:, 0:2 * P], wdownT[:], wup[:], True, True).then_inc(prep_mm, 1)
            mm(bank[2][0:1, 0:2 * P], bdown[:], wup[:], True, True).then_inc(prep_mm, 1)
            pe.wait_ge(prep_out, 4)
            mm(bank[0][:, 0:P], wt01T[:], wt[2][:], True, True).then_inc(prep_mm, 1)
            pe.wait_ge(kv_bias_ready, 1)
            pe.wait_ge(prep_out, 6)
            pe.wait_ge(bias3_in, 64)
            pe.wait_ge(dve_prep, 6 + EXPERTS)

            def xT_mm(st):
                if not st.runs(LAG_IN):
                    return
                b = st.buf(LAG_IN)
                pe.wait_ge(x_in[b], 16 * (st.batch(LAG_IN) + 1))
                st.after(pe, (h_act, LAG_MLP, 0, FF), (xT_ready, LAG_IN, 1))
                turn4(bank[0], x_tok[b]).then_inc(xT_psum, 1)

            def q_in(st):
                if not st.runs(LAG_IN):
                    return
                st.wait(pe, xT_ready, LAG_IN)
                st.after(pe, (normed[2], LAG_MLP), (q_ready, LAG_IN, 1))
                mm(bank[3][:], row3("bq"), ones_bf[:], start=True)
                mm(bank[3][:], wq[:], xT[st.buf(LAG_IN)][:], stop=True).then_inc(q_psum, 1)

            def k_in(st):
                if not st.runs(LAG_IN):
                    return
                st.wait(pe, xT_ready, LAG_IN)
                st.after(pe, (qk_ready, LAG_HEADS, 0, TILES), (uT_ready, LAG_TANH), (k_ready, LAG_IN, 1))
                mm(bank[4][:], ones_bf[:, 0:P], row3_by_tile("bk"), start=True)
                for j in range(TILES):
                    last = mm(tile(bank[4], j), tile(xT[st.buf(LAG_IN)], j), wk[:], stop=True)
                last.then_inc(k_psum, 1)

            def v_in(st):
                if not st.runs(LAG_IN):
                    return
                st.wait(pe, xT_ready, LAG_IN)
                st.after(pe, (qk_ready, LAG_HEADS, 0, TILES, 1), (v_ready, LAG_IN, 1))
                mm(bank[1][:], ones_bf[:, 0:P], row3_by_tile("bv"), start=True)
                for j in range(TILES):
                    last = mm(tile(bank[1], j), tile(xT[st.buf(LAG_IN)], j), wv[:], stop=True)
                last.then_inc(v_psum, 1)

            def kv_sums(st):
                if not st.runs(LAG_IN):
                    return
                st.wait(pe, k_ready, LAG_IN)
                st.wait(pe, v_ready, LAG_IN)
                first = st.buf(LAG_IN) == 0
                if first and (st.inside is not None or st.s >= 2):
                    pe.wait_ge(kv_ready, st.batch(LAG_IN))
                for j in range(TILES):
                    last = mm(kv_acc[:, 0:P + 1], tile(k_tok, j), v_one[:, j, :], start=first and j == 0,
                              stop=not first and j == TILES - 1)
                last.then_inc(kv_psum, 1)

            def linear_attn(st):
                if not st.runs(LAG_MLP):
                    return
                q = qT[st.buf(LAG_MLP)]
                pe.wait_ge(kv_ready, st.batch(LAG_MLP) + 1)
                if not st.ran(LAG_IN, 1):
                    st.wait(pe, q_ready, LAG_MLP)
                st.after(pe, (q_ready, LAG_IN, 1), (normed[2], LAG_MLP, 1))
                for j in range(TILES):
                    last = mm(bank[3][:, j * HEADS:(j + 1) * HEADS], tile(q, j), kv[:, P:], start=j == 0, stop=True)
                last.then_inc(den_psum, 1)
                st.after(pe, (xT_ready, LAG_IN, 1), (h_act, LAG_MLP, 1, FF))
                for j in range(TILES):
                    last = mm(tile(bank[0], j), tile(q, j), kv[:, 0:P], start=j == 0, stop=True)
                last.then_inc(num_psum, 1)

            def attnT_mm(st):
                if not st.runs(LAG_MLP):
                    return
                st.wait(pe, attn_ready, LAG_MLP)
                turn4(bank[0], attn_tok).then_inc(attnT_psum, 1)

            def s1_mm(st):
                if not st.runs(LAG_MLP):
                    return
                st.wait(pe, attnT_ready, LAG_MLP)
                st.wait(pe, den_ready, LAG_MLP)
                mm(bank[3][:], ones_bf[:, 0:P], row3_by_tile("bo"), start=True)
                turn4(bank[3], xT[st.buf(LAG_MLP)], start=False)
                for j in range(TILES):
                    last = mm(tile(bank[3], j), tile(attnT, j), wo[:], stop=True)
                last.then_inc(s_psum[1], 1)

            def x1T_mm(st):
                if not st.runs(LAG_MLP):
                    return
                st.wait(pe, normed[1], LAG_MLP)
                turn4(bank[0], n1).then_inc(n1T_psum, 1)

            def mlp_in(st, f):
                if not st.runs(LAG_MLP):
                    return
                if f == 0:
                    st.wait(pe, x1T_ready, LAG_MLP)
                    st.after(pe, (tT_ready, LAG_TANH), (h_act, LAG_MLP, 1, FF))
                elif f >= 2:
                    st.wait(pe, h_act, LAG_MLP, per=FF, short=FF + 1 - f)
                mm(bank[2 if f % 2 == 0 else 0][:], w1[:, f * P:(f + 1) * P], x1T[:], True, True).then_inc(h_psum, 1)

            def mlp_out(st, f):
                if not st.runs(LAG_MLP):
                    return
                if f == 0:
                    mm(bank[3][:], ones_bf[:, 0:P], row3_by_tile("b2"), start=True)
                    turn4(bank[3], x1T, start=False)
                st.wait(pe, h_act, LAG_MLP, per=FF, short=FF - 1 - f)
                for j in range(TILES):
                    last = mm(tile(bank[3], j), tile(hT[:, f, :], j), w2[:, f, :], stop=f == FF - 1)
                if f == FF - 1:
                    last.then_inc(s_psum[2], 1)

            def n2T_mm(st):
                if not st.runs(LAG_TANH):
                    return
                st.wait(pe, normed[2], LAG_TANH)
                st.after(pe, (k_ready, LAG_IN, 1), (qk_ready, LAG_HEADS, 1, TILES))
                turn4(bank[4], n2).then_inc(n2T_psum, 1)

            def s3_mm(st):
                if not st.runs(LAG_TANH):
                    return
                b = st.buf(LAG_TANH)
                pe.wait_ge(x_copied[b], 16 * (st.batch(LAG_TANH) + 1))
                st.wait(pe, x3T_ready, LAG_TANH, before=1)
                turn4(bank[5], x_kept[b], stop=False)
                st.wait(pe, uT_ready, LAG_TANH)
                turn4(bank[5], uT, start=False).then_inc(s_psum[3], 1)

            def x2T_mm(st):
                if not st.runs(LAG_TANH):
                    return
                st.wait(pe, normed[3], LAG_TANH)
                turn4(bank[5], x2).then_inc(x2T_psum, 1)

            def tanh_mm(st):
                if not st.runs(LAG_TANH):
                    return
                st.wait(pe, x2T_ready, LAG_TANH)
                st.after(pe, (normed[5], LAG_OUT, 1), (h_act, LAG_MLP, 1, FF))
                mm(bank[2][:], w_tanh[:], x2T[:], True, True).then_inc(t_psum, 1)

            def s4_mm(st):
                if not st.runs(LAG_TANH):
                    return
                st.wait(pe, tT_ready, LAG_TANH)
                turn4(bank[5], x2T, stop=False)
                turn4(bank[5], tT, start=False).then_inc(s_psum[4], 1)

            def x3T_mm(st):
                if not st.runs(LAG_TANH):
                    return
                st.wait(pe, normed[4], LAG_TANH)
                turn4(bank[5], x3).then_inc(x3T_psum, 1)

            def heads_qkv(st, j):
                if not st.runs(LAG_HEADS):
                    return
                st.wait(pe, x3T_ready, LAG_HEADS)
                if j == 0:
                    st.after(pe, (v_ready, LAG_IN, 1), (qk_ready, LAG_HEADS, 1, TILES))
                elif j == 1:
                    st.after(pe, (uT_ready, LAG_TANH), (qk_ready, LAG_HEADS, 1, TILES))
                else:
                    st.wait(pe, qk_ready, LAG_HEADS, per=TILES, short=TILES + 1 - j)
                b = bank[1 if j % 2 == 0 else 4][:, 0:3 * P]
                mm(b, ones_bf[:, 0:P], row3("bqkv", 3), start=True)
                mm(b, tile(x3T[st.buf(LAG_HEADS)], j), w_qkv[:], stop=True).then_inc(qkv_psum, 1)

            def o_sums(st, tiles):
                if not st.runs(LAG_OUT):
                    return
                for j in tiles:
                    st.wait(pe, pv_ready, LAG_OUT, per=TILES, short=TILES - 1 - j)
                    if j == 0:
                        st.wait(pe, oT_ready, LAG_OUT, before=1)
                    for g in range(HEADS):
                        last = turn(tile(o_acc, j), tile(pv[j], g), start=g == 0, stop=g == HEADS - 1)
                    last.then_inc(o_psum, 1)

            def s5_mm(st):
                if not st.runs(LAG_OUT):
                    return
                st.wait(pe, oT_ready, LAG_OUT)
                st.after(pe, (h_act, LAG_MLP, 0, FF, 1), (tT_ready, LAG_TANH), (normed[5], LAG_OUT, 1))
                mm(bank[2][:], ones_bf[:, 0:P], row3_by_tile("bout"), start=True)
                turn4(bank[2], x3T[st.buf(LAG_OUT)], start=False)
                for j in range(TILES):
                    last = mm(tile(bank[2], j), tile(oT, j), wout[:], stop=True)
                last.then_inc(s_psum[5], 1)

            def body(st):
                heads_qkv(st, 0)
                linear_attn(st)
                n2T_mm(st)
                attnT_mm(st)
                o_sums(st, (0,))
                s3_mm(st)
                s1_mm(st)
                o_sums(st, (1,))
                heads_qkv(st, 1)
                o_sums(st, (2,))
                x2T_mm(st)
                x1T_mm(st)
                tanh_mm(st)
                o_sums(st, (3,))
                s4_mm(st)
                mlp_in(st, 0)
                mlp_in(st, 1)
                heads_qkv(st, 2)
                mlp_out(st, 0)
                mlp_in(st, 2)
                mlp_in(st, 3)
                mlp_out(st, 1)
                s5_mm(st)
                mlp_out(st, 2)
                mlp_out(st, 3)
                xT_mm(st)
                heads_qkv(st, 3)
                x3T_mm(st)
                q_in(st)
                k_in(st)
                v_in(st)
                kv_sums(st)

            run_steps(pe, chunks, body)

            def yT_mm(st):
                if not st.runs(LAG_Y):
                    return
                pe.wait_ge(y_in[st.buf(LAG_Y)], 16 * (st.batch(LAG_Y) + 1))
                if st.ran(LAG_Y, 1):
                    st.wait(pe, yT_ready, LAG_Y, before=1)
                turn4(bank[0], y_tok[st.buf(LAG_Y)]).then_inc(yT_psum, 1)

            def gate_mm(st):
                if not st.runs(LAG_GATE):
                    return
                st.wait(pe, yT_ready, LAG_GATE)
                if st.ran(LAG_GATE, 1):
                    st.wait(pe, gate_read, LAG_GATE, before=1)
                mm(bank[1][:, 0:TILES * EXPERTS], ones_bf[:, 0:P],
                   bias3[:, N_ROWS * P:].unsqueeze(1).broadcast_to([P, TILES, EXPERTS]), start=True)
                for j in range(TILES):
                    last = mm(bank[1][:, j * EXPERTS:(j + 1) * EXPERTS], tile(yT[st.buf(LAG_GATE)], j), wg[:], stop=True)
                last.then_inc(gate_psum, 1)

            def chosenT_mm(st):
                if not st.runs(LAG_GATE):
                    return
                st.wait(pe, chosen_ready, LAG_GATE)
                if st.ran(LAG_GATE, 1):
                    st.wait(pe, chosenT_ready, LAG_GATE, before=1)
                for j in range(TILES):
                    last = pe.matmul(chosenT_bank[:, j * P:(j + 1) * P], chosen[:, j, :], ident_bf[:],
                                     is_transpose=True, start=True, stop=True, skip_group_check=True)
                last.then_inc(chosenT_psum, 1)

            def experts_mm(st, layer, experts):
                if not st.runs(LAG_EXPERTS):
                    return
                w, acc = (e1, bank[3]) if layer == 0 else (e2, bank[4])
                for e in experts:
                    if e == 0:
                        if st.ran(LAG_EXPERTS, 1):
                            st.wait(pe, (gT_ready, moeT_ready)[layer], LAG_EXPERTS, before=1)
                        if layer == 0:
                            st.wait(pe, chosenT_ready, LAG_EXPERTS)
                        mm(acc[:], eb3[:, layer * P:(layer + 1) * P], chosenT[st.buf(LAG_EXPERTS)][:], start=True)
                    st.wait(pe, masked_ready, LAG_EXPERTS, per=2 * EXPERTS,
                            short=2 * EXPERTS - 1 - (layer * EXPERTS + e))
                    mm(acc[:], w[:, e, :], masked[e % AHEAD], stop=e == EXPERTS - 1).then_inc(used, 1)

            def result_mm(st):
                if not st.runs(LAG_RESULT):
                    return
                if st.ran(LAG_RESULT, 1):
                    st.wait(pe, normed[6], LAG_RESULT, before=1)
                pe.wait_ge(y_copied[st.buf(LAG_RESULT)], 16 * (st.batch(LAG_RESULT) + 1))
                turn4(bank[5], y_kept[st.buf(LAG_RESULT)], stop=False)
                st.wait(pe, moeT_ready, LAG_RESULT)
                turn4(bank[5], moeT, start=False).then_inc(s_psum[6], 1)

            def body2(st):
                gate_mm(st)
                experts_mm(st, 0, range(0, 4))
                chosenT_mm(st)
                experts_mm(st, 0, range(4, 8))
                result_mm(st)
                yT_mm(st)
                experts_mm(st, 1, range(0, 8))

            run_steps(pe, chunks, body2, 0, PEELED2, LAG_RESULT)

        @block.scalar
        def _(act):
            def normalise(st, k, lag, src, dst):
                st.wait(act, shift_ready[k], lag)
                for j in range(TILES):
                    last = act.activation(tile(dst, j), tile(src, j), ACT.Identity,
                                          bias=shift[k][:, j:j + 1], scale=rstd[k][:, j:j + 1])
                last.then_inc(normed[k], 1)

            act.wait_ge(prep_mm, 1)
            act.activation(wtT[:], bank[0][:, 0:P], ACT.Copy).then_inc(prep_out, 1)
            act.wait_ge(prep_mm, 2)
            act.activation(wdownT[:], bank[1][0:LATENT, 0:P], ACT.Copy).then_inc(prep_out, 1)
            act.wait_ge(prep_mm, 3)
            act.activation(cols[:], bank[3][:, 0:FF + 5], ACT.Copy).then_inc(prep_out, 1)
            act.wait_ge(prep_mm, 4)
            act.activation(wt01T[:], bank[0][:, 0:P], ACT.Copy).then_inc(prep_out, 1)
            act.wait_ge(prep_mm, 5)
            act.activation(w_qkv[:, P:3 * P], bank[1][:, 0:2 * P], ACT.Copy).then_inc(prep_out, 1)
            act.wait_ge(prep_mm, 7)
            act.activation(w_tanh[:], bank[0][:, 0:P], ACT.Copy).then_inc(prep_out, 1)

            def xT_copy(st):
                if not st.runs(LAG_IN):
                    return
                st.wait(act, xT_psum, LAG_IN)
                if st.ran(LAG_IN, 2):
                    st.wait(act, s_psum[1], LAG_MLP)
                    act.wait_ge(x_copied[st.buf(LAG_IN)], 16 * st.batch(LAG_IN))
                act.activation(xT[st.buf(LAG_IN)][:], bank[0][:], ACT.Copy).then_inc(xT_ready, 1)

            def elu(st, psum, psum_bank, neg, neg_done, exp, exp_done, ready):
                st.wait(act, psum, LAG_IN)
                st.wait(act, exp_done, LAG_IN, before=1)
                act.activation(neg[:], psum_bank[:], ACT.Relu, scale=-1.0).then_inc(neg_done, 1)
                st.wait(act, neg_done, LAG_IN)
                st.wait(act, ready, LAG_IN, before=1)
                act.activation(exp[:], neg[:], ACT.Exp, scale=-1.0).then_inc(exp_done, 1)

            def q_k_v(st):
                if not st.runs(LAG_IN):
                    return
                elu(st, q_psum, bank[3], neg_q, q_neg, exp_q, q_exp, q_ready)
                elu(st, k_psum, bank[4], neg_k, k_neg, exp_k, k_exp, k_ready)
                st.wait(act, v_psum, LAG_IN)
                st.wait(act, kv_psum, LAG_IN, before=1)
                act.activation(v_one[:, :, 0:P], bank[1][:].rearrange("p (j d) -> p j d", j=TILES),
                               ACT.Copy).then_inc(v_ready, 1)

            def attnT_copy(st):
                if not st.runs(LAG_MLP):
                    return
                st.wait(act, attnT_psum, LAG_MLP)
                act.activation(attnT[:], bank[0][:], ACT.Copy).then_inc(attnT_ready, 1)

            def n1_act(st):
                if st.runs(LAG_MLP):
                    normalise(st, 1, LAG_MLP, bank[3], n1)

            def x1T_act(st):
                if not st.runs(LAG_MLP):
                    return
                st.wait(act, n1T_psum, LAG_MLP)
                act.activation(x1T[:], bank[0][:], ACT.Identity, bias=col(beta1_col),
                               scale=col(g1_col)).then_inc(x1T_ready, 1)

            def relu_act(st, f):
                if not st.runs(LAG_MLP):
                    return
                st.wait(act, h_psum, LAG_MLP, per=FF, short=FF - 1 - f)
                act.activation(hT[:, f, :], bank[2 if f % 2 == 0 else 0][:], ACT.Relu,
                               bias=col(b1_col + f)).then_inc(h_act, 1)

            def n2_act(st):
                if st.runs(LAG_MLP):
                    st.wait(act, n2T_psum, LAG_TANH)
                    normalise(st, 2, LAG_MLP, bank[3], n2)

            def uT_act(st):
                if not st.runs(LAG_TANH):
                    return
                st.wait(act, n2T_psum, LAG_TANH)
                act.activation(uT[:], bank[4][:], ACT.Identity, bias=col(beta2_col),
                               scale=col(g2_col)).then_inc(uT_ready, 1)

            def x2_act(st):
                if st.runs(LAG_TANH):
                    normalise(st, 3, LAG_TANH, bank[5], x2)

            def x2T_copy(st):
                if not st.runs(LAG_TANH):
                    return
                st.wait(act, x2T_psum, LAG_TANH)
                act.activation(x2T[:], bank[5][:], ACT.Copy).then_inc(x2T_ready, 1)

            def tanh_act(st):
                if not st.runs(LAG_TANH):
                    return
                st.wait(act, t_psum, LAG_TANH)
                act.activation(tT[:], bank[2][:], ACT.Tanh, bias=col(tanh_col)).then_inc(tT_ready, 1)

            def x3_act(st):
                if st.runs(LAG_TANH):
                    normalise(st, 4, LAG_TANH, bank[5], x3)

            def x3T_copy(st):
                if not st.runs(LAG_TANH):
                    return
                st.wait(act, x3T_psum, LAG_TANH)
                st.wait(act, s_psum[5], LAG_OUT)
                act.activation(x3T[st.buf(LAG_TANH)][:], bank[5][:], ACT.Copy).then_inc(x3T_ready, 1)

            def qv_copy(st, j):
                if not st.runs(LAG_HEADS):
                    return
                b = bank[1 if j % 2 == 0 else 4]
                st.wait(act, qkv_psum, LAG_HEADS, per=TILES, short=TILES - 1 - j)
                st.wait(act, qk_ready, LAG_HEADS, per=TILES, short=TILES - 1 - j, before=1)
                st.wait(act, pv_ready, LAG_OUT, per=TILES, short=TILES - 1 - j)
                act.activation(q_tok[:, j, :], b[:, 0:P], ACT.Copy)
                act.activation(v_tok[:, j, :].rearrange("p (g d) -> p g d", g=HEADS),
                               b[:, P:3 * P].rearrange("p (g w) -> p g w", g=HEADS)[:, :, HD:],
                               ACT.Copy).then_inc(qv_ready, 1)

            def prob_exp(st, pair):
                if not st.runs(LAG_HEADS):
                    return
                st.wait(act, below_top, LAG_HEADS, per=2, short=1 - pair)
                st.wait(act, prob_ready, LAG_HEADS, per=2, short=1 - pair, before=1)
                act.activation(prob_e[:, 2 * pair:2 * pair + 2, :], score[:, 2 * pair:2 * pair + 2, :], ACT.Exp,
                               scale=float(HD) ** -0.5).then_inc(exp_ready, 1)

            def oT_copy(st):
                if not st.runs(LAG_OUT):
                    return
                st.wait(act, o_psum, LAG_OUT, per=TILES)
                act.activation(oT[:], o_acc[:], ACT.Copy).then_inc(oT_ready, 1)

            def x4_act(st):
                if not st.runs(LAG_OUT):
                    return
                b = st.buf(LAG_OUT)
                if st.inside is not None or st.s - LAG_OUT >= 2:
                    act.wait_ge(x4_out[b], 16 * st.batch(LAG_OUT))
                normalise(st, 5, LAG_OUT, bank[2], x4[b])

            def body(st):
                qv_copy(st, 0)
                uT_act(st)
                attnT_copy(st)
                qv_copy(st, 1)
                x2_act(st)
                n1_act(st)
                x2T_copy(st)
                tanh_act(st)
                x1T_act(st)
                prob_exp(st, 0)
                relu_act(st, 0)
                relu_act(st, 1)
                oT_copy(st)
                qv_copy(st, 2)
                relu_act(st, 2)
                relu_act(st, 3)
                x3_act(st)
                xT_copy(st)
                qv_copy(st, 3)
                x3T_copy(st)
                n2_act(st)
                x4_act(st)
                q_k_v(st)
                prob_exp(st, 1)

            run_steps(act, chunks, body)

            def yT_act(st):
                if not st.runs(LAG_Y):
                    return
                st.wait(act, yT_psum, LAG_Y)
                if st.ran(LAG_Y, 2):
                    st.wait(act, masked_ready, LAG_EXPERTS, per=2 * EXPERTS, short=EXPERTS)
                    act.wait_ge(y_copied[st.buf(LAG_Y)], 16 * st.batch(LAG_Y))
                act.activation(yT[st.buf(LAG_Y)][:], bank[0][:], ACT.Copy).then_inc(yT_ready, 1)

            def chosenT_act(st):
                if not st.runs(LAG_GATE):
                    return
                st.wait(act, chosenT_psum, LAG_GATE)
                if st.ran(LAG_GATE, 2):
                    st.wait(act, used, LAG_EXPERTS, per=2 * EXPERTS, before=1)
                    act.wait_ge(choice_out[st.buf(LAG_GATE)], 16 * st.batch(LAG_GATE))
                act.activation(chosenT[st.buf(LAG_GATE)][:], chosenT_bank, ACT.Copy).then_inc(chosenT_ready, 1)

            def gelu_act(st):
                if not st.runs(LAG_EXPERTS):
                    return
                st.wait(act, used, LAG_EXPERTS, per=2 * EXPERTS, short=EXPERTS)
                if st.ran(LAG_EXPERTS, 1):
                    st.wait(act, masked_ready, LAG_EXPERTS, per=2 * EXPERTS, before=1)
                act.activation(gT, bank[3][:], ACT.Gelu).then_inc(gT_ready, 1)

            def moeT_act(st):
                if not st.runs(LAG_EXPERTS):
                    return
                st.wait(act, used, LAG_EXPERTS, per=2 * EXPERTS)
                if st.ran(LAG_EXPERTS, 1):
                    st.wait(act, s_psum[6], LAG_RESULT)
                act.activation(moeT, bank[4][:], ACT.Copy).then_inc(moeT_ready, 1)

            def result_act(st):
                if not st.runs(LAG_RESULT):
                    return
                b = st.buf(LAG_RESULT)
                if st.ran(LAG_RESULT, 2):
                    act.wait_ge(result_out[b], 16 * st.batch(LAG_RESULT))
                normalise(st, 6, LAG_RESULT, bank[5], result[b])

            def body2(st):
                chosenT_act(st)
                gelu_act(st)
                yT_act(st)
                result_act(st)
                moeT_act(st)

            run_steps(act, chunks, body2, 0, PEELED2, LAG_RESULT)

        @block.vector
        def _(dve):
            dve.memset(ones_bf[:], 1.0).then_inc(dve_prep, 1)
            dve.memset(v_one[:, :, P:], 1.0).then_inc(dve_prep, 1)
            dve.memset(minus_half[:], -0.5).then_inc(dve_prep, 1)
            dve.memset(bias3[:], 0.0).then_inc(dve_prep, 1)
            dve.wait_ge(consts, 1)
            dve.tensor_copy(ident_bf[:], ident[:]).then_inc(dve_prep, 1)
            dve.wait_ge(pool_prep, 4)
            dve.tensor_copy(head_mask[:].rearrange("p (h m) -> p h m", h=HEADS),
                            head_of[:].unsqueeze(2).broadcast_to([P, HEADS, HD])).then_inc(dve_prep, 1)
            for e in range(EXPERTS):
                dve.memset(prefer[:, e:e + 1], float(EXPERTS - e)).then_inc(dve_prep, 1)
            dve.wait_ge(dve_prep, 6 + EXPERTS)
            up = rows[:, (ROW["bqkv"] + 1) * P:(ROW["bqkv"] + 3) * P]
            dve.wait_ge(prep_mm, 6)
            dve.tensor_tensor(up, bank[2][0:1, 0:2 * P], up, ALU.add).then_inc(kv_bias_ready, 1)
            dve.wait_ge(kv_bias_ready, 1)
            dve.tensor_copy(eb_parts[:, 0, :], eb[:]).then_inc(eb_split, 1)
            dve.wait_ge(eb_split, 1)
            dve.tensor_tensor(eb_left[:], eb[:], eb_parts[:, 0, :], ALU.subtract).then_inc(eb_split, 1)
            dve.wait_ge(eb_split, 2)
            dve.tensor_copy(eb_parts[:, 1, :], eb_left[:]).then_inc(eb_split, 1)
            dve.wait_ge(eb_split, 3)
            dve.tensor_tensor(eb_left[:], eb_left[:], eb_parts[:, 1, :], ALU.subtract).then_inc(eb_split, 1)
            dve.wait_ge(eb_split, 4)
            dve.tensor_copy(eb_parts[:, 2, :], eb_left[:]).then_inc(eb_split, 1)
            dve.tensor_copy(parts[:, 0, :], rows[:]).then_inc(rows_split, 1)
            dve.wait_ge(rows_split, 1)
            dve.tensor_tensor(rows_left[:], rows[:], parts[:, 0, :], ALU.subtract).then_inc(rows_split, 1)
            dve.wait_ge(rows_split, 2)
            dve.tensor_copy(parts[:, 1, :], rows_left[:]).then_inc(rows_split, 1)
            dve.wait_ge(rows_split, 3)
            dve.tensor_tensor(rows_left[:], rows_left[:], parts[:, 1, :], ALU.subtract).then_inc(rows_split, 1)
            dve.wait_ge(rows_split, 4)
            dve.tensor_copy(parts[:, 2, :], rows_left[:]).then_inc(rows_split, 1)

            def moments(n, k, src):
                for j in range(TILES):
                    last = dve.bn_stats(stats[k][:, j, :], tile(src, j))
                last.then_inc(stats_done[k], 1)
                dve.wait_ge(dve_prep, 1)
                dve.wait_ge(stats_done[k], n)
                for j in range(TILES):
                    last = dve.bn_aggr(mean_var[k][:, j, :], stats[k][:, j, :])
                last.then_inc(mean_done[k], 1)
                dve.wait_ge(mean_done[k], n)
                dve.tensor_scalar(minus_mean[k][:], mean_var[k][:, :, 0], -1.0, None, ALU.mult)
                dve.tensor_scalar(var_eps[k][:], mean_var[k][:, :, 1], EPS_LN, None, ALU.add).then_inc(moments_ready[k], 1)

            def elu_q(st):
                if not st.runs(LAG_IN):
                    return
                st.wait(dve, q_exp, LAG_IN)
                st.wait(dve, num_psum, LAG_MLP)
                dve.scalar_tensor_tensor(qT[st.buf(LAG_IN)][:], bank[3][:], 0.0, exp_q[:], ALU.max,
                                         ALU.add).then_inc(q_ready, 1)

            def elu_k(st):
                if not st.runs(LAG_IN):
                    return
                st.wait(dve, k_exp, LAG_IN)
                st.wait(dve, kv_psum, LAG_IN, before=1)
                dve.scalar_tensor_tensor(k_tok[:], bank[4][:], 0.0, exp_k[:], ALU.max,
                                         ALU.add).then_inc(k_ready, 1)

            def kv_blocks(st):
                if not st.runs(LAG_IN) or st.buf(LAG_IN) == 0:
                    return
                st.wait(dve, kv_psum, LAG_IN)
                st.wait(dve, num_psum, LAG_MLP)
                dve.tensor_copy(k_sum[:], kv_acc[:, P:P + 1]).then_inc(kv_sum, 1)
                dve.tensor_tensor(kv[:, 0:P], kv_acc[:, 0:P], head_mask[:], ALU.mult)
                dve.wait_ge(kv_sum, st.batch(LAG_IN) + 1)
                dve.tensor_scalar(kv[:, P:], head_of[:], k_sum[:, 0:1], None, ALU.mult).then_inc(kv_ready, 1)

            def attn(st):
                if not st.runs(LAG_MLP):
                    return
                st.wait(dve, den_psum, LAG_MLP)
                dve.tensor_scalar(den[:], bank[3][:, 0:TILES * HEADS], EPS_ATTN, None, ALU.add).then_inc(den_ready, 1)
                st.wait(dve, den_ready, LAG_MLP)
                dve.reciprocal(z[:], den[:]).then_inc(z_ready, 1)
                st.wait(dve, z_ready, LAG_MLP)
                st.wait(dve, num_psum, LAG_MLP)
                dve.tensor_tensor(attn_tok[:].rearrange("p (a m) -> p a m", m=HD),
                                  bank[0][:].rearrange("p (a m) -> p a m", m=HD),
                                  z[:].unsqueeze(2).broadcast_to([P, TILES * HEADS, HD]),
                                  ALU.mult).then_inc(attn_ready, 1)

            def moments_of(st, k, lag, src):
                if st.runs(lag):
                    st.wait(dve, s_psum[k], lag)
                    moments(st.done(lag), k, src)

            def heads_scores(st, j):
                if not st.runs(LAG_HEADS):
                    return
                b = bank[1 if j % 2 == 0 else 4]
                k_view = b[:, P:3 * P].rearrange("p (g w) -> p g w", g=HEADS)[:, :, 0:HD]
                q_view = q_tok[:, j, :].rearrange("p (h d) -> p h d", h=HEADS)
                st.wait(dve, qv_ready, LAG_HEADS, per=TILES, short=TILES - 1 - j)
                dve.tensor_tensor(qk[j % 2][:].rearrange("p (h g d) -> p h g d", h=HEADS, g=HEADS),
                                  k_view.unsqueeze(1).broadcast_to([P, HEADS, HEADS, HD]),
                                  q_view.unsqueeze(2).broadcast_to([P, HEADS, HEADS, HD]),
                                  ALU.mult).then_inc(qk_ready, 1)
                st.wait(dve, qk_ready, LAG_HEADS, per=TILES, short=TILES - 1 - j)
                if j % 2 == 0:
                    st.wait(dve, exp_ready, LAG_HEADS, per=2, short=1 - j // 2, before=1)
                dve.tensor_reduce(score[:, j, :], qk[j % 2][:].rearrange("p (a d) -> p a d", d=HD), AX.X,
                                  ALU.add).then_inc(score_ready, 1)

            def softmax_top(st, pair):
                if not st.runs(LAG_HEADS):
                    return
                two = slice(2 * pair, 2 * pair + 2)
                view = score[:, two, :].rearrange("p j (h g) -> p (j h) g", g=HEADS)
                st.wait(dve, score_ready, LAG_HEADS, per=TILES, short=2 - 2 * pair)
                dve.tensor_reduce(top[:, two, :].rearrange("p j h -> p (j h)"), view, AX.X, ALU.max).then_inc(top_ready, 1)
                st.wait(dve, top_ready, LAG_HEADS, per=2, short=1 - pair)
                dve.tensor_tensor(view, view, top[:, two, :].rearrange("p j h -> p (j h)").unsqueeze(2)
                                  .broadcast_to([P, 2 * HEADS, HEADS]), ALU.subtract).then_inc(below_top, 1)

            def softmax_total(st, pair):
                if not st.runs(LAG_HEADS):
                    return
                two = slice(2 * pair, 2 * pair + 2)
                st.wait(dve, exp_ready, LAG_HEADS, per=2, short=1 - pair)
                dve.tensor_reduce(total[:, two, :].rearrange("p j h -> p (j h)"),
                                  prob_e[:, two, :].rearrange("p j (h g) -> p (j h) g", g=HEADS), AX.X,
                                  ALU.add).then_inc(total_ready, 1)
                st.wait(dve, total_ready, LAG_HEADS, per=2, short=1 - pair)
                st.wait(dve, prob_ready, LAG_HEADS, per=2, short=1 - pair, before=1)
                dve.reciprocal(inv_total[:, two, :], total[:, two, :]).then_inc(inv_ready, 1)

            def body(st):
                attn(st)
                heads_scores(st, 0)
                moments_of(st, 3, LAG_TANH, bank[5])
                moments_of(st, 1, LAG_MLP, bank[3])
                heads_scores(st, 1)
                softmax_top(st, 0)
                softmax_total(st, 0)
                moments_of(st, 4, LAG_TANH, bank[5])
                heads_scores(st, 2)
                moments_of(st, 5, LAG_OUT, bank[2])
                moments_of(st, 2, LAG_MLP, bank[3])
                heads_scores(st, 3)
                softmax_top(st, 1)
                elu_q(st)
                elu_k(st)
                kv_blocks(st)
                softmax_total(st, 1)

            run_steps(dve, chunks, body)

            def choose(st):
                if not st.runs(LAG_GATE):
                    return
                by_expert = [P, TILES, EXPERTS]
                st.wait(dve, gate_psum, LAG_GATE)
                dve.tensor_copy(gate[:], bank[1][:, 0:TILES * EXPERTS]
                                .rearrange("p (j e) -> p j e", e=EXPERTS)).then_inc(gate_read, 1)
                st.wait(dve, gate_read, LAG_GATE)
                dve.tensor_reduce(gate_top[:], gate[:], AX.X, ALU.max).then_inc(gate_step, 1)
                st.wait(dve, gate_step, LAG_GATE, per=4, short=3)
                dve.tensor_tensor(gate_is[:], gate[:], gate_top[:].unsqueeze(2).broadcast_to(by_expert),
                                  ALU.is_equal).then_inc(gate_step, 1)
                st.wait(dve, gate_step, LAG_GATE, per=4, short=2)
                dve.tensor_tensor(gate_pref[:], gate_is[:], prefer[:].unsqueeze(1).broadcast_to(by_expert),
                                  ALU.mult).then_inc(gate_step, 1)
                st.wait(dve, gate_step, LAG_GATE, per=4, short=1)
                dve.tensor_reduce(gate_first[:], gate_pref[:], AX.X, ALU.max).then_inc(gate_step, 1)
                st.wait(dve, gate_step, LAG_GATE, per=4)
                if st.ran(LAG_GATE, 1):
                    st.wait(dve, chosenT_psum, LAG_GATE, before=1)
                for r in range(3):
                    last = dve.tensor_tensor(chosen[:, :, r * EXPERTS:(r + 1) * EXPERTS], gate_pref[:],
                                             gate_first[:].unsqueeze(2).broadcast_to(by_expert), ALU.is_equal)
                last.then_inc(chosen_ready, 1)

            def mask_operand(st, layer, experts):
                if not st.runs(LAG_EXPERTS):
                    return
                b = st.buf(LAG_EXPERTS)
                src = gT if layer else yT[b]
                for e in experts:
                    n = layer * EXPERTS + e
                    if n == 0:
                        st.wait(dve, yT_ready, LAG_EXPERTS)
                        dve.wait_ge(mask_in[b], 16 * (st.batch(LAG_EXPERTS) + 1))
                    if layer and e == 0:
                        st.wait(dve, gT_ready, LAG_EXPERTS)
                    if n >= AHEAD:
                        st.wait(dve, used, LAG_EXPERTS, per=2 * EXPERTS, short=2 * EXPERTS - 1 - (n - AHEAD))
                    elif st.ran(LAG_EXPERTS, 1):
                        st.wait(dve, used, LAG_EXPERTS, per=2 * EXPERTS, short=AHEAD - 1 - n, before=1)
                    dve.tensor_tensor(masked[e % AHEAD], mask[b][:, e * CHUNK:(e + 1) * CHUNK], src[:],
                                      ALU.mult).then_inc(masked_ready, 1)

            def body2(st):
                mask_operand(st, 0, range(0, 6))
                choose(st)
                mask_operand(st, 0, range(6, 8))
                mask_operand(st, 1, range(0, 6))
                moments_of(st, 6, LAG_RESULT, bank[5])
                mask_operand(st, 1, range(6, 8))

            run_steps(dve, chunks, body2, 0, PEELED2, LAG_RESULT)

        @block.gpsimd
        def _(pool):
            pool.memset(ident[:], 0.0).then_inc(pool_prep, 1)
            pool.memset(head_of[:], 1.0).then_inc(pool_prep, 1)
            pool.wait_ge(pool_prep, 2)
            pool.affine_select(out=ident[:], in_=ident[:], compare_op=ALU.not_equal, fill=1.0, base=0,
                               pattern=[[-1, P]], channel_multiplier=1).then_inc(consts, 1)
            pool.affine_select(out=head_of[:], in_=head_of[:], compare_op=ALU.is_ge, fill=0.0, base=0,
                               pattern=[[-HD, HEADS]], channel_multiplier=1).then_inc(pool_prep, 1)
            pool.wait_ge(pool_prep, 3)
            pool.affine_select(out=head_of[:], in_=head_of[:], compare_op=ALU.is_ge, fill=0.0, base=HD - 1,
                               pattern=[[HD, HEADS]], channel_multiplier=-1).then_inc(pool_prep, 1)

            def rsqrt(n, k):
                pool.wait_ge(moments_ready[k], n)
                pool.tensor_tensor(rstd[k][:], var_eps[k][:], minus_half[:], ALU.pow).then_inc(rstd_ready[k], 1)
                pool.wait_ge(rstd_ready[k], n)
                pool.tensor_tensor(shift[k][:], minus_mean[k][:], rstd[k][:], ALU.mult).then_inc(shift_ready[k], 1)

            def rsqrt_of(st, k, lag):
                if st.runs(lag):
                    rsqrt(st.done(lag), k)

            def probs(st, pair, lag, before=0):
                if not st.runs(lag):
                    return
                two = slice(2 * pair, 2 * pair + 2)
                st.wait(pool, inv_ready, lag, per=2, short=1 - pair)
                pool.tensor_tensor(prob[:, two, :].rearrange("p j (h g) -> p (j h) g", g=HEADS),
                                   prob_e[:, two, :].rearrange("p j (h g) -> p (j h) g", g=HEADS),
                                   inv_total[:, two, :].rearrange("p j h -> p (j h)").unsqueeze(2)
                                   .broadcast_to([P, 2 * HEADS, HEADS]), ALU.mult).then_inc(prob_ready, 1)

            def weigh(st, j, lag, parts=range(4)):
                if not st.runs(lag):
                    return
                if 0 in parts:
                    st.wait(pool, prob_ready, lag, per=2, short=1 - j // 2)
                    st.wait(pool, o_psum, lag, per=TILES, short=TILES - 1 - j if lag < LAG_OUT else 0, before=1)
                p_view = prob[:, j, :].rearrange("p (h g) -> p g h", g=HEADS)
                v_view = v_tok[:, j, :].rearrange("p (g d) -> p g d", g=HEADS)
                quarter = HEADS // 4
                for part in parts:
                    g = slice(part * quarter, (part + 1) * quarter)
                    last = pool.tensor_tensor(
                        pv[j][:, part * quarter * P:(part + 1) * quarter * P]
                        .rearrange("p (g h d) -> p g h d", g=quarter, h=HEADS),
                        p_view[:, g, :].unsqueeze(3).broadcast_to([P, quarter, HEADS, HD]),
                        v_view[:, g, :].unsqueeze(2).broadcast_to([P, quarter, HEADS, HD]), ALU.mult)
                if 3 in parts:
                    last.then_inc(pv_ready, 1)

            def body(st):
                probs(st, 1, LAG_OUT)
                weigh(st, 2, LAG_OUT)
                weigh(st, 3, LAG_OUT, (0, 1))
                rsqrt_of(st, 3, LAG_TANH)
                rsqrt_of(st, 1, LAG_MLP)
                weigh(st, 3, LAG_OUT, (2, 3))
                probs(st, 0, LAG_HEADS)
                rsqrt_of(st, 4, LAG_TANH)
                weigh(st, 0, LAG_HEADS, (0, 1))
                weigh(st, 0, LAG_HEADS, (2, 3))
                rsqrt_of(st, 5, LAG_OUT)
                rsqrt_of(st, 2, LAG_MLP)
                weigh(st, 1, LAG_HEADS)

            run_steps(pool, chunks, body)

            def body2(st):
                rsqrt_of(st, 6, LAG_RESULT)

            run_steps(pool, chunks, body2, 0, PEELED2, LAG_RESULT)


def kernel(**inputs):
    import numpy as np
    import concourse.bacc as bacc
    from concourse.bass_utils import run_bass_kernel_spmd

    nc = bacc.Bacc("TRN2", target_bir_lowering=False, num_devices=1)
    arrays, aps = {}, {}
    for name, value in inputs.items():
        a = np.ascontiguousarray(value)
        arrays[f"in_{name}"] = a
        aps[name] = nc.dram_tensor(f"in_{name}", a.shape, mybir.dt.from_np(a.dtype), kind="ExternalInput").ap()
    shape = arrays["in_L0_attn_x"].shape
    out = nc.dram_tensor("out_0", shape, F32, kind="ExternalOutput").ap()
    scratch = nc.dram_tensor("x4_scratch", (shape[0] * shape[1] // TILES, CHUNK), F32, kind="Internal").ap()
    choice = nc.dram_tensor("choice_scratch", (shape[0] * shape[1] // CHUNK * EXPERTS, CHUNK), BF16, kind="Internal").ap()
    build(nc, aps, out, scratch, choice)
    r = run_bass_kernel_spmd(nc, [arrays], core_ids=[0])
    return r.results[0]["out_0"]
```

```python
from contextlib import ExitStack

import concourse.bass as bass
from concourse import mybir

F32 = mybir.dt.float32
BF16 = mybir.dt.bfloat16
ALU = mybir.AluOpType
ACT = mybir.ActivationFunctionType
AX = mybir.AxisListType

P = 128
HEADS = 16
HD = P // HEADS
TILES = 4
CHUNK = TILES * P
EPS_LN = 1e-5
EPS_ATTN = 1e-6
FF = 4
EXPERTS = 8
LATENT = 32

ROW = {"bq": 0, "bk": 1, "bv": 2, "bo": 3, "b2": 4, "bout": 5, "bqkv": 6}
KV_ROW = 7
N_ROWS = 9

LAG_IN, LAG_MLP, LAG_TANH, LAG_HEADS, LAG_OUT = 0, 2, 3, 4, 5
LAG_Y, LAG_GATE, LAG_EXPERTS, LAG_RESULT = range(4)
PEELED2 = 4
AHEAD = 8
PEELED = LAG_OUT + 1


class Step:

    def __init__(self, s, chunks, inside=None, pair=None):
        self.s, self.chunks, self.inside, self.pair = s, chunks, inside, pair
        self.par = (s if inside is None else inside) % 2

    def runs(self, lag):
        return self.inside is not None or 0 <= self.s - lag < self.chunks

    def chunk(self, lag):
        return self.s - lag

    def buf(self, lag):
        return (self.par - lag) % 2

    def done(self, lag, before=0):
        n = self.s - (lag + before - 1)
        return n if self.inside is not None else max(0, min(self.chunks, n))

    def ran(self, lag, before=0):
        return self.inside is not None or 0 <= self.s - lag - before < self.chunks

    def after(self, eng, *uses):
        for sem, lag, *more in uses:
            before, per, short = (*more, *(0, 1, 0)[len(more):])
            if self.ran(lag, before):
                return self.wait(eng, sem, lag, per, short, before)

    def batch(self, lag):
        return (self.s - lag) // 2 if self.inside is None else self.pair + (self.inside - lag) // 2

    def wait(self, eng, sem, lag, per=1, short=0, before=0):
        n = self.done(lag, before)
        if self.inside is not None:
            eng.wait_ge(sem, n * per - short if short else n * per)
        elif n * per - short > 0:
            eng.wait_ge(sem, n * per - short)


def loop_steps(eng, chunks, body, peeled):
    with eng.Fori(peeled // 2, chunks // 2) as pair:
        for u in range(2):
            body(Step(2 * pair + u, chunks, inside=u, pair=pair))


def run_steps(eng, chunks, body, body2, first=0):
    for s in range(first, PEELED):
        body(Step(s, chunks))
    loop_steps(eng, chunks, body, PEELED)
    for s in range(chunks, chunks + LAG_OUT - 2):
        body(Step(s, chunks))
    body2(Step(0, chunks))
    body2(Step(1, chunks))
    body(Step(chunks + LAG_OUT - 2, chunks))
    body2(Step(2, chunks))
    body(Step(chunks + LAG_OUT - 1, chunks))
    body2(Step(3, chunks))
    loop_steps(eng, chunks, body2, PEELED2)
    for s in range(chunks, chunks + LAG_RESULT):
        body2(Step(s, chunks))


def build(nc, t, out, scratch, choice):
    n_tokens = t["L0_attn_x"].shape[0] * t["L0_attn_x"].shape[1]
    chunks = n_tokens // CHUNK
    per_batch = t["L0_attn_x"].shape[1] // CHUNK
    assert per_batch == 2 and chunks % 2 == 0 and chunks > PEELED

    x_d = t["L0_attn_x"].rearrange("n (c p j) d -> (n c) p (j d)", c=per_batch, j=TILES)
    out_d = out.rearrange("n (c p j) d -> (n c) p (j d)", c=per_batch, j=TILES)
    choice_d = choice.rearrange("(c e) n -> c e n", e=EXPERTS)
    scratch_d = scratch.rearrange("(c p) w -> c p w", p=P)

    with ExitStack() as ctx:
        def sb(name, shape, dt=F32):
            return ctx.enter_context(nc.sbuf_tensor(name, shape, dt))

        def sem(name):
            return ctx.enter_context(nc.semaphore(name))

        bank = [ctx.enter_context(nc.psum_tensor(f"bank{i}", [P, CHUNK], F32)) for i in range(8)]
        kv_acc, o_acc = bank[6], bank[7]

        ident = sb("ident", [P, P])
        ident_bf = sb("ident_bf", [P, P], BF16)
        ones_bf = sb("ones_bf", [P, CHUNK], BF16)
        head_of = sb("head_of", [P, HEADS])
        head_mask = sb("head_mask", [P, P])
        minus_half = sb("minus_half", [P, TILES])
        minus_one = sb("minus_one", [P, TILES])
        eps = sb("eps", [P, TILES])
        prefer = sb("prefer", [P, EXPERTS])

        wq, wk, wv, wo = (sb(n, [P, P]) for n in ("wq", "wk", "wv", "wo"))
        w1 = sb("w1", [P, FF * P])
        w2 = sb("w2", [P, FF, P])
        wt = [sb(f"wt{i}", [P, P]) for i in range(3)]
        wtT = sb("wtT", [P, P])
        wt01T = sb("wt01T", [P, P])
        w_tanh = sb("w_tanh", [P, P])
        w_qkv = sb("w_qkv", [P, 3 * P])
        wdown = sb("wdown", [P, LATENT])
        wdownT = sb("wdownT", [LATENT, P])
        wup = sb("wup", [LATENT, 2 * P])
        bdown = sb("bdown", [LATENT, 1])
        wout = sb("wout", [P, P])
        wg = sb("wg", [P, EXPERTS])
        e1 = sb("e1", [P, EXPERTS, P])
        e2 = sb("e2", [P, EXPERTS, P])
        eb = sb("eb", [EXPERTS, 2 * P])
        eb_left = sb("eb_left", [EXPERTS, 2 * P])
        eb_parts = sb("eb_parts", [EXPERTS, 3, 2 * P], BF16)
        eb3 = sb("eb3", [3 * EXPERTS, 2 * P], BF16)
        cols = sb("cols", [P, FF + 5])
        col_rows = sb("col_rows", [FF + 5, P])
        rows = sb("rows", [KV_ROW, P])
        rows_left = sb("rows_left", [KV_ROW, P])
        parts = sb("parts", [KV_ROW, 3, P], BF16)
        kv_row = sb("kv_row", [1, 2 * P + EXPERTS])
        kv_row_left = sb("kv_row_left", [1, 2 * P + EXPERTS])
        kv_row_parts = sb("kv_row_parts", [1, 3, 2 * P + EXPERTS], BF16)
        bias3 = sb("bias3", [P, N_ROWS * P + EXPERTS], BF16)

        def row3(name, n=1):
            return bias3[:, ROW[name] * P:(ROW[name] + n) * P]

        def row3_by_tile(name):
            return row3(name).unsqueeze(1).broadcast_to([P, TILES, P])

        x_and_xT = sb("x_and_xT", [P, 4 * CHUNK])
        x_tok = [x_and_xT[:, i * CHUNK:(i + 1) * CHUNK] for i in range(2)]
        xT = [x_and_xT[:, (2 + i) * CHUNK:(3 + i) * CHUNK] for i in range(2)]
        qT = [sb(f"qT{i}", [P, CHUNK]) for i in range(2)]
        neg_q, neg_k = sb("neg_q", [P, CHUNK]), sb("neg_k", [P, CHUNK])
        exp_q, exp_k = sb("exp_q", [P, CHUNK]), sb("exp_k", [P, CHUNK])
        k_tok = sb("k_tok", [P, CHUNK])
        v_one = sb("v_one", [P, TILES, P + 1])
        kv = sb("kv", [P, P + HEADS])
        k_sum = sb("k_sum", [P, 1])
        den = sb("den", [P, TILES * HEADS])
        z = sb("z", [P, TILES * HEADS])
        attn_tok = sb("attn_tok", [P, CHUNK])
        attnT = sb("attnT", [P, CHUNK])
        n1 = sb("n1", [P, CHUNK])
        x1T = sb("x1T", [P, CHUNK])
        hT = sb("hT", [P, FF, CHUNK])
        n2 = sb("n2", [P, CHUNK])
        uT = sb("uT", [P, CHUNK])
        x2 = sb("x2", [P, CHUNK])
        x2T = sb("x2T", [P, CHUNK])
        tT = sb("tT", [P, CHUNK])
        x3 = sb("x3", [P, CHUNK])
        x3T = [sb(f"x3T{i}", [P, CHUNK]) for i in range(2)]
        q_tok = sb("q_tok", [P, TILES, P])
        v_tok = sb("v_tok", [P, TILES, P])
        qk = [sb(f"qk{i}", [P, HEADS * P]) for i in range(2)]
        score = sb("score", [P, TILES, HEADS * HEADS])
        top = sb("top", [P, TILES, HEADS])
        prob_e = sb("prob_e", [P, TILES, HEADS * HEADS])
        total = sb("total", [P, TILES, HEADS])
        inv_total = sb("inv_total", [P, TILES, HEADS])
        prob = sb("prob", [P, TILES, HEADS * HEADS])
        pv = [sb(f"pv{i}", [P, HEADS * P]) for i in range(TILES)]
        oT = sb("oT", [P, CHUNK])
        x_kept = [sb(f"x_kept{i}", [P, CHUNK]) for i in range(2)]
        x4 = [sb(f"x4{i}", [P, CHUNK]) for i in range(2)]

        norms = range(1, 7)
        stats = {k: sb(f"stats{k}", [P, TILES, 6]) for k in norms}
        mean_var = {k: sb(f"mean_var{k}", [P, TILES, 2]) for k in norms}
        minus_mean = {k: sb(f"minus_mean{k}", [P, TILES]) for k in norms}
        var_eps = {k: sb(f"var_eps{k}", [P, TILES]) for k in norms}
        rstd = {k: sb(f"rstd{k}", [P, TILES]) for k in norms}
        shift = {k: sb(f"shift{k}", [P, TILES]) for k in norms}
        stats_done = {k: sem(f"stats_done{k}") for k in norms}
        eps_added = {k: sem(f"eps_added{k}") for k in norms}
        moments_ready = {k: sem(f"moments_ready{k}") for k in norms}
        rstd_ready = {k: sem(f"rstd_ready{k}") for k in norms}
        shift_ready = {k: sem(f"shift_ready{k}") for k in norms}
        normed = {k: sem(f"normed{k}") for k in norms}

        y_tok = [sb(f"y_tok{i}", [P, CHUNK]) for i in range(2)]
        yT = [sb(f"yT{i}", [P, CHUNK]) for i in range(2)]
        gate = sb("gate", [P, TILES, EXPERTS])
        gate_top = sb("gate_top", [P, TILES])
        gate_is = sb("gate_is", [P, TILES, EXPERTS])
        gate_pref = sb("gate_pref", [P, TILES, EXPERTS])
        gate_first = sb("gate_first", [P, TILES])
        chosen = sb("chosen", [P, TILES, 3 * EXPERTS], BF16)
        chosenT = [sb(f"chosenT{i}", [3 * EXPERTS, CHUNK], BF16) for i in range(2)]
        gate_bank = bank[6][:, CHUNK // 2:CHUNK // 2 + TILES * EXPERTS]
        chosenT_bank = bank[6][0:3 * EXPERTS, 0:CHUNK // 2].bitcast(BF16)
        mask = [a[:].bitcast(BF16) for a in (hT, x_and_xT)]
        mask[0] = mask[0].rearrange("p a b -> p (a b)")
        masked = [qk[i // 4][:, (i % 4) * CHUNK:(i % 4 + 1) * CHUNK] for i in range(AHEAD)]
        gT, moeT = n1[:], x1T[:]
        result = [n2[:], uT[:]]
        y_kept = [x2[:], x2T[:]]

        biases_in, small_in, eb_in = sem("biases_in"), sem("small_in"), sem("eb_in")
        matrices_in, late_matrices_in = sem("matrices_in"), sem("late_matrices_in")
        x_in = [sem(f"x_in{i}") for i in range(2)]
        consts = sem("consts")
        pool_prep = sem("pool_prep")
        dve_prep = sem("dve_prep")
        prep_mm = sem("prep_mm")
        prep_out = sem("prep_out")
        kv_bias_ready = sem("kv_bias_ready")
        rows_split = sem("rows_split")
        kv_row_split = sem("kv_row_split")
        bias3_in, late_bias_in = sem("bias3_in"), sem("late_bias_in")
        eb_split = sem("eb_split")
        xT_psum, xT_ready = sem("xT_psum"), sem("xT_ready")
        q_psum, q_neg, q_exp, q_ready = sem("q_psum"), sem("q_neg"), sem("q_exp"), sem("q_ready")
        k_psum, k_neg, k_exp, k_ready = sem("k_psum"), sem("k_neg"), sem("k_exp"), sem("k_ready")
        v_psum, v_ready = sem("v_psum"), sem("v_ready")
        kv_psum, kv_sum, kv_ready = sem("kv_psum"), sem("kv_sum"), sem("kv_ready")
        den_psum, den_ready, z_ready = sem("den_psum"), sem("den_ready"), sem("z_ready")
        num_psum, attn_ready = sem("num_psum"), sem("attn_ready")
        attnT_psum, attnT_ready = sem("attnT_psum"), sem("attnT_ready")
        s_psum = {k: sem(f"s_psum{k}") for k in norms}
        n1T_psum, x1T_ready = sem("n1T_psum"), sem("x1T_ready")
        h_psum, h_act = sem("h_psum"), sem("h_act")
        n2T_psum, uT_ready = sem("n2T_psum"), sem("uT_ready")
        x2T_psum, x2T_ready = sem("x2T_psum"), sem("x2T_ready")
        t_psum, tT_ready = sem("t_psum"), sem("tT_ready")
        x3T_psum, x3T_ready = sem("x3T_psum"), sem("x3T_ready")
        qkv_psum, qv_ready = sem("qkv_psum"), sem("qv_ready")
        qk_ready, score_ready = sem("qk_ready"), sem("score_ready")
        top_ready, below_top, exp_ready = sem("top_ready"), sem("below_top"), sem("exp_ready")
        total_ready, inv_ready, prob_ready = sem("total_ready"), sem("inv_ready"), sem("prob_ready")
        pv_ready, o_psum, oT_ready = sem("pv_ready"), sem("o_psum"), sem("oT_ready")
        x_copied = [sem(f"x_copied{i}") for i in range(2)]
        x4_out = [sem(f"x4_out{i}") for i in range(2)]
        y_copied = [sem(f"y_copied{i}") for i in range(2)]
        y_in = [sem(f"y_in{i}") for i in range(2)]
        yT_psum, yT_ready = sem("yT_psum"), sem("yT_ready")
        gate_psum, gate_step = sem("gate_psum"), sem("gate_step")
        gate_read = sem("gate_read")
        chosen_ready, chosenT_psum, chosenT_ready = sem("chosen_ready"), sem("chosenT_psum"), sem("chosenT_ready")
        choice_out = [sem(f"choice_out{i}") for i in range(2)]
        mask_in = [sem(f"mask_in{i}") for i in range(2)]
        masked_ready, used = sem("masked_ready"), sem("used")
        gT_ready, moeT_ready = sem("gT_ready"), sem("moeT_ready")
        result_out = [sem(f"result_out{i}") for i in range(2)]

        bias_loads = [
            (rows[ROW[key]:ROW[key] + 1, :], t[name].rearrange("(a n) -> a n", a=1))
            for key, name in (("bq", "L0_attn_bq"), ("bk", "L0_attn_bk"), ("bv", "L0_attn_bv"), ("bo", "L0_attn_bo"),
                              ("b2", "L0_attn_b2"), ("bout", "L1_attn_bout"), ("bqkv", "L1_attn_bq"))]
        small_loads = [
            (wdown, t["L1_attn_Wdown"]), (wup, t["L1_attn_Wup"]),
            (bdown, t["L1_attn_bdown"].rearrange("(p a) -> p a", a=1)),
            (kv_row[:, 0:2 * P], t["L1_attn_bup"].rearrange("(a n) -> a n", a=1)),
            (kv_row[:, 2 * P:], t["L1_ffn_bg"].rearrange("(a n) -> a n", a=1)),
            (col_rows[0:FF, :], t["L0_attn_b1"].rearrange("(f p) -> f p", p=P)),
        ] + [
            (col_rows[FF + i:FF + i + 1, :], t[name].rearrange("(a p) -> a p", a=1))
            for i, name in enumerate(("L0_ffn_bias", "L0_attn_g1", "L0_attn_beta1", "L0_attn_g2", "L0_attn_beta2"))]
        expert_bias_loads = [(eb[:, 0:P], t["L1_ffn_b1"]), (eb[:, P:], t["L1_ffn_b2"])]
        matrix_loads = [
            (wt[0], t["L0_ffn_weight"]), (wt[1], t["L0_ffn_aux_weight1"]), (wt[2], t["L0_ffn_aux_weight2"]),
            (wq, t["L0_attn_Wq"]), (wk, t["L0_attn_Wk"]), (wv, t["L0_attn_Wv"]), (wo, t["L0_attn_Wo"]),
            (w1, t["L0_attn_W1"]), (w2, t["L0_attn_W2"].rearrange("(f p) n -> p f n", p=P)),
            (w_qkv[:, 0:P], t["L1_attn_Wq"]), (wout, t["L1_attn_Wout"]), (wg, t["L1_ffn_Wg"]),
            (e1, t["L1_ffn_W1"].rearrange("e p i -> p e i")),
            (e2, t["L1_ffn_W2"].rearrange("e p i -> p e i")),
        ]
        EARLY = 6
        b1_col, tanh_col, g1_col, beta1_col, g2_col, beta2_col = (
            0, *(FF + i for i in range(5)))

        def col(i):
            return cols[:, i:i + 1]

        def tile(a, j):
            return a[:, j * P:(j + 1) * P]

        block = ctx.enter_context(nc.Block())

        @block.sync
        def _(sp):
            def load_x(st):
                if not st.runs(LAG_IN):
                    return
                st.wait(sp, xT_psum, LAG_IN, before=2)
                sp.dma_start(x_tok[st.buf(LAG_IN)][:], x_d[st.chunk(LAG_IN)]).then_inc(x_in[st.buf(LAG_IN)], 16)

            def store_x4(st):
                if not st.runs(LAG_OUT):
                    return
                st.wait(sp, normed[5], LAG_OUT)
                sp.dma_start(scratch_d[st.chunk(LAG_OUT)], x4[st.buf(LAG_OUT)][:]).then_inc(x4_out[st.buf(LAG_OUT)], 16)

            def keep_x(st):
                if not st.runs(LAG_MLP):
                    return
                b = st.buf(LAG_MLP)
                sp.wait_ge(rows_split, 5)
                st.wait(sp, xT_ready, LAG_MLP)
                st.wait(sp, s_psum[3], LAG_TANH, before=1)
                sp.dma_start(x_kept[b][:], xT[b][:]).then_inc(x_copied[b], 16)

            def body(st):
                load_x(st)
                keep_x(st)
                store_x4(st)
                if st.inside is None and st.s == chunks + LAG_OUT - 4:
                    load_y(Step(0, chunks))
                    load_y(Step(1, chunks))

            sp.dma_start(x_tok[0][:], x_d[0]).then_inc(x_in[0], 16)
            for dst, src in bias_loads:
                sp.dma_start(dst[:], src).then_inc(biases_in, 16)
            for dst, src in small_loads:
                sp.dma_start(dst[:], src).then_inc(small_in, 16)
            sp.wait_ge(rows_split, 5)
            for r in range(3):
                sp.dma_start(bias3[r:r + 1, 0:KV_ROW * P], parts[:, r, :]).then_inc(bias3_in, 16)
            for dst, src in expert_bias_loads:
                sp.dma_start(dst[:], src).then_inc(eb_in, 16)
            sp.dma_start(x_tok[1][:], x_d[1]).then_inc(x_in[1], 16)
            sp.wait_ge(kv_row_split, 5)
            sp.dma_start(bias3[0:3, KV_ROW * P:], kv_row_parts[0:1, :, :]).then_inc(late_bias_in, 16)
            sp.wait_ge(eb_split, 5)
            for r in range(3):
                sp.dma_start(eb3[r * EXPERTS:(r + 1) * EXPERTS, :], eb_parts[:, r, :]).then_inc(late_bias_in, 16)
            def load_y(st):
                if not st.runs(LAG_Y):
                    return
                if st.inside is None and st.s <= 3:
                    for i in range(2):
                        sp.wait_ge(x4_out[i], 16 * (chunks // 2 - (2, 2, 1, 0)[st.s]))
                if st.ran(LAG_Y, 2):
                    st.wait(sp, yT_psum, LAG_Y, before=2)
                sp.dma_start(y_tok[st.buf(LAG_Y)][:], scratch_d[st.chunk(LAG_Y)]
                             ).then_inc(y_in[st.buf(LAG_Y)], 16)

            def keep_y(st):
                if not st.runs(LAG_EXPERTS):
                    return
                b = st.buf(LAG_EXPERTS)
                sp.wait_ge(rows_split, 5)
                st.wait(sp, yT_ready, LAG_EXPERTS)
                if st.ran(LAG_RESULT, 1):
                    st.wait(sp, s_psum[6], LAG_RESULT, before=1)
                sp.dma_start(y_kept[b], yT[b][:]).then_inc(y_copied[b], 16)

            def spread_choice(st):
                if not st.runs(LAG_GATE):
                    return
                b = st.buf(LAG_GATE)
                st.wait(sp, chosenT_ready, LAG_GATE)
                sp.dma_start(choice_d[st.chunk(LAG_GATE)], chosenT[b][0:EXPERTS, :]).then_inc(choice_out[b], 16)
                sp.wait_ge(choice_out[b], 16 * (st.batch(LAG_GATE) + 1))
                sp.dma_start(mask[b], choice_d[st.chunk(LAG_GATE)].rearrange("(a e) n -> a (e n)", a=1)
                             .broadcast_to([P, EXPERTS * CHUNK])).then_inc(mask_in[b], 16)

            def store(st):
                if not st.runs(LAG_RESULT):
                    return
                st.wait(sp, normed[6], LAG_RESULT)
                sp.dma_start(out_d[st.chunk(LAG_RESULT)], result[st.buf(LAG_RESULT)]
                             ).then_inc(result_out[st.buf(LAG_RESULT)], 16)

            def body2(st):
                if st.inside is not None or st.s >= 2:
                    load_y(st)
                keep_y(st)
                spread_choice(st)
                store(st)

            run_steps(sp, chunks, body, body2, first=2)
            for u in range(2):
                sp.wait_ge(result_out[u], 16 * (chunks // 2))

        @block.tensor
        def _(pe):
            def mm(out_, lhsT, rhs, start=False, stop=False):
                return pe.matmul(out_, lhsT, rhs, start=start, stop=stop, skip_group_check=True)

            def turn(out_, in_, start=True, stop=True):
                return pe.matmul(out_, in_, ident[:], is_transpose=True, start=start, stop=stop,
                                 skip_group_check=True)

            def turn4(out_, in_, start=True, stop=True):
                for j in range(TILES):
                    last = turn(tile(out_, j), tile(in_, j), start=start and j == 0, stop=stop)
                return last

            pe.wait_ge(consts, 1)
            pe.wait_ge(small_in, 16 * len(small_loads))
            pe.wait_ge(matrices_in, 16 * EARLY)
            turn(bank[0][:, 0:P], wt[0][:]).then_inc(prep_mm, 1)
            pe.matmul(bank[1][0:LATENT, 0:P], wdown[:], ident[:], is_transpose=True,
                      start=True, stop=True).then_inc(prep_mm, 1)
            pe.matmul(bank[3][:, 0:FF + 5], col_rows[:], ident[0:FF + 5, 0:FF + 5], is_transpose=True,
                      start=True, stop=True).then_inc(prep_mm, 1)
            pe.wait_ge(prep_out, 1)
            mm(bank[0][:, 0:P], wt[1][:], wtT[:], True, True).then_inc(prep_mm, 1)
            pe.wait_ge(prep_out, 2)
            mm(bank[1][:, 0:2 * P], wdownT[:], wup[:], True, True).then_inc(prep_mm, 1)
            mm(bank[7][0:1, 0:2 * P], bdown[:], wup[:], True, True).then_inc(prep_mm, 1)
            pe.wait_ge(prep_out, 4)
            mm(bank[0][:, 0:P], wt01T[:], wt[2][:], True, True).then_inc(prep_mm, 1)
            pe.wait_ge(prep_out, 6)
            pe.wait_ge(bias3_in, 48)
            pe.wait_ge(dve_prep, 6 + EXPERTS)

            def xT_mm(st):
                if not st.runs(LAG_IN):
                    return
                b = st.buf(LAG_IN)
                pe.wait_ge(x_in[b], 16 * (st.batch(LAG_IN) + 1))
                st.after(pe, (h_act, LAG_MLP, 0, FF), (xT_ready, LAG_IN, 1))
                turn4(bank[0], x_tok[b]).then_inc(xT_psum, 1)

            def q_in(st):
                if not st.runs(LAG_IN):
                    return
                st.wait(pe, xT_ready, LAG_IN)
                st.after(pe, (normed[5], LAG_OUT), (h_act, LAG_MLP, 0, FF), (q_ready, LAG_IN, 1))
                mm(bank[2][:], row3("bq"), ones_bf[:], start=True)
                mm(bank[2][:], wq[:], xT[st.buf(LAG_IN)][:], stop=True).then_inc(q_psum, 1)

            def k_in(st):
                if not st.runs(LAG_IN):
                    return
                st.wait(pe, xT_ready, LAG_IN)
                st.after(pe, (qk_ready, LAG_HEADS, 0, TILES), (uT_ready, LAG_TANH), (k_ready, LAG_IN, 1))
                mm(bank[4][:], ones_bf[:, 0:P], row3_by_tile("bk"), start=True)
                for j in range(TILES):
                    last = mm(tile(bank[4], j), tile(xT[st.buf(LAG_IN)], j), wk[:], stop=True)
                last.then_inc(k_psum, 1)

            def v_in(st):
                if not st.runs(LAG_IN):
                    return
                st.wait(pe, xT_ready, LAG_IN)
                st.after(pe, (qk_ready, LAG_HEADS, 0, TILES, 1), (v_ready, LAG_IN, 1))
                mm(bank[1][:], ones_bf[:, 0:P], row3_by_tile("bv"), start=True)
                for j in range(TILES):
                    last = mm(tile(bank[1], j), tile(xT[st.buf(LAG_IN)], j), wv[:], stop=True)
                last.then_inc(v_psum, 1)

            def kv_sums(st):
                if not st.runs(LAG_IN):
                    return
                st.wait(pe, k_ready, LAG_IN)
                st.wait(pe, v_ready, LAG_IN)
                first = st.buf(LAG_IN) == 0
                if first and (st.inside is not None or st.s >= 2):
                    pe.wait_ge(kv_ready, st.batch(LAG_IN))
                for j in range(TILES):
                    last = mm(kv_acc[:, 0:P + 1], tile(k_tok, j), v_one[:, j, :], start=first and j == 0,
                              stop=not first and j == TILES - 1)
                last.then_inc(kv_psum, 1)

            def linear_attn(st):
                if not st.runs(LAG_MLP):
                    return
                if st.inside is None and st.s == LAG_MLP:
                    pe.wait_ge(late_matrices_in, 16 * (len(matrix_loads) - EARLY))
                    pe.wait_ge(late_bias_in, 64)
                q = qT[st.buf(LAG_MLP)]
                pe.wait_ge(kv_ready, st.batch(LAG_MLP) + 1)
                st.wait(pe, q_ready, LAG_MLP)
                st.after(pe, (x3T_ready, LAG_TANH, 1), (den_ready, LAG_MLP, 1))
                for j in range(TILES):
                    last = mm(bank[5][:, j * HEADS:(j + 1) * HEADS], tile(q, j), kv[:, P:], start=j == 0, stop=True)
                last.then_inc(den_psum, 1)
                st.after(pe, (xT_ready, LAG_IN, 1), (h_act, LAG_MLP, 1, FF))
                for j in range(TILES):
                    last = mm(tile(bank[0], j), tile(q, j), kv[:, 0:P], start=j == 0, stop=True)
                last.then_inc(num_psum, 1)

            def attnT_mm(st):
                if not st.runs(LAG_MLP):
                    return
                st.wait(pe, attn_ready, LAG_MLP)
                turn4(bank[0], attn_tok).then_inc(attnT_psum, 1)

            def s1_mm(st):
                if not st.runs(LAG_MLP):
                    return
                st.wait(pe, attnT_ready, LAG_MLP)
                st.wait(pe, normed[2], LAG_MLP, before=1)
                mm(bank[3][:], ones_bf[:, 0:P], row3_by_tile("bo"), start=True)
                turn4(bank[3], xT[st.buf(LAG_MLP)], start=False)
                for j in range(TILES):
                    last = mm(tile(bank[3], j), tile(attnT, j), wo[:], stop=True)
                last.then_inc(s_psum[1], 1)

            def x1T_mm(st):
                if not st.runs(LAG_MLP):
                    return
                st.wait(pe, normed[1], LAG_MLP)
                turn4(bank[0], n1).then_inc(n1T_psum, 1)

            def mlp_in(st, f):
                if not st.runs(LAG_MLP):
                    return
                if f == 0:
                    st.wait(pe, x1T_ready, LAG_MLP)
                    st.after(pe, (tT_ready, LAG_TANH), (q_ready, LAG_IN, 1), (h_act, LAG_MLP, 1, FF))
                elif f >= 2:
                    st.wait(pe, h_act, LAG_MLP, per=FF, short=FF + 1 - f)
                mm(bank[2 if f % 2 == 0 else 0][:], w1[:, f * P:(f + 1) * P], x1T[:], True, True).then_inc(h_psum, 1)

            def mlp_out(st, f):
                if not st.runs(LAG_MLP):
                    return
                if f == 0:
                    mm(bank[3][:], ones_bf[:, 0:P], row3_by_tile("b2"), start=True)
                    turn4(bank[3], x1T, start=False)
                st.wait(pe, h_act, LAG_MLP, per=FF, short=FF - 1 - f)
                for j in range(TILES):
                    last = mm(tile(bank[3], j), tile(hT[:, f, :], j), w2[:, f, :], stop=f == FF - 1)
                if f == FF - 1:
                    last.then_inc(s_psum[2], 1)

            def n2T_mm(st):
                if not st.runs(LAG_TANH):
                    return
                st.wait(pe, normed[2], LAG_TANH)
                st.after(pe, (k_ready, LAG_IN, 1), (qk_ready, LAG_HEADS, 1, TILES))
                turn4(bank[4], n2).then_inc(n2T_psum, 1)

            def s3_mm(st):
                if not st.runs(LAG_TANH):
                    return
                b = st.buf(LAG_TANH)
                pe.wait_ge(x_copied[b], 16 * (st.batch(LAG_TANH) + 1))
                st.after(pe, (den_ready, LAG_MLP), (x3T_ready, LAG_TANH, 1))
                turn4(bank[5], x_kept[b], stop=False)
                st.wait(pe, uT_ready, LAG_TANH)
                turn4(bank[5], uT, start=False).then_inc(s_psum[3], 1)

            def x2T_mm(st):
                if not st.runs(LAG_TANH):
                    return
                st.wait(pe, normed[3], LAG_TANH)
                turn4(bank[5], x2).then_inc(x2T_psum, 1)

            def tanh_mm(st):
                if not st.runs(LAG_TANH):
                    return
                st.wait(pe, x2T_ready, LAG_TANH)
                st.after(pe, (q_ready, LAG_IN, 1), (normed[5], LAG_OUT, 1), (h_act, LAG_MLP, 1, FF))
                mm(bank[2][:], w_tanh[:], x2T[:], True, True).then_inc(t_psum, 1)

            def s4_mm(st):
                if not st.runs(LAG_TANH):
                    return
                st.wait(pe, tT_ready, LAG_TANH)
                turn4(bank[5], x2T, stop=False)
                turn4(bank[5], tT, start=False).then_inc(s_psum[4], 1)

            def x3T_mm(st):
                if not st.runs(LAG_TANH):
                    return
                st.wait(pe, normed[4], LAG_TANH)
                turn4(bank[5], x3).then_inc(x3T_psum, 1)

            def heads_qkv(st, j):
                if not st.runs(LAG_HEADS):
                    return
                st.wait(pe, x3T_ready, LAG_HEADS)
                if j == 0:
                    st.after(pe, (v_ready, LAG_IN, 1), (qk_ready, LAG_HEADS, 1, TILES))
                elif j == 1:
                    st.after(pe, (uT_ready, LAG_TANH), (qk_ready, LAG_HEADS, 1, TILES))
                else:
                    st.wait(pe, qk_ready, LAG_HEADS, per=TILES, short=TILES + 1 - j)
                b = bank[1 if j % 2 == 0 else 4][:, 0:3 * P]
                mm(b, ones_bf[:, 0:P], row3("bqkv", 3), start=True)
                mm(b, tile(x3T[st.buf(LAG_HEADS)], j), w_qkv[:], stop=True).then_inc(qkv_psum, 1)

            def o_sums(st, tiles):
                if not st.runs(LAG_OUT):
                    return
                for j in tiles:
                    st.wait(pe, pv_ready, LAG_OUT, per=TILES, short=TILES - 1 - j)
                    if j == 0:
                        st.wait(pe, oT_ready, LAG_OUT, before=1)
                    for g in range(HEADS):
                        last = turn(tile(o_acc, j), tile(pv[j], g), start=g == 0, stop=g == HEADS - 1)
                    last.then_inc(o_psum, 1)

            def s5_mm(st):
                if not st.runs(LAG_OUT):
                    return
                st.wait(pe, oT_ready, LAG_OUT)
                st.after(pe, (h_act, LAG_MLP, 0, FF, 1), (tT_ready, LAG_TANH), (normed[5], LAG_OUT, 1))
                mm(bank[2][:], ones_bf[:, 0:P], row3_by_tile("bout"), start=True)
                turn4(bank[2], x3T[st.buf(LAG_OUT)], start=False)
                for j in range(TILES):
                    last = mm(tile(bank[2], j), tile(oT, j), wout[:], stop=True)
                last.then_inc(s_psum[5], 1)

            def body(st):
                heads_qkv(st, 0)
                linear_attn(st)
                o_sums(st, (0,))
                n2T_mm(st)
                attnT_mm(st)
                o_sums(st, (1,))
                s3_mm(st)
                s1_mm(st)
                heads_qkv(st, 1)
                o_sums(st, (2,))
                heads_qkv(st, 2)
                x2T_mm(st)
                x1T_mm(st)
                tanh_mm(st)
                o_sums(st, (3,))
                mlp_in(st, 0)
                s4_mm(st)
                mlp_in(st, 1)
                mlp_in(st, 2)
                mlp_out(st, 0)
                s5_mm(st)
                mlp_in(st, 3)
                mlp_out(st, 1)
                mlp_out(st, 2)
                mlp_out(st, 3)
                heads_qkv(st, 3)
                xT_mm(st)
                x3T_mm(st)
                q_in(st)
                k_in(st)
                v_in(st)
                kv_sums(st)

            def yT_mm(st):
                if not st.runs(LAG_Y):
                    return
                pe.wait_ge(y_in[st.buf(LAG_Y)], 16 * (st.batch(LAG_Y) + 1))
                if st.ran(LAG_Y, 1):
                    st.wait(pe, yT_ready, LAG_Y, before=1)
                turn4(bank[0], y_tok[st.buf(LAG_Y)]).then_inc(yT_psum, 1)

            def gate_mm(st):
                if not st.runs(LAG_GATE):
                    return
                st.wait(pe, yT_ready, LAG_GATE)
                if st.ran(LAG_GATE, 1):
                    st.wait(pe, gate_read, LAG_GATE, before=1)
                    st.wait(pe, chosenT_ready, LAG_GATE, before=1)
                mm(gate_bank, ones_bf[:, 0:P],
                   bias3[:, N_ROWS * P:].unsqueeze(1).broadcast_to([P, TILES, EXPERTS]), start=True)
                for j in range(TILES):
                    last = mm(gate_bank[:, j * EXPERTS:(j + 1) * EXPERTS], tile(yT[st.buf(LAG_GATE)], j), wg[:], stop=True)
                last.then_inc(gate_psum, 1)

            def chosenT_mm(st):
                if not st.runs(LAG_GATE):
                    return
                st.wait(pe, chosen_ready, LAG_GATE)
                for j in range(TILES):
                    last = pe.matmul(chosenT_bank[:, j * P:(j + 1) * P], chosen[:, j, :], ident_bf[:],
                                     is_transpose=True, start=True, stop=True, skip_group_check=True)
                last.then_inc(chosenT_psum, 1)

            def experts_mm(st, layer, experts):
                if not st.runs(LAG_EXPERTS):
                    return
                w, acc = (e1, bank[3]) if layer == 0 else (e2, bank[5])
                for e in experts:
                    if e == 0:
                        if st.ran(LAG_EXPERTS, 1):
                            st.wait(pe, (gT_ready, moeT_ready)[layer], LAG_EXPERTS, before=1)
                        if layer == 0:
                            st.wait(pe, chosenT_ready, LAG_EXPERTS)
                        mm(acc[:], eb3[:, layer * P:(layer + 1) * P], chosenT[st.buf(LAG_EXPERTS)][:], start=True)
                    st.wait(pe, masked_ready, LAG_EXPERTS, per=2 * EXPERTS,
                            short=2 * EXPERTS - 1 - (layer * EXPERTS + e))
                    mm(acc[:], w[:, e, :], masked[e % AHEAD], stop=e == EXPERTS - 1).then_inc(used, 1)

            def result_mm(st):
                if not st.runs(LAG_RESULT):
                    return
                if st.ran(LAG_RESULT, 1):
                    st.wait(pe, normed[6], LAG_RESULT, before=1)
                else:
                    pe.wait_ge(qk_ready, TILES * chunks)
                pe.wait_ge(y_copied[st.buf(LAG_RESULT)], 16 * (st.batch(LAG_RESULT) + 1))
                turn4(bank[4], y_kept[st.buf(LAG_RESULT)], stop=False)
                st.wait(pe, moeT_ready, LAG_RESULT)
                turn4(bank[4], moeT, start=False).then_inc(s_psum[6], 1)

            def body2(st):
                gate_mm(st)
                experts_mm(st, 0, range(0, 4))
                experts_mm(st, 0, range(4, 8))
                chosenT_mm(st)
                result_mm(st)
                yT_mm(st)
                experts_mm(st, 1, range(0, 8))

            run_steps(pe, chunks, body, body2)

        @block.scalar
        def _(act):
            def normalise(st, k, lag, src, dst):
                st.wait(act, shift_ready[k], lag)
                for j in range(TILES):
                    last = act.activation(tile(dst, j), tile(src, j), ACT.Identity,
                                          bias=shift[k][:, j:j + 1], scale=rstd[k][:, j:j + 1])
                last.then_inc(normed[k], 1)

            act.wait_ge(prep_mm, 1)
            act.activation(wtT[:], bank[0][:, 0:P], ACT.Copy).then_inc(prep_out, 1)
            act.wait_ge(prep_mm, 2)
            act.activation(wdownT[:], bank[1][0:LATENT, 0:P], ACT.Copy).then_inc(prep_out, 1)
            act.wait_ge(prep_mm, 3)
            act.activation(cols[:], bank[3][:, 0:FF + 5], ACT.Copy).then_inc(prep_out, 1)
            act.wait_ge(prep_mm, 4)
            act.activation(wt01T[:], bank[0][:, 0:P], ACT.Copy).then_inc(prep_out, 1)
            act.wait_ge(prep_mm, 5)
            act.activation(w_qkv[:, P:3 * P], bank[1][:, 0:2 * P], ACT.Copy).then_inc(prep_out, 1)
            act.wait_ge(prep_mm, 7)
            act.activation(w_tanh[:], bank[0][:, 0:P], ACT.Copy).then_inc(prep_out, 1)

            def xT_copy(st):
                if not st.runs(LAG_IN):
                    return
                st.wait(act, xT_psum, LAG_IN)
                if st.ran(LAG_IN, 2):
                    st.wait(act, s_psum[1], LAG_MLP)
                    act.wait_ge(x_copied[st.buf(LAG_IN)], 16 * st.batch(LAG_IN))
                act.activation(xT[st.buf(LAG_IN)][:], bank[0][:], ACT.Copy).then_inc(xT_ready, 1)

            def elu(st, psum, psum_bank, neg, neg_done, exp, exp_done, ready):
                st.wait(act, psum, LAG_IN)
                st.wait(act, exp_done, LAG_IN, before=1)
                act.activation(neg[:], psum_bank[:], ACT.Relu, scale=-1.0).then_inc(neg_done, 1)
                st.wait(act, neg_done, LAG_IN)
                st.wait(act, ready, LAG_IN, before=1)
                act.activation(exp[:], neg[:], ACT.Exp, scale=-1.0).then_inc(exp_done, 1)

            def q_act(st):
                if st.runs(LAG_IN):
                    elu(st, q_psum, bank[2], neg_q, q_neg, exp_q, q_exp, q_ready)

            def k_act(st):
                if st.runs(LAG_IN):
                    elu(st, k_psum, bank[4], neg_k, k_neg, exp_k, k_exp, k_ready)

            def v_act(st):
                if not st.runs(LAG_IN):
                    return
                st.wait(act, v_psum, LAG_IN)
                st.wait(act, kv_psum, LAG_IN, before=1)
                act.activation(v_one[:, :, 0:P], bank[1][:].rearrange("p (j d) -> p j d", j=TILES),
                               ACT.Copy).then_inc(v_ready, 1)

            def attnT_copy(st):
                if not st.runs(LAG_MLP):
                    return
                st.wait(act, attnT_psum, LAG_MLP)
                act.activation(attnT[:], bank[0][:], ACT.Copy).then_inc(attnT_ready, 1)

            def n1_act(st):
                if st.runs(LAG_MLP):
                    normalise(st, 1, LAG_MLP, bank[3], n1)

            def x1T_act(st):
                if not st.runs(LAG_MLP):
                    return
                st.wait(act, n1T_psum, LAG_MLP)
                act.activation(x1T[:], bank[0][:], ACT.Identity, bias=col(beta1_col),
                               scale=col(g1_col)).then_inc(x1T_ready, 1)

            def relu_act(st, f):
                if not st.runs(LAG_MLP):
                    return
                st.wait(act, h_psum, LAG_MLP, per=FF, short=FF - 1 - f)
                act.activation(hT[:, f, :], bank[2 if f % 2 == 0 else 0][:], ACT.Relu,
                               bias=col(b1_col + f)).then_inc(h_act, 1)

            def n2_act(st):
                if st.runs(LAG_MLP):
                    st.wait(act, n2T_psum, LAG_TANH)
                    normalise(st, 2, LAG_MLP, bank[3], n2)

            def uT_act(st):
                if not st.runs(LAG_TANH):
                    return
                st.wait(act, n2T_psum, LAG_TANH)
                act.activation(uT[:], bank[4][:], ACT.Identity, bias=col(beta2_col),
                               scale=col(g2_col)).then_inc(uT_ready, 1)

            def x2_act(st):
                if st.runs(LAG_TANH):
                    normalise(st, 3, LAG_TANH, bank[5], x2)

            def x2T_copy(st):
                if not st.runs(LAG_TANH):
                    return
                st.wait(act, x2T_psum, LAG_TANH)
                act.activation(x2T[:], bank[5][:], ACT.Copy).then_inc(x2T_ready, 1)

            def tanh_act(st):
                if not st.runs(LAG_TANH):
                    return
                st.wait(act, t_psum, LAG_TANH)
                act.activation(tT[:], bank[2][:], ACT.Tanh, bias=col(tanh_col)).then_inc(tT_ready, 1)

            def x3_act(st):
                if st.runs(LAG_TANH):
                    normalise(st, 4, LAG_TANH, bank[5], x3)

            def x3T_copy(st):
                if not st.runs(LAG_TANH):
                    return
                st.wait(act, x3T_psum, LAG_TANH)
                st.wait(act, s_psum[5], LAG_OUT)
                act.activation(x3T[st.buf(LAG_TANH)][:], bank[5][:], ACT.Copy).then_inc(x3T_ready, 1)

            def qv_copy(st, j):
                if not st.runs(LAG_HEADS):
                    return
                b = bank[1 if j % 2 == 0 else 4]
                st.wait(act, qkv_psum, LAG_HEADS, per=TILES, short=TILES - 1 - j)
                st.wait(act, qk_ready, LAG_HEADS, per=TILES, short=TILES - 1 - j, before=1)
                st.wait(act, pv_ready, LAG_OUT, per=TILES, short=TILES - 1 - j)
                act.activation(q_tok[:, j, :], b[:, 0:P], ACT.Copy)
                act.activation(v_tok[:, j, :].rearrange("p (g d) -> p g d", g=HEADS),
                               b[:, P:3 * P].rearrange("p (g w) -> p g w", g=HEADS)[:, :, HD:],
                               ACT.Copy).then_inc(qv_ready, 1)

            def prob_exp(st, pair):
                if not st.runs(LAG_HEADS):
                    return
                st.wait(act, below_top, LAG_HEADS, per=2, short=1 - pair)
                st.wait(act, prob_ready, LAG_HEADS, per=2, short=1 - pair, before=1)
                act.activation(prob_e[:, 2 * pair:2 * pair + 2, :], score[:, 2 * pair:2 * pair + 2, :], ACT.Exp,
                               scale=float(HD) ** -0.5).then_inc(exp_ready, 1)

            def oT_copy(st):
                if not st.runs(LAG_OUT):
                    return
                st.wait(act, o_psum, LAG_OUT, per=TILES)
                act.activation(oT[:], o_acc[:], ACT.Copy).then_inc(oT_ready, 1)

            def x4_act(st):
                if not st.runs(LAG_OUT):
                    return
                b = st.buf(LAG_OUT)
                if st.inside is not None or st.s - LAG_OUT >= 2:
                    act.wait_ge(x4_out[b], 16 * st.batch(LAG_OUT))
                normalise(st, 5, LAG_OUT, bank[2], x4[b])

            def body(st):
                qv_copy(st, 0)
                attnT_copy(st)
                uT_act(st)
                qv_copy(st, 1)
                x2_act(st)
                n1_act(st)
                x2T_copy(st)
                x1T_act(st)
                qv_copy(st, 2)
                tanh_act(st)
                oT_copy(st)
                prob_exp(st, 0)
                relu_act(st, 0)
                relu_act(st, 1)
                relu_act(st, 2)
                relu_act(st, 3)
                x3_act(st)
                qv_copy(st, 3)
                xT_copy(st)
                x4_act(st)
                x3T_copy(st)
                k_act(st)
                v_act(st)
                q_act(st)
                prob_exp(st, 1)
                n2_act(st)

            def yT_act(st):
                if not st.runs(LAG_Y):
                    return
                st.wait(act, yT_psum, LAG_Y)
                if st.ran(LAG_Y, 2):
                    st.wait(act, masked_ready, LAG_EXPERTS, per=2 * EXPERTS, short=EXPERTS)
                    act.wait_ge(y_copied[st.buf(LAG_Y)], 16 * st.batch(LAG_Y))
                act.activation(yT[st.buf(LAG_Y)][:], bank[0][:], ACT.Copy).then_inc(yT_ready, 1)

            def chosenT_act(st):
                if not st.runs(LAG_GATE):
                    return
                st.wait(act, chosenT_psum, LAG_GATE)
                if st.ran(LAG_GATE, 2):
                    st.wait(act, used, LAG_EXPERTS, per=2 * EXPERTS, before=1)
                    act.wait_ge(choice_out[st.buf(LAG_GATE)], 16 * st.batch(LAG_GATE))
                act.activation(chosenT[st.buf(LAG_GATE)][:], chosenT_bank, ACT.Copy).then_inc(chosenT_ready, 1)

            def gelu_act(st):
                if not st.runs(LAG_EXPERTS):
                    return
                st.wait(act, used, LAG_EXPERTS, per=2 * EXPERTS, short=EXPERTS)
                if st.ran(LAG_EXPERTS, 1):
                    st.wait(act, masked_ready, LAG_EXPERTS, per=2 * EXPERTS, before=1)
                act.activation(gT, bank[3][:], ACT.Gelu).then_inc(gT_ready, 1)

            def moeT_act(st):
                if not st.runs(LAG_EXPERTS):
                    return
                st.wait(act, used, LAG_EXPERTS, per=2 * EXPERTS)
                if st.ran(LAG_EXPERTS, 1):
                    st.wait(act, s_psum[6], LAG_RESULT)
                act.activation(moeT, bank[5][:], ACT.Copy).then_inc(moeT_ready, 1)

            def result_act(st):
                if not st.runs(LAG_RESULT):
                    return
                b = st.buf(LAG_RESULT)
                if st.ran(LAG_RESULT, 2):
                    act.wait_ge(result_out[b], 16 * st.batch(LAG_RESULT))
                normalise(st, 6, LAG_RESULT, bank[4], result[b])

            def body2(st):
                gelu_act(st)
                chosenT_act(st)
                yT_act(st)
                result_act(st)
                moeT_act(st)

            run_steps(act, chunks, body, body2)

        @block.vector
        def _(dve):
            dve.memset(ones_bf[:], 1.0).then_inc(dve_prep, 1)
            dve.memset(v_one[:, :, P:], 1.0).then_inc(dve_prep, 1)
            dve.memset(minus_half[:], -0.5).then_inc(dve_prep, 1)
            dve.memset(bias3[:], 0.0).then_inc(dve_prep, 1)
            dve.wait_ge(consts, 1)
            dve.tensor_copy(ident_bf[:], ident[:]).then_inc(dve_prep, 1)
            dve.wait_ge(pool_prep, 4)
            dve.tensor_copy(head_mask[:].rearrange("p (h m) -> p h m", h=HEADS),
                            head_of[:].unsqueeze(2).broadcast_to([P, HEADS, HD])).then_inc(dve_prep, 1)
            for e in range(EXPERTS):
                dve.memset(prefer[:, e:e + 1], float(EXPERTS - e)).then_inc(dve_prep, 1)
            dve.wait_ge(dve_prep, 6 + EXPERTS)
            def split(whole, left, parts, done):
                dve.tensor_copy(parts[:, 0, :], whole[:]).then_inc(done, 1)
                dve.wait_ge(done, 1)
                dve.tensor_tensor(left[:], whole[:], parts[:, 0, :], ALU.subtract).then_inc(done, 1)
                dve.wait_ge(done, 2)
                dve.tensor_copy(parts[:, 1, :], left[:]).then_inc(done, 1)
                dve.wait_ge(done, 3)
                dve.tensor_tensor(left[:], left[:], parts[:, 1, :], ALU.subtract).then_inc(done, 1)
                dve.wait_ge(done, 4)
                dve.tensor_copy(parts[:, 2, :], left[:]).then_inc(done, 1)

            dve.wait_ge(biases_in, 16 * len(bias_loads))
            split(rows, rows_left, parts, rows_split)
            dve.wait_ge(prep_mm, 6)
            dve.tensor_tensor(kv_row[:, 0:2 * P], bank[7][0:1, 0:2 * P], kv_row[:, 0:2 * P], ALU.add
                              ).then_inc(kv_bias_ready, 1)
            dve.wait_ge(kv_bias_ready, 1)
            split(kv_row, kv_row_left, kv_row_parts, kv_row_split)
            dve.wait_ge(eb_in, 16 * len(expert_bias_loads))
            split(eb, eb_left, eb_parts, eb_split)

            def stats_of(st, k, lag, src):
                if not st.runs(lag):
                    return
                st.wait(dve, s_psum[k], lag)
                for j in range(TILES):
                    last = dve.bn_stats(stats[k][:, j, :], tile(src, j))
                last.then_inc(stats_done[k], 1)

            def moments_of(st, k, lag):
                if not st.runs(lag):
                    return
                dve.wait_ge(dve_prep, 1)
                st.wait(dve, stats_done[k], lag)
                for j in range(TILES):
                    last = dve.bn_aggr(mean_var[k][:, j, :], stats[k][:, j, :])
                last.then_inc(moments_ready[k], 1)

            def elu_q(st):
                if not st.runs(LAG_IN):
                    return
                st.wait(dve, q_exp, LAG_IN)
                st.wait(dve, num_psum, LAG_MLP)
                dve.scalar_tensor_tensor(qT[st.buf(LAG_IN)][:], bank[2][:], 0.0, exp_q[:], ALU.max,
                                         ALU.add).then_inc(q_ready, 1)

            def elu_k(st):
                if not st.runs(LAG_IN):
                    return
                st.wait(dve, k_exp, LAG_IN)
                st.wait(dve, kv_psum, LAG_IN, before=1)
                dve.scalar_tensor_tensor(k_tok[:], bank[4][:], 0.0, exp_k[:], ALU.max,
                                         ALU.add).then_inc(k_ready, 1)

            def kv_blocks(st):
                if not st.runs(LAG_IN) or st.buf(LAG_IN) == 0:
                    return
                st.wait(dve, kv_psum, LAG_IN)
                st.wait(dve, num_psum, LAG_MLP)
                dve.tensor_copy(k_sum[:], kv_acc[:, P:P + 1]).then_inc(kv_sum, 1)
                dve.tensor_tensor(kv[:, 0:P], kv_acc[:, 0:P], head_mask[:], ALU.mult)
                dve.wait_ge(kv_sum, st.batch(LAG_IN) + 1)
                dve.tensor_scalar(kv[:, P:], head_of[:], k_sum[:, 0:1], None, ALU.mult).then_inc(kv_ready, 1)

            def attn_den(st):
                if not st.runs(LAG_MLP):
                    return
                st.wait(dve, den_psum, LAG_MLP)
                dve.tensor_scalar(den[:], bank[5][:, 0:TILES * HEADS], EPS_ATTN, None, ALU.add).then_inc(den_ready, 1)

            def attn_z(st):
                if not st.runs(LAG_MLP):
                    return
                st.wait(dve, den_ready, LAG_MLP)
                dve.reciprocal(z[:], den[:]).then_inc(z_ready, 1)

            def attn(st):
                if not st.runs(LAG_MLP):
                    return
                st.wait(dve, z_ready, LAG_MLP)
                st.wait(dve, num_psum, LAG_MLP)
                dve.tensor_tensor(attn_tok[:].rearrange("p (a m) -> p a m", m=HD),
                                  bank[0][:].rearrange("p (a m) -> p a m", m=HD),
                                  z[:].unsqueeze(2).broadcast_to([P, TILES * HEADS, HD]),
                                  ALU.mult).then_inc(attn_ready, 1)

            def heads_qk(st, j):
                if not st.runs(LAG_HEADS):
                    return
                b = bank[1 if j % 2 == 0 else 4]
                k_view = b[:, P:3 * P].rearrange("p (g w) -> p g w", g=HEADS)[:, :, 0:HD]
                q_view = q_tok[:, j, :].rearrange("p (h d) -> p h d", h=HEADS)
                st.wait(dve, qv_ready, LAG_HEADS, per=TILES, short=TILES - 1 - j)
                dve.tensor_tensor(qk[j % 2][:].rearrange("p (h g d) -> p h g d", h=HEADS, g=HEADS),
                                  k_view.unsqueeze(1).broadcast_to([P, HEADS, HEADS, HD]),
                                  q_view.unsqueeze(2).broadcast_to([P, HEADS, HEADS, HD]),
                                  ALU.mult).then_inc(qk_ready, 1)

            def heads_scores(st, j):
                if not st.runs(LAG_HEADS):
                    return
                st.wait(dve, qk_ready, LAG_HEADS, per=TILES, short=TILES - 1 - j)
                if j % 2 == 0:
                    st.wait(dve, exp_ready, LAG_HEADS, per=2, short=1 - j // 2, before=1)
                dve.tensor_reduce(score[:, j, :], qk[j % 2][:].rearrange("p (a d) -> p a d", d=HD), AX.X,
                                  ALU.add).then_inc(score_ready, 1)

            def tops(two):
                return top[:, two, :].rearrange("p j h -> p (j h)")

            def softmax_top(st, pair):
                if not st.runs(LAG_HEADS):
                    return
                two = slice(2 * pair, 2 * pair + 2)
                st.wait(dve, score_ready, LAG_HEADS, per=TILES, short=2 - 2 * pair)
                dve.tensor_reduce(tops(two), score[:, two, :].rearrange("p j (h g) -> p (j h) g", g=HEADS), AX.X,
                                  ALU.max).then_inc(top_ready, 1)

            def softmax_sub(st, pair):
                if not st.runs(LAG_HEADS):
                    return
                two = slice(2 * pair, 2 * pair + 2)
                view = score[:, two, :].rearrange("p j (h g) -> p (j h) g", g=HEADS)
                st.wait(dve, top_ready, LAG_HEADS, per=2, short=1 - pair)
                dve.tensor_tensor(view, view, tops(two).unsqueeze(2).broadcast_to([P, 2 * HEADS, HEADS]),
                                  ALU.subtract).then_inc(below_top, 1)

            def softmax_total(st, pair):
                if not st.runs(LAG_HEADS):
                    return
                two = slice(2 * pair, 2 * pair + 2)
                st.wait(dve, exp_ready, LAG_HEADS, per=2, short=1 - pair)
                dve.tensor_reduce(total[:, two, :].rearrange("p j h -> p (j h)"),
                                  prob_e[:, two, :].rearrange("p j (h g) -> p (j h) g", g=HEADS), AX.X,
                                  ALU.add).then_inc(total_ready, 1)

            def softmax_inv(st, pair):
                if not st.runs(LAG_HEADS):
                    return
                two = slice(2 * pair, 2 * pair + 2)
                st.wait(dve, total_ready, LAG_HEADS, per=2, short=1 - pair)
                st.wait(dve, prob_ready, LAG_HEADS, per=2, short=1 - pair, before=1)
                dve.reciprocal(inv_total[:, two, :], total[:, two, :]).then_inc(inv_ready, 1)

            def body(st):
                attn_den(st)
                attn_z(st)
                attn(st)
                heads_qk(st, 0)
                heads_scores(st, 0)
                stats_of(st, 3, LAG_TANH, bank[5])
                moments_of(st, 3, LAG_TANH)
                stats_of(st, 1, LAG_MLP, bank[3])
                moments_of(st, 1, LAG_MLP)
                heads_qk(st, 1)
                heads_scores(st, 1)
                softmax_top(st, 0)
                softmax_sub(st, 0)
                heads_qk(st, 2)
                stats_of(st, 4, LAG_TANH, bank[5])
                softmax_total(st, 0)
                softmax_inv(st, 0)
                moments_of(st, 4, LAG_TANH)
                stats_of(st, 5, LAG_OUT, bank[2])
                heads_scores(st, 2)
                moments_of(st, 5, LAG_OUT)
                stats_of(st, 2, LAG_MLP, bank[3])
                moments_of(st, 2, LAG_MLP)
                heads_qk(st, 3)
                heads_scores(st, 3)
                softmax_top(st, 1)
                elu_k(st)
                softmax_sub(st, 1)
                kv_blocks(st)
                elu_q(st)
                softmax_total(st, 1)
                softmax_inv(st, 1)

            def choose(st):
                if not st.runs(LAG_GATE):
                    return
                by_expert = [P, TILES, EXPERTS]
                st.wait(dve, gate_psum, LAG_GATE)
                dve.tensor_copy(gate[:], gate_bank
                                .rearrange("p (j e) -> p j e", e=EXPERTS)).then_inc(gate_read, 1)
                st.wait(dve, gate_read, LAG_GATE)
                dve.tensor_reduce(gate_top[:], gate[:], AX.X, ALU.max).then_inc(gate_step, 1)
                st.wait(dve, gate_step, LAG_GATE, per=4, short=3)
                dve.tensor_tensor(gate_is[:], gate[:], gate_top[:].unsqueeze(2).broadcast_to(by_expert),
                                  ALU.is_equal).then_inc(gate_step, 1)
                st.wait(dve, gate_step, LAG_GATE, per=4, short=2)
                dve.tensor_tensor(gate_pref[:], gate_is[:], prefer[:].unsqueeze(1).broadcast_to(by_expert),
                                  ALU.mult).then_inc(gate_step, 1)
                st.wait(dve, gate_step, LAG_GATE, per=4, short=1)
                dve.tensor_reduce(gate_first[:], gate_pref[:], AX.X, ALU.max).then_inc(gate_step, 1)
                st.wait(dve, gate_step, LAG_GATE, per=4)
                if st.ran(LAG_GATE, 1):
                    st.wait(dve, chosenT_psum, LAG_GATE, before=1)
                for r in range(3):
                    last = dve.tensor_tensor(chosen[:, :, r * EXPERTS:(r + 1) * EXPERTS], gate_pref[:],
                                             gate_first[:].unsqueeze(2).broadcast_to(by_expert), ALU.is_equal)
                last.then_inc(chosen_ready, 1)

            def mask_operand(st, layer, experts):
                if not st.runs(LAG_EXPERTS):
                    return
                b = st.buf(LAG_EXPERTS)
                src = gT if layer else yT[b]
                for e in experts:
                    n = layer * EXPERTS + e
                    if n == 0:
                        st.wait(dve, yT_ready, LAG_EXPERTS)
                        dve.wait_ge(mask_in[b], 16 * (st.batch(LAG_EXPERTS) + 1))
                    if layer and e == 0:
                        st.wait(dve, gT_ready, LAG_EXPERTS)
                    if n >= AHEAD:
                        st.wait(dve, used, LAG_EXPERTS, per=2 * EXPERTS, short=2 * EXPERTS - 1 - (n - AHEAD))
                    elif st.ran(LAG_EXPERTS, 1):
                        st.wait(dve, used, LAG_EXPERTS, per=2 * EXPERTS, short=AHEAD - 1 - n, before=1)
                    dve.tensor_tensor(masked[e % AHEAD], mask[b][:, e * CHUNK:(e + 1) * CHUNK], src[:],
                                      ALU.mult).then_inc(masked_ready, 1)

            def body2(st):
                mask_operand(st, 0, range(0, 6))
                mask_operand(st, 0, range(6, 8))
                choose(st)
                mask_operand(st, 1, range(0, 6))
                stats_of(st, 6, LAG_RESULT, bank[4])
                moments_of(st, 6, LAG_RESULT)
                mask_operand(st, 1, range(6, 7))
                mask_operand(st, 1, range(7, 8))

            run_steps(dve, chunks, body, body2)

        @block.gpsimd
        def _(pool):
            pool.memset(ident[:], 0.0).then_inc(pool_prep, 1)
            pool.memset(head_of[:], 1.0).then_inc(pool_prep, 1)
            pool.memset(minus_one[:], -1.0)
            pool.memset(eps[:], EPS_LN)
            pool.wait_ge(pool_prep, 2)
            pool.affine_select(out=ident[:], in_=ident[:], compare_op=ALU.not_equal, fill=1.0, base=0,
                               pattern=[[-1, P]], channel_multiplier=1).then_inc(consts, 1)
            pool.affine_select(out=head_of[:], in_=head_of[:], compare_op=ALU.is_ge, fill=0.0, base=0,
                               pattern=[[-HD, HEADS]], channel_multiplier=1).then_inc(pool_prep, 1)
            pool.wait_ge(pool_prep, 3)
            pool.affine_select(out=head_of[:], in_=head_of[:], compare_op=ALU.is_ge, fill=0.0, base=HD - 1,
                               pattern=[[HD, HEADS]], channel_multiplier=-1).then_inc(pool_prep, 1)
            for i, (dst, src) in enumerate(matrix_loads):
                pool.dma_start(dst[:], src).then_inc(matrices_in if i < EARLY else late_matrices_in, 16)

            def rsqrt(n, k):
                pool.wait_ge(moments_ready[k], n)
                pool.tensor_tensor(var_eps[k][:], mean_var[k][:, :, 1], eps[:], ALU.add).then_inc(eps_added[k], 1)
                pool.tensor_tensor(minus_mean[k][:], mean_var[k][:, :, 0], minus_one[:], ALU.mult)
                pool.wait_ge(eps_added[k], n)
                pool.tensor_tensor(rstd[k][:], var_eps[k][:], minus_half[:], ALU.pow).then_inc(rstd_ready[k], 1)
                pool.wait_ge(rstd_ready[k], n)
                pool.tensor_tensor(shift[k][:], minus_mean[k][:], rstd[k][:], ALU.mult).then_inc(shift_ready[k], 1)

            def rsqrt_of(st, k, lag):
                if st.runs(lag):
                    rsqrt(st.done(lag), k)

            def probs(st, pair, lag, before=0):
                if not st.runs(lag):
                    return
                two = slice(2 * pair, 2 * pair + 2)
                st.wait(pool, inv_ready, lag, per=2, short=1 - pair)
                pool.tensor_tensor(prob[:, two, :].rearrange("p j (h g) -> p (j h) g", g=HEADS),
                                   prob_e[:, two, :].rearrange("p j (h g) -> p (j h) g", g=HEADS),
                                   inv_total[:, two, :].rearrange("p j h -> p (j h)").unsqueeze(2)
                                   .broadcast_to([P, 2 * HEADS, HEADS]), ALU.mult).then_inc(prob_ready, 1)

            def weigh(st, j, lag, parts=range(4)):
                if not st.runs(lag):
                    return
                if 0 in parts:
                    st.wait(pool, prob_ready, lag, per=2, short=1 - j // 2)
                    st.wait(pool, o_psum, lag, per=TILES, short=TILES - 1 - j if lag < LAG_OUT else 0, before=1)
                p_view = prob[:, j, :].rearrange("p (h g) -> p g h", g=HEADS)
                v_view = v_tok[:, j, :].rearrange("p (g d) -> p g d", g=HEADS)
                quarter = HEADS // 4
                for part in parts:
                    g = slice(part * quarter, (part + 1) * quarter)
                    last = pool.tensor_tensor(
                        pv[j][:, part * quarter * P:(part + 1) * quarter * P]
                        .rearrange("p (g h d) -> p g h d", g=quarter, h=HEADS),
                        p_view[:, g, :].unsqueeze(3).broadcast_to([P, quarter, HEADS, HD]),
                        v_view[:, g, :].unsqueeze(2).broadcast_to([P, quarter, HEADS, HD]), ALU.mult)
                if 3 in parts:
                    last.then_inc(pv_ready, 1)

            def body(st):
                probs(st, 1, LAG_OUT)
                weigh(st, 2, LAG_OUT)
                weigh(st, 3, LAG_OUT, (0, 1))
                rsqrt_of(st, 3, LAG_TANH)
                rsqrt_of(st, 1, LAG_MLP)
                weigh(st, 3, LAG_OUT, (2, 3))
                rsqrt_of(st, 4, LAG_TANH)
                probs(st, 0, LAG_HEADS)
                weigh(st, 0, LAG_HEADS, (0, 1))
                rsqrt_of(st, 5, LAG_OUT)
                weigh(st, 0, LAG_HEADS, (2, 3))
                rsqrt_of(st, 2, LAG_MLP)
                weigh(st, 1, LAG_HEADS)








            def body2(st):
                rsqrt_of(st, 6, LAG_RESULT)

            run_steps(pool, chunks, body, body2)


def kernel(**inputs):
    import numpy as np
    import concourse.bacc as bacc
    from concourse.bass_utils import run_bass_kernel_spmd

    nc = bacc.Bacc("TRN2", target_bir_lowering=False, num_devices=1)
    arrays, aps = {}, {}
    for name, value in inputs.items():
        a = np.ascontiguousarray(value)
        arrays[f"in_{name}"] = a
        aps[name] = nc.dram_tensor(f"in_{name}", a.shape, mybir.dt.from_np(a.dtype), kind="ExternalInput").ap()
    shape = arrays["in_L0_attn_x"].shape
    out = nc.dram_tensor("out_0", shape, F32, kind="ExternalOutput").ap()
    scratch = nc.dram_tensor("x4_scratch", (shape[0] * shape[1] // TILES, CHUNK), F32, kind="Internal").ap()
    choice = nc.dram_tensor("choice_scratch", (shape[0] * shape[1] // CHUNK * EXPERTS, CHUNK), BF16, kind="Internal").ap()
    build(nc, aps, out, scratch, choice)
    r = run_bass_kernel_spmd(nc, [arrays], core_ids=[0])
    return r.results[0]["out_0"]
```
